# Optimizing a Trainium2 kernel written in Bass

```python
import numpy as np
import jax
import jax.numpy as jnp

def _softmax(x, axis=-1):
    return jax.nn.softmax(x, axis=axis)

def _gelu(x):
    return jax.nn.gelu(x, approximate=True)

def _silu(x):
    return jax.nn.silu(x)

def _sigmoid(x):
    return jax.nn.sigmoid(x)

def _layernorm(x, axis=-1, eps=1e-05):
    m = jnp.mean(x, axis=axis, keepdims=True)
    v = jnp.var(x, axis=axis, keepdims=True)
    return (x - m) / jnp.sqrt(v + eps)

def _scatter_add(tgt, idx, src, axis=0):
    return tgt.at[idx].add(src)

def _segment_sum(src, seg, n):
    return jax.ops.segment_sum(src, seg, n)
kernel_name = 'mk_xattn_ffn_d1_seqx_r2_95a615'

def setup_inputs(seed: int=0):
    np.random.seed(seed)
    _w = jnp.asarray

    def _rec_inputs():
        import jax
        import jax.numpy as jnp
        _rk = jax.random.key(seed)
        x = 4.136e-05 + 0.9999 * jax.random.normal(jax.random.fold_in(_rk, 1), (1, 4096, 512), jnp.float32)
        _lenS = 4096 - jax.random.randint(jax.random.fold_in(_rk, 7), (1,), 0, max(1, 4096 // 4) + 1, jnp.int32)
        _lenS2 = 3202 - jax.random.randint(jax.random.fold_in(_rk, 8), (1,), 0, max(1, 3202 // 4) + 1, jnp.int32)
        _ctx_1024P = jax.random.normal(jax.random.fold_in(_rk, 11), (1, 16, 512), jnp.float32)
        _ctx_1024c = jax.random.dirichlet(jax.random.fold_in(_rk, 511), 0.3 * jnp.ones((16,), jnp.float32), (1, 3202))
        _ctx_1024t = jnp.einsum('bsk,bkd->bsd', _ctx_1024c, _ctx_1024P)
        _ctx_1024t = _ctx_1024t * jax.lax.rsqrt(jnp.mean(jnp.square(_ctx_1024t)) + 1e-12) * 0.953939
        ctx_1024 = 7.22013e-05 + 1.00017 * (_ctx_1024t + 0.3 * jax.random.normal(jax.random.fold_in(_rk, 611), (1, 3202, 512), jnp.float32))
        return (x, ctx_1024)
    x, ctx_1024 = _rec_inputs()

    def _L0_xattn_setup():
        import jax, jax.numpy as jnp
        import numpy as np
        B, L_Q, L_KV, D, H = (4, 1024, 1024, 512, 16)
        key = jax.random.key(seed)
        ks = jax.random.split(key, 11)
        s = 0.02
        return {'kv': jax.random.normal(ks[0], (B, L_KV, D), dtype=jnp.float32), 'q': jax.random.normal(ks[1], (B, L_Q, D), dtype=jnp.float32), 'Wq': jax.random.normal(ks[2], (D, D), dtype=jnp.float32) * s, 'bq': jnp.zeros((D,), dtype=jnp.float32), 'Wk': jax.random.normal(ks[3], (D, D), dtype=jnp.float32) * s, 'bk': jnp.zeros((D,), dtype=jnp.float32), 'Wv': jax.random.normal(ks[4], (D, D), dtype=jnp.float32) * s, 'bv': jnp.zeros((D,), dtype=jnp.float32), 'Wo': jax.random.normal(ks[5], (D, D), dtype=jnp.float32) * s, 'bo': jnp.zeros((D,), dtype=jnp.float32)}
    _L0_xattn_all = _L0_xattn_setup()
    _L0_xattn_in = {k: v for k, v in _L0_xattn_all.items() if k in ('Wq', 'bq', 'Wk', 'bk', 'Wv', 'bv', 'Wo', 'bo')}
    del _L0_xattn_all

    def _L0_ffn_setup():
        import jax, jax.numpy as jnp
        import numpy as np
        B, S, D, H, M, E, K = (8, 1024, 512, 1024, 64, 8, 2)
        EH = H // 2

        def _layernorm(x, g, b, eps=1e-05):
            mu = jnp.mean(x, axis=-1, keepdims=True)
            var = jnp.var(x, axis=-1, keepdims=True)
            return (x - mu) * jax.lax.rsqrt(var + eps) * g + b
        key = jax.random.key(seed)
        ks = jax.random.split(key, 16)
        sc = lambda *shape: 1.0 / np.sqrt(shape[0])
        return {'inputs_embeds': jax.random.normal(ks[0], (B, S, D), jnp.float32), 'W_enc': jax.random.normal(ks[1], (D, H), jnp.float32) * sc(D), 'b_enc': jnp.zeros((H,), jnp.float32), 'W_s2c': jax.random.normal(ks[2], (H, M), jnp.float32) * sc(H), 'b_s2c': jnp.zeros((M,), jnp.float32), 'Wr': jax.random.normal(ks[3], (M, E), jnp.float32) * sc(M), 'br': jnp.zeros((E,), jnp.float32), 'W1': jax.random.normal(ks[4], (E, M, EH), jnp.float32) * sc(M), 'b1': jnp.zeros((E, EH), jnp.float32), 'W2': jax.random.normal(ks[5], (E, EH, M), jnp.float32) * sc(EH), 'b2': jnp.zeros((E, M), jnp.float32), 'W_c2s': jax.random.normal(ks[6], (M, H), jnp.float32) * sc(M), 'b_c2s': jnp.zeros((H,), jnp.float32), 'W_dec': jax.random.normal(ks[7], (H, D), jnp.float32) * sc(H), 'b_dec': jnp.zeros((D,), jnp.float32), 'ln_g': jnp.ones((D,), jnp.float32), 'ln_b': jnp.zeros((D,), jnp.float32)}
    _L0_ffn_all = _L0_ffn_setup()
    _L0_ffn_in = {k: v for k, v in _L0_ffn_all.items() if k in ('W_enc', 'b_enc', 'W_s2c', 'b_s2c', 'Wr', 'br', 'W1', 'b1', 'W2', 'b2', 'W_c2s', 'b_c2s', 'W_dec', 'b_dec', 'ln_g', 'ln_b')}
    del _L0_ffn_all
    return {'x': x, 'ctx_1024': ctx_1024, 'L0_xattn_Wq': _L0_xattn_in['Wq'], 'L0_xattn_bq': _L0_xattn_in['bq'], 'L0_xattn_Wk': _L0_xattn_in['Wk'], 'L0_xattn_bk': _L0_xattn_in['bk'], 'L0_xattn_Wv': _L0_xattn_in['Wv'], 'L0_xattn_bv': _L0_xattn_in['bv'], 'L0_xattn_Wo': _L0_xattn_in['Wo'], 'L0_xattn_bo': _L0_xattn_in['bo'], 'L0_ffn_W_enc': _L0_ffn_in['W_enc'], 'L0_ffn_b_enc': _L0_ffn_in['b_enc'], 'L0_ffn_W_s2c': _L0_ffn_in['W_s2c'], 'L0_ffn_b_s2c': _L0_ffn_in['b_s2c'], 'L0_ffn_Wr': _L0_ffn_in['Wr'], 'L0_ffn_br': _L0_ffn_in['br'], 'L0_ffn_W1': _L0_ffn_in['W1'], 'L0_ffn_b1': _L0_ffn_in['b1'], 'L0_ffn_W2': _L0_ffn_in['W2'], 'L0_ffn_b2': _L0_ffn_in['b2'], 'L0_ffn_W_c2s': _L0_ffn_in['W_c2s'], 'L0_ffn_b_c2s': _L0_ffn_in['b_c2s'], 'L0_ffn_W_dec': _L0_ffn_in['W_dec'], 'L0_ffn_b_dec': _L0_ffn_in['b_dec'], 'L0_ffn_ln_g': _L0_ffn_in['ln_g'], 'L0_ffn_ln_b': _L0_ffn_in['ln_b']}

def reference(x, ctx_1024, L0_xattn_Wq, L0_xattn_bq, L0_xattn_Wk, L0_xattn_bk, L0_xattn_Wv, L0_xattn_bv, L0_xattn_Wo, L0_xattn_bo, L0_ffn_W_enc, L0_ffn_b_enc, L0_ffn_W_s2c, L0_ffn_b_s2c, L0_ffn_Wr, L0_ffn_br, L0_ffn_W1, L0_ffn_b1, L0_ffn_W2, L0_ffn_b2, L0_ffn_W_c2s, L0_ffn_b_c2s, L0_ffn_W_dec, L0_ffn_b_dec, L0_ffn_ln_g, L0_ffn_ln_b):
    import jax
    import jax.numpy as jnp

    def _L0_xattn_ref(kv, q, Wq, bq, Wk, bk, Wv, bv, Wo, bo):
        import jax, jax.numpy as jnp
        import numpy as np
        B, L_Q, L_KV, D, H = (4, 1024, 1024, 512, 16)
        Bb, Lkv, Dm = kv.shape
        Lq = q.shape[1]
        hd = Dm // H
        scale = hd ** (-0.5)
        qh = (q @ Wq.T + bq).reshape(Bb, Lq, H, hd).transpose(0, 2, 1, 3)
        kh = (kv @ Wk.T + bk).reshape(Bb, Lkv, H, hd).transpose(0, 2, 1, 3)
        vh = (kv @ Wv.T + bv).reshape(Bb, Lkv, H, hd).transpose(0, 2, 1, 3)
        scores = jnp.einsum('bhqd,bhkd->bhqk', qh, kh) * scale
        mask = jnp.arange(Lkv)[None, :] <= jnp.arange(Lq)[:, None]
        scores = jnp.where(mask[None, None], scores, -jnp.inf)
        attn = jax.nn.softmax(scores, axis=-1)
        out = jnp.einsum('bhqk,bhkd->bhqd', attn, vh)
        out = out.transpose(0, 2, 1, 3).reshape(Bb, Lq, Dm)
        return out @ Wo.T + bo

    def _L0_ffn_ref(inputs_embeds, W_enc, b_enc, W_s2c, b_s2c, Wr, br, W1, b1, W2, b2, W_c2s, b_c2s, W_dec, b_dec, ln_g, ln_b):
        import jax, jax.numpy as jnp
        import numpy as np
        B, S, D, H, M, E, K = (8, 1024, 512, 1024, 64, 8, 2)
        EH = H // 2

        def _layernorm(x, g, b, eps=1e-05):
            mu = jnp.mean(x, axis=-1, keepdims=True)
            var = jnp.var(x, axis=-1, keepdims=True)
            return (x - mu) * jax.lax.rsqrt(var + eps) * g + b
        b, s, d = inputs_embeds.shape
        spikes_enc = jax.nn.sigmoid(inputs_embeds @ W_enc + b_enc)
        flat = spikes_enc.reshape(b * s, -1)
        cont = flat @ W_s2c + b_s2c
        probs = jax.nn.softmax(cont @ Wr + br, axis=-1)
        topk_w, topk_idx = jax.lax.top_k(probs, K)
        topk_w = topk_w / jnp.sum(topk_w, axis=-1, keepdims=True)
        gate = jnp.sum(jax.nn.one_hot(topk_idx, E, dtype=cont.dtype) * topk_w[..., None], axis=1)
        h = jax.nn.relu(jnp.einsum('tm,emh->eth', cont, W1) + b1[:, None, :])
        y = jnp.einsum('eth,ehm->etm', h, W2) + b2[:, None, :]
        expert_out = jnp.einsum('etm,te->tm', y, gate)
        spikes_moe = jax.nn.sigmoid(expert_out @ W_c2s + b_c2s)
        spikes_moe = spikes_moe.reshape(b, s, -1)
        decoded = spikes_moe @ W_dec + b_dec
        return _layernorm(decoded, ln_g, ln_b)
    x = x + _L0_xattn_ref(ctx_1024, _layernorm(x, axis=-1), L0_xattn_Wq, L0_xattn_bq, L0_xattn_Wk, L0_xattn_bk, L0_xattn_Wv, L0_xattn_bv, L0_xattn_Wo, L0_xattn_bo)
    x = x + _L0_ffn_ref(_layernorm(x, axis=-1), L0_ffn_W_enc, L0_ffn_b_enc, L0_ffn_W_s2c, L0_ffn_b_s2c, L0_ffn_Wr, L0_ffn_br, L0_ffn_W1, L0_ffn_b1, L0_ffn_W2, L0_ffn_b2, L0_ffn_W_c2s, L0_ffn_b_c2s, L0_ffn_W_dec, L0_ffn_b_dec, L0_ffn_ln_g, L0_ffn_ln_b)
    return x

_drawn_inputs = setup_inputs


def setup_inputs(seed=0):
    import zlib

    import numpy as np

    out = dict(_drawn_inputs(seed))
    spreads = {'L0_xattn_bq': (0.0, 0.8),
     'L0_xattn_bk': (0.0, 0.8),
     'L0_xattn_bv': (0.0, 0.1),
     'L0_xattn_bo': (0.0, 0.1),
     'L0_ffn_b_enc': (0.0, 0.665),
     'L0_ffn_b_s2c': (0.0, 0.1),
     'L0_ffn_br': (0.0, 0.1),
     'L0_ffn_b1': (0.0, 0.488),
     'L0_ffn_b2': (0.0, 0.375),
     'L0_ffn_b_c2s': (0.0, 0.1),
     'L0_ffn_b_dec': (0.0, 0.1),
     'L0_ffn_ln_g': (1.0, 0.2),
     'L0_ffn_ln_b': (0.0, 0.1)}
    factors = {'L0_xattn_Wq': 8.0, 'L0_xattn_Wk': 8.0}
    for name, (base, spread) in spreads.items():
        noise = np.random.default_rng([zlib.crc32(name.encode()), seed]).standard_normal(out[name].shape)
        drawn = base * np.exp(spread * noise) if base else spread * noise
        out[name] = jnp.asarray(drawn.astype(out[name].dtype))
    for name, factor in factors.items():
        out[name] = (out[name] * factor).astype(out[name].dtype)
    return out
```

```python
from contextlib import ExitStack

import concourse.bass as bass
from concourse import mybir

F32 = mybir.dt.float32
F32R = mybir.dt.float32r
BF16 = mybir.dt.bfloat16
ALU = mybir.AluOpType
ACT = mybir.ActivationFunctionType
AX_X = mybir.AxisListType.X

P = 128
BLK = 512
NQ = 4096
NK = 3202
NK_PAD = 3584
D = 512
DC = D // P
H = 16
HD = 32
HG = P // HD
NG = H // HG
SCALE = HD ** -0.5
EPS = 1e-5
QB = NQ // BLK
KB = NK_PAD // BLK
KT = -(-NK // P)
K_LAST = NK - (KT - 1) * P
MASKED = -1e30
FH = 1024
FC = FH // P
M = 64
E = 8
EH = 512
EC = EH // P


def as_f32(ap):
    return ap.bitcast(F32)


def hold(eng, sem, value, passed):
    eng.wait_ge(sem, value)
    eng.sem_inc(passed, 1)


class Tools:

    def __init__(self, nc, ctx):
        self.nc, self.ctx = nc, ctx

    def sb(self, name, shape, dt=F32):
        return self.ctx.enter_context(self.nc.sbuf_tensor(name, shape, dt))

    def banks(self, n, name):
        return [self.ctx.enter_context(self.nc.psum_tensor(f"{name}{i}", [P, BLK], F32)) for i in range(n)]

    def sem(self, name):
        return self.ctx.enter_context(self.nc.semaphore(name))


def project_keys_values(nc, ctxT, wkT, wvT, bk, bv, kT_hi, kT_lo, v_dram):
    ctx = ExitStack()
    with ctx:
        t = Tools(nc, ctx)
        w_in = t.sb("kv_w_in", [P, 2, DC, D])
        wk_hi, wk_lo = t.sb("wk_hi", [P, DC, D], F32R), t.sb("wk_lo", [P, DC, D], F32R)
        wv_hi, wv_lo = t.sb("wv_hi", [P, DC, D], F32R), t.sb("wv_lo", [P, DC, D], F32R)
        bk_col = t.sb("bk_col", [P, DC])
        bv_all = t.sb("bv_all", [P, D])
        c_in = t.sb("c_in", [P, 2, DC, BLK])
        c_hi, c_lo = t.sb("c_hi", [P, 2, DC, BLK], F32R), t.sb("c_lo", [P, 2, DC, BLK], F32R)
        k_hi, k_lo = t.sb("k_hi", [P, 2, DC, BLK], F32R), t.sb("k_lo", [P, 2, DC, BLK], F32R)
        v_out = t.sb("v_out", [P, 2, DC, D])
        bank = t.banks(4, "kv_bank")

        passed = t.sem("kv_bias_loaded_sp_passed")
        bias_loaded = t.sem("kv_bias_loaded")
        w_loaded = [t.sem("wk_loaded"), t.sem("wv_loaded")]
        w_hi_ready, w_lo_ready = t.sem("kv_w_hi_ready"), t.sem("kv_w_lo_ready")
        c_loaded = [t.sem("c_loaded0"), t.sem("c_loaded1")]
        c_hi_ready, c_lo_ready = t.sem("c_hi_ready"), t.sem("c_lo_ready")
        job_done = t.sem("kv_job_done")
        k_hi_ready = t.sem("k_hi_ready")
        bank_free = t.sem("kv_bank_free")
        k_stored = [t.sem("k_stored0"), t.sem("k_stored1")]
        v_stored = [t.sem("v_stored0"), t.sem("v_stored1")]

        JOBS = 2 * DC
        PAIRS = (KB - 1) // 2
        assert KB == 2 * PAIRS + 1

        def blocks(eng, body):
            with eng.Fori(0, PAIRS) as i:
                for u in range(2):
                    body(2 * i + u, u, i, True)
            body(2 * PAIRS, 0, PAIRS, False)

        with nc.Block() as block:
            @block.sync
            def _(sp):
                sp.dma_start(w_in[:, 0], wkT.rearrange("(c p) n -> p c n", p=P)).then_inc(w_loaded[0], 16)
                sp.dma_start(c_in[:, 0], ctxT[:, 0:BLK].rearrange("(c p) n -> p c n", p=P)).then_inc(c_loaded[0], 16)
                sp.dma_start(w_in[:, 1], wvT.rearrange("(c p) n -> p c n", p=P)).then_inc(w_loaded[1], 16)

                def load_next(b, u, before, more):
                    if more:
                        hold(sp, c_lo_ready, DC * b, passed)
                        sp.dma_start(c_in[:, 1 - u], ctxT[:, bass.ds((b + 1) * BLK, BLK)].rearrange(
                            "(c p) n -> p c n", p=P)).then_inc(c_loaded[1 - u], 16)
                blocks(sp, load_next)

            @block.gpsimd
            def _(pool):
                pool.dma_start(bk_col[:, :], bk).then_inc(bias_loaded, 16)
                pool.dma_start(bv_all[:, :], bv.partition_broadcast(P)).then_inc(bias_loaded, 16)

                def store(b, u, before, more):
                    cols = bass.ds(b * BLK, BLK)
                    pool.wait_ge(bank_free, 4 + JOBS * b + DC)
                    pool.dma_start(kT_hi[:, cols].rearrange("(c p) n -> p c n", p=P), as_f32(k_hi[:, u])).then_inc(k_stored[u], 16)
                    pool.dma_start(kT_lo[:, cols].rearrange("(c p) n -> p c n", p=P), as_f32(k_lo[:, u])).then_inc(k_stored[u], 16)
                    pool.wait_ge(bank_free, 4 + JOBS * b + 2 * DC)
                    pool.dma_start(v_dram[cols, :].rearrange("(t p) n -> p t n", p=P), v_out[:, u]).then_inc(v_stored[u], 16)
                blocks(pool, store)
                for u in range(2):
                    pool.wait_ge(k_stored[u], 32 * (PAIRS + 1 - u))
                    pool.wait_ge(v_stored[u], 16 * (PAIRS + 1 - u))

            @block.scalar
            def _(act):
                for w, hi in enumerate((wk_hi, wv_hi)):
                    act.wait_ge(w_loaded[w], 16)
                    act.activation(hi[:, :, :], w_in[:, w], ACT.Copy).then_inc(w_hi_ready, 1)
                    if w == 0:
                        act.wait_ge(c_loaded[0], 16)
                        for c in range(DC):
                            act.activation(c_hi[:, 0, c], c_in[:, 0, c], ACT.Copy).then_inc(c_hi_ready, 1)

                def body(b, u, before, more):
                    for n in range(DC):
                        act.wait_ge(job_done, JOBS * b + n + 1)
                        if n == 0:
                            act.wait_ge(bias_loaded, 32)
                            act.wait_ge(k_stored[u], 32 * before)
                        act.activation(k_hi[:, u, n], bank[n][:, :], ACT.Identity, bias=bk_col[:, n:n + 1]).then_inc(k_hi_ready, 1)
                    if more:
                        act.wait_ge(c_loaded[1 - u], 16 * (before + 1 + u))
                        for c in range(DC):
                            act.activation(c_hi[:, 1 - u, c], c_in[:, 1 - u, c], ACT.Copy).then_inc(c_hi_ready, 1)
                blocks(act, body)

            @block.vector
            def _(dve):
                dve.sem_inc(bank_free, 4)
                for w, (hi, lo) in enumerate(((wk_hi, wk_lo), (wv_hi, wv_lo))):
                    dve.wait_ge(w_hi_ready, w + 1)
                    dve.tensor_tensor(lo[:, :, :], w_in[:, w], as_f32(hi[:, :, :]), ALU.subtract).then_inc(w_lo_ready, 1)
                    if w == 0:
                        for c in range(DC):
                            dve.wait_ge(c_hi_ready, c + 1)
                            dve.tensor_tensor(c_lo[:, 0, c], c_in[:, 0, c], as_f32(c_hi[:, 0, c]), ALU.subtract).then_inc(c_lo_ready, 1)

                def body(b, u, before, more):
                    dve.wait_ge(bias_loaded, 32)
                    for n in range(DC):
                        dve.wait_ge(k_hi_ready, DC * b + n + 1)
                        dve.scalar_tensor_tensor(k_lo[:, u, n], bank[n][:, :], bk_col[:, n:n + 1], as_f32(k_hi[:, u, n]),
                                                 ALU.add, ALU.subtract).then_inc(bank_free, 1)
                    for n in range(DC):
                        dve.wait_ge(job_done, JOBS * b + DC + n + 1)
                        if n == 0:
                            dve.wait_ge(v_stored[u], 16 * before)
                        dve.tensor_tensor(v_out[:, u, n], bank[n][:, :], bv_all[:, :], ALU.add).then_inc(bank_free, 1)
                        if more:
                            dve.wait_ge(c_hi_ready, DC * (b + 1) + n + 1)
                            dve.tensor_tensor(c_lo[:, 1 - u, n], c_in[:, 1 - u, n], as_f32(c_hi[:, 1 - u, n]),
                                              ALU.subtract).then_inc(c_lo_ready, 1)
                blocks(dve, body)

            @block.tensor
            def _(pe):
                pe.wait_ge(w_lo_ready, 1)

                def body(b, u, before, more):
                    pe.wait_ge(c_lo_ready, DC * (b + 1))
                    for n in range(JOBS):
                        pe.wait_ge(bank_free, JOBS * b + n + 1)
                        if n == DC:
                            pe.wait_ge(w_lo_ready, 2)
                        first = True
                        for c in range(DC):
                            if n < DC:
                                cols = slice(n * P, (n + 1) * P)
                                terms = [(wk_hi[:, c, cols], c_hi[:, u, c]), (wk_hi[:, c, cols], c_lo[:, u, c]),
                                         (wk_lo[:, c, cols], c_hi[:, u, c])]
                            else:
                                cols = slice((n - DC) * P, (n - DC + 1) * P)
                                terms = [(c_hi[:, u, c, cols], wv_hi[:, c]), (c_hi[:, u, c, cols], wv_lo[:, c]),
                                         (c_lo[:, u, c, cols], wv_hi[:, c])]
                            for k, (lhsT, rhs) in enumerate(terms):
                                mm = pe.matmul(bank[n % DC][:, :], lhsT, rhs, start=first, stop=(c == DC - 1 and k == 2))
                                first = False
                        mm.then_inc(job_done, 1)
                blocks(pe, body)


def project_queries(nc, x, wqT, bq, ident, neg_half, eps, qT_hi, qT_lo):
    ctx = ExitStack()
    with ctx:
        t = Tools(nc, ctx)
        w_in = t.sb("q_w_in", [P, DC, D])
        wq_hi, wq_lo = t.sb("wq_hi", [P, DC, D], F32R), t.sb("wq_lo", [P, DC, D], F32R)
        bq_col = t.sb("bq_col", [P, DC])
        x_in = t.sb("x_in", [P, 2, 4, D])
        xn = t.sb("xn", [P, 2, 4, D])
        stats = t.sb("q_stats", [P, 2, 4, 6])
        mean_var = t.sb("q_mean_var", [P, 2, 4, 2])
        var_eps = t.sb("q_var_eps", [P, 2, 4])
        rstd = t.sb("q_rstd", [P, 2, 4])
        xT_hi, xT_lo = t.sb("xT_hi", [P, 2, DC, BLK], F32R), t.sb("xT_lo", [P, 2, DC, BLK], F32R)
        q_hi, q_lo = t.sb("q_hi", [P, 2, DC, BLK], F32R), t.sb("q_lo", [P, 2, DC, BLK], F32R)
        bank = t.banks(4, "q_bank")
        tbank = t.banks(4, "q_tbank")

        passed = t.sem("q_bias_loaded_sp_passed")
        bias_loaded, w_loaded = t.sem("q_bias_loaded"), t.sem("wq_loaded")
        w_hi_ready, w_lo_ready = t.sem("wq_hi_ready"), t.sem("wq_lo_ready")
        x_loaded = [t.sem("x_loaded0"), t.sem("x_loaded1")]
        stats_ready, mv_ready, eps_ready = t.sem("q_stats_ready"), t.sem("q_mv_ready"), t.sem("q_eps_ready")
        passed_dve = t.sem("q_dve_passed")
        rstd_ready, xn_ready = t.sem("q_rstd_ready"), t.sem("xn_ready")
        xT_done = t.sem("xT_done")
        xT_hi_ready, xT_lo_ready = t.sem("xT_hi_ready"), t.sem("xT_lo_ready")
        job_done, q_hi_ready, q_lo_ready = t.sem("q_job_done"), t.sem("q_hi_ready"), t.sem("q_lo_ready")
        q_stored = [t.sem("q_stored0"), t.sem("q_stored1")]
        PAIRS = QB // 2 - 1

        def blocks(eng, prepare, process):
            prepare(0, 0, 0)
            with eng.Fori(0, PAIRS) as i:
                for u in range(2):
                    process(2 * i + u, u, i, prepare and (lambda: prepare(2 * i + u + 1, 1 - u, i + u)))
            process(2 * PAIRS, 0, PAIRS, lambda: prepare(2 * PAIRS + 1, 1, PAIRS))
            process(2 * PAIRS + 1, 1, PAIRS, None)

        with nc.Block() as block:
            @block.sync
            def _(sp):
                sp.dma_start(w_in[:, :, :], wqT.rearrange("(c p) n -> p c n", p=P)).then_inc(w_loaded, 16)

                def process(b, u, before, prepare_next):
                    if prepare_next:
                        hold(sp, xn_ready, 4 * b, passed)
                        sp.dma_start(x_in[:, 1 - u], x[bass.ds((b + 1) * BLK, BLK), :].rearrange(
                            "(t p) n -> p t n", p=P)).then_inc(x_loaded[1 - u], 16)

                def first(b, u, before):
                    sp.dma_start(x_in[:, 0], x[0:BLK, :].rearrange("(t p) n -> p t n", p=P)).then_inc(x_loaded[0], 16)
                blocks(sp, first, process)

            @block.gpsimd
            def _(pool):
                pool.dma_start(bq_col[:, :], bq).then_inc(bias_loaded, 16)

                def prepare(b, u, before):
                    pool.wait_ge(mv_ready, 4 * (b + 1))
                    pool.tensor_tensor(var_eps[:, u], mean_var[:, u, :, 1], eps[:, :], ALU.add).then_inc(eps_ready, 1)
                    pool.wait_ge(eps_ready, b + 1)
                    pool.tensor_tensor(rstd[:, u], var_eps[:, u], neg_half[:, 0:4], ALU.pow).then_inc(rstd_ready, 1)

                def process(b, u, before, prepare_next):
                    if prepare_next:
                        prepare_next()
                    cols = bass.ds(b * BLK, BLK)
                    pool.wait_ge(q_lo_ready, 4 + DC * (b + 1))
                    pool.dma_start(qT_hi[:, cols].rearrange("(c p) n -> p c n", p=P), as_f32(q_hi[:, u])).then_inc(q_stored[u], 16)
                    pool.dma_start(qT_lo[:, cols].rearrange("(c p) n -> p c n", p=P), as_f32(q_lo[:, u])).then_inc(q_stored[u], 16)
                blocks(pool, prepare, process)
                for u in range(2):
                    pool.wait_ge(q_stored[u], 32 * (QB // 2))

            @block.scalar
            def _(act):
                act.wait_ge(w_loaded, 16)
                act.activation(wq_hi[:, :, :], w_in[:, :, :], ACT.Copy).then_inc(w_hi_ready, 1)

                def prepare(b, u, before):
                    for c in range(DC):
                        act.wait_ge(xT_done, DC * b + c + 1)
                        act.activation(xT_hi[:, u, c], tbank[c][:, :], ACT.Copy).then_inc(xT_hi_ready, 1)

                def process(b, u, before, prepare_next):
                    for n in range(DC):
                        if n == 2 and prepare_next:
                            prepare_next()
                        act.wait_ge(job_done, DC * b + n + 1)
                        if n == 0:
                            act.wait_ge(bias_loaded, 16)
                            act.wait_ge(q_stored[u], 32 * before)
                        act.activation(q_hi[:, u, n], bank[n][:, :], ACT.Identity, bias=bq_col[:, n:n + 1]).then_inc(q_hi_ready, 1)
                blocks(act, prepare, process)

            @block.vector
            def _(dve):
                def normalise_stats(b, u):
                    for k in range(4):
                        dve.bn_stats(stats[:, u, k], x_in[:, u, k]).then_inc(stats_ready, 1)
                    hold(dve, stats_ready, 4 * (b + 1), passed_dve)
                    for k in range(4):
                        dve.bn_aggr(mean_var[:, u, k], stats[:, u, k]).then_inc(mv_ready, 1)

                def normalise(b, u):
                    dve.wait_ge(rstd_ready, b + 1)
                    for k in range(4):
                        dve.tensor_scalar(xn[:, u, k], x_in[:, u, k], mean_var[:, u, k, 0:1], rstd[:, u, k:k + 1],
                                          ALU.subtract, ALU.mult).then_inc(xn_ready, 1)

                def low_parts(b, u):
                    for c in range(DC):
                        dve.wait_ge(xT_hi_ready, DC * b + c + 1)
                        dve.tensor_tensor(xT_lo[:, u, c], tbank[c][:, :], as_f32(xT_hi[:, u, c]), ALU.subtract).then_inc(xT_lo_ready, 1)

                def q_low(b, u, n):
                    dve.wait_ge(q_hi_ready, DC * b + n + 1)
                    dve.scalar_tensor_tensor(q_lo[:, u, n], bank[n][:, :], bq_col[:, n:n + 1], as_f32(q_hi[:, u, n]),
                                             ALU.add, ALU.subtract).then_inc(q_lo_ready, 1)

                def first(b, u, before):
                    dve.sem_inc(q_lo_ready, 4)
                    dve.wait_ge(x_loaded[0], 16)
                    normalise_stats(0, 0)
                    normalise(0, 0)
                    low_parts(0, 0)
                    dve.wait_ge(w_hi_ready, 1)
                    dve.tensor_tensor(wq_lo[:, :, :], w_in[:, :, :], as_f32(wq_hi[:, :, :]), ALU.subtract).then_inc(w_lo_ready, 1)
                    dve.wait_ge(bias_loaded, 16)

                def process(b, u, before, prepare_next):
                    if prepare_next:
                        dve.wait_ge(x_loaded[1 - u], 16 * (before + 1 + u))
                        normalise_stats(b + 1, 1 - u)
                    q_low(b, u, 0)
                    if prepare_next:
                        normalise(b + 1, 1 - u)
                    q_low(b, u, 1)
                    if prepare_next:
                        low_parts(b + 1, 1 - u)
                    q_low(b, u, 2)
                    q_low(b, u, 3)
                blocks(dve, first, process)

            @block.tensor
            def _(pe):
                def prepare(b, u, before):
                    pe.wait_ge(xn_ready, 4 * (b + 1))
                    pe.wait_ge(xT_lo_ready, DC * b)
                    for c in range(DC):
                        for k in range(4):
                            mm = pe.transpose(tbank[c][:, k * P:(k + 1) * P], xn[:, u, k, c * P:(c + 1) * P], ident[:, :])
                        mm.then_inc(xT_done, 1)

                def process(b, u, before, prepare_next):
                    for n in range(DC):
                        if n == 2 and prepare_next:
                            prepare_next()
                        if n == 0:
                            pe.wait_ge(xT_lo_ready, DC * (b + 1))
                            pe.wait_ge(w_lo_ready, 1)
                        pe.wait_ge(q_lo_ready, DC * b + n + 1)
                        for c in range(DC):
                            cols = slice(n * P, (n + 1) * P)
                            for k, (w, xx) in enumerate(((wq_hi, xT_hi), (wq_hi, xT_lo), (wq_lo, xT_hi))):
                                mm = pe.matmul(bank[n][:, :], w[:, c, cols], xx[:, u, c],
                                               start=(c == 0 and k == 0), stop=(c == DC - 1 and k == 2))
                        mm.then_inc(job_done, 1)
                blocks(pe, prepare, process)


R_HI, R_MID, R_LO, R_MAX = 0, HD, 2 * HD, 3 * HD
R_END = R_MAX + 2 * HG
SLOTS = 4
QBUFS = 3


def key_tiles(j):
    return min(4 * j + 4, KT)


def key_chunks(j):
    return min(j + 1, KB)


STEPS = [(j, kt) for j in range(QB) for kt in range(key_tiles(j))]
ST = len(STEPS)
FIRST_STEP = [STEPS.index((j, 0)) for j in range(QB)] + [ST]


def pool_sums(j, kt):
    return j > 0 and kt % 3 != 2 and kt < key_tiles(j) - 2


def pool_adds(j, kt):
    return pool_sums(j, kt) and kt != 0


PO = sum(pool_adds(j, kt) for j, kt in STEPS)
PO_BEFORE = [sum(pool_adds(j, kt) for j, kt in STEPS[:s]) for s in range(ST + 1)]


def max_units(j):
    units = []
    for r in range(4):
        seen = min((4 * j + r + 1) * P, NK)
        for h in range(HG):
            for c in range(key_chunks(j)):
                n = min(BLK, seen - c * BLK)
                first_masked = (4 * j + r) * P - c * BLK
                masked = min(P, n - first_masked) if first_masked < n else 0
                units.append((r, h, c, n, first_masked, masked))
    return units


UNITS = [max_units(j) for j in range(QB)]
NU = sum(map(len, UNITS))
UNITS_BEFORE = [sum(map(len, UNITS[:j])) for j in range(QB + 1)]


def spread(j):
    n = len(UNITS[j + 1]) if j + 1 < QB else 0
    quarters = 4 * (key_tiles(j) - 2)
    return [[n * (4 * s + k + 1) // quarters - n * (4 * s + k) // quarters if s < key_tiles(j) - 2 else 0
             for k in range(4)] for s in range(key_tiles(j))]


def attend(nc, qT_hi, qT_lo, kT_hi, kT_lo, v_dram, aT, ident_b, mask, maskT, head_rows):
    ctx = ExitStack()
    with ctx:
        t = Tools(nc, ctx)
        k_sb = t.sb("k_sb", [P, HG, KT * P], F32R)
        v_sb = t.sb("v_sb", [P, KT, P])
        q_sb = [t.sb(f"q_sb{i}", [P, HG, BLK], F32R) for i in range(QBUFS)]
        pT = t.sb("pT", [P, SLOTS, HG, BLK])
        ones = t.sb("ones", [P, HD])
        part_sum = t.sb("part_sum", [P, 2, HG, BLK])
        row_max = t.sb("row_max", [P, 2, 4, HG, KB])
        neg_max = t.sb("neg_max", [P, 4, HG])
        neg_parts = t.sb("neg_parts", [P, 4, HG, 2], BF16)
        o_sb, den_sb = t.sb("o_sb", [P, 2, BLK]), t.sb("den_sb", [P, 2, BLK])
        rden, a_out = t.sb("rden", [P, BLK]), t.sb("a_out", [P, 2, BLK])
        s_bank = ctx.enter_context(nc.psum_tensor("s_bank", [P, HG, BLK], F32))
        m_bank = t.banks(2, "m_bank")
        [o_bank] = t.banks(1, "o_bank")
        [den_bank] = t.banks(1, "den_bank")

        passed = t.sem("att_const_ready_sp_passed")
        passed_pe = t.sem("att_pe_passed")
        const_ready = t.sem("att_const_ready")
        q_loaded = [t.sem(f"q_loaded{i}") for i in range(QBUFS)]
        k_loaded = [t.sem(f"k_loaded{c}") for c in range(KB)]
        v_loaded = [t.sem(f"v_loaded{c}") for c in range(KB)]
        unit_done, unit_max = t.sem("unit_done"), t.sem("unit_max")
        neg_ready = t.sem("neg_ready")
        maxT_done, max_rows = t.sem("maxT_done"), t.sem("max_rows")
        s_done = t.sem("s_done")
        exp_done = t.sem("exp_done")
        p_used = t.sem("p_used")
        pool_added = t.sem("pool_added")
        block_done, block_copied = t.sem("block_done"), t.sem("block_copied")
        rden_ready, a_ready = t.sem("rden_ready"), t.sem("a_ready")
        a_stored = [t.sem("a_stored0"), t.sem("a_stored1")]

        q_uses = [len([j for j in range(QB) if j % QBUFS == i]) for i in range(QBUFS)]

        with nc.Block() as block:
            @block.sync
            def _(sp):
                with sp.Fori(0, NG) as g:
                    def load_q(j):
                        buf = j % QBUFS
                        prev = j - QBUFS if j >= QBUFS else max(i for i in range(QB) if i % QBUFS == buf)
                        last = FIRST_STEP[prev + 1] + (ST if j >= QBUFS else 0)
                        hold(sp, s_done, 2 * ST * g + 2 * last, passed)
                        for row, src in ((R_HI, qT_hi), (R_MID, qT_lo), (R_LO, qT_hi)):
                            sp.dma_start(as_f32(q_sb[buf][row:row + HD, :, :]),
                                         src[bass.ds(g * P, P), j * BLK:(j + 1) * BLK].rearrange("(h d) n -> d h n", d=HD)
                                         ).then_inc(q_loaded[buf], 16)

                    load_q(0)
                    for c in range(KB):
                        n = min(BLK, KT * P - c * BLK)
                        last = FIRST_STEP[QB - 1] + min(4 * c + 4, KT)
                        hold(sp, s_done, 2 * ST * g + 2 * last, passed)
                        for row, src in ((R_HI, kT_hi), (R_MID, kT_hi), (R_LO, kT_lo)):
                            sp.dma_start(as_f32(k_sb[row:row + HD, :, c * BLK:c * BLK + n]),
                                         src[bass.ds(g * P, P), c * BLK:c * BLK + n].rearrange("(h d) n -> d h n", d=HD)
                                         ).then_inc(k_loaded[c], 16)
                        hold(sp, p_used, ST * g + last, passed)
                        sp.dma_start(v_sb[:, 4 * c:4 * c + n // P, :],
                                     v_dram[c * BLK:c * BLK + n, bass.ds(g * P, P)].rearrange("(t p) n -> p t n", p=P)
                                     ).then_inc(v_loaded[c], 16)
                        if c == 0:
                            load_q(2)
                    load_q(1)
                    for j in range(QBUFS, QB):
                        load_q(j)

            @block.gpsimd
            def _(pool):
                pool.memset(ones[:, :], 1.0).then_inc(const_ready, 1)
                with pool.Fori(0, NG) as g:
                    for s, (j, kt) in enumerate(STEPS):
                        if not pool_adds(j, kt):
                            continue
                        if kt == 1:
                            pool.wait_ge(block_done, (QB - 1) * g + max(0, j - 2))
                        pool.wait_ge(exp_done, 2 * ST * g + 2 * (s + 1))
                        pool.wait_ge(pool_added, PO * g + PO_BEFORE[s])
                        q0 = max(0, kt - 4 * j) * P
                        total = part_sum[:, j % 2, :, q0:]
                        pool.tensor_tensor(total, pT[:, (s - 1) % SLOTS, :, q0:] if kt == 1 else total,
                                           pT[:, s % SLOTS, :, q0:], ALU.add).then_inc(pool_added, 1)

            @block.scalar
            def _(act):
                with act.Fori(0, NG) as g:
                    def copy_block(j):
                        if j == 0:
                            act.wait_ge(p_used, ST * g + ST + key_tiles(0))
                        else:
                            act.wait_ge(block_done, (QB - 1) * g + j)
                        act.wait_ge(a_ready, QB * g + max(0, j - 1))
                        act.activation(o_sb[:, j % 2], o_bank[:, :], ACT.Copy).then_inc(block_copied, 1)
                        act.activation(den_sb[:, j % 2], den_bank[:, :], ACT.Copy).then_inc(block_copied, 1)

                    def store_block(j):
                        act.wait_ge(a_ready, QB * g + j + 1)
                        act.dma_start(aT[bass.ds(g * P, P), j * BLK:(j + 1) * BLK], a_out[:, j % 2]).then_inc(a_stored[j % 2], 16)

                    def max_to_rows(j):
                        act.wait_ge(maxT_done, QB * g + j + 1)
                        rows = slice(R_MAX, R_END)
                        n = UNITS_BEFORE[j + 1] + j
                        src = m_bank[n % 2][rows, :].unsqueeze(1).to_broadcast([R_END - R_MAX, HG, BLK])
                        act.activation(q_sb[j % QBUFS][rows, :, :], src, ACT.Copy).then_inc(max_rows, 1)

                    max_to_rows(0)
                    for s, (j, kt) in enumerate(STEPS):
                        q0 = max(0, kt - 4 * j) * P
                        rows = P if kt < KT - 1 else K_LAST
                        act.wait_ge(p_used, ST * g + ST + s + 1 - SLOTS)
                        act.wait_ge(pool_added, PO * g + (PO_BEFORE[s - SLOTS + 1 + (STEPS[s - SLOTS][1] == 0)] if s >= SLOTS else 0))
                        for p in range(2):
                            act.wait_ge(s_done, 2 * ST * g + 2 * ST + 2 * s + p + 1)
                            act.activation(pT[0:rows, s % SLOTS, 2 * p:2 * p + 2, q0:], s_bank[0:rows, 2 * p:2 * p + 2, q0:],
                                           ACT.Exp, scale=SCALE).then_inc(exp_done, 1)
                        if kt == 0 and j > 0:
                            copy_block(j - 1)
                        if kt == 7:
                            store_block(j - 1)
                        if kt == key_tiles(j) - 2 and j + 1 < QB:
                            max_to_rows(j + 1)
                    copy_block(QB - 1)
                    store_block(QB - 1)
                for i in range(2):
                    act.wait_ge(a_stored[i], 16 * NG * QB // 2)

            @block.vector
            def _(dve):
                for h in range(HG):
                    dve.tensor_copy(k_sb[R_MAX:R_END, h, :], head_rows[R_MAX:R_END, h:h + 1].to_broadcast([R_END - R_MAX, KT * P])
                                    ).then_inc(const_ready, 1)
                with dve.Fori(0, NG) as g:
                    def take_max(j, i):
                        r, h, c, n, _, _ = UNITS[j][i]
                        k = UNITS_BEFORE[j] + i
                        dve.wait_ge(unit_done, NU * g + k + 1)
                        dve.tensor_reduce(row_max[:, j % 2, r, h, c:c + 1], m_bank[(k + j) % 2][:, 0:n], AX_X, ALU.max
                                          ).then_inc(unit_max, 1)

                    def negate(j):
                        dve.wait_ge(unit_max, NU * g + UNITS_BEFORE[j + 1])
                        dve.tensor_reduce(neg_max[:, :, :], row_max[:, j % 2, :, :, 0:key_chunks(j)], AX_X, ALU.max,
                                          negate=True).then_inc(neg_ready, 1)
                        dve.wait_ge(neg_ready, 3 * QB * g + 3 * j + 1)
                        dve.wait_ge(maxT_done, QB * g + j)
                        dve.tensor_copy(neg_parts[:, :, :, 0], neg_max[:, :, :]).then_inc(neg_ready, 1)
                        dve.wait_ge(neg_ready, 3 * QB * g + 3 * j + 2)
                        dve.tensor_tensor(neg_parts[:, :, :, 1], neg_max[:, :, :], neg_parts[:, :, :, 0], ALU.subtract
                                          ).then_inc(neg_ready, 1)

                    def invert(j, quarter):
                        if quarter == 0:
                            dve.wait_ge(block_copied, 2 * QB * g + 2 * j + 2)
                        cols = slice(quarter * P, (quarter + 1) * P)
                        dve.reciprocal(rden[:, cols], den_sb[:, j % 2, cols]).then_inc(rden_ready, 1)

                    def normalise(j):
                        dve.wait_ge(rden_ready, 4 * (QB * g + j + 1))
                        dve.wait_ge(a_stored[j % 2], 16 * (QB // 2 * g + j // 2))
                        dve.tensor_tensor(a_out[:, j % 2], o_sb[:, j % 2], rden[:, :], ALU.mult).then_inc(a_ready, 1)

                    for i in range(len(UNITS[0])):
                        take_max(0, i)
                    negate(0)
                    for j in range(QB):
                        at = 0
                        plan = spread(j)
                        for kt in range(key_tiles(j)):
                            for n in plan[kt]:
                                for _ in range(n):
                                    take_max(j + 1, at)
                                    at += 1
                            if j > 0 and kt < 4:
                                invert(j - 1, kt)
                            if j > 0 and kt == 4:
                                normalise(j - 1)
                            if kt == key_tiles(j) - 3 and j + 1 < QB:
                                negate(j + 1)
                    for quarter in range(4):
                        invert(QB - 1, quarter)
                    normalise(QB - 1)

            @block.tensor
            def _(pe):
                pe.sem_inc(s_done, 2 * ST)
                pe.sem_inc(p_used, ST)
                pe.wait_ge(const_ready, 1 + HG)
                with pe.Fori(0, NG) as g:
                    def bank_free(n):
                        if n < 2:
                            pe.wait_ge(unit_max, NU * g)
                            pe.wait_ge(max_rows, QB * g)
                            return
                        k, j = n - 2, 0
                        while k > UNITS_BEFORE[j + 1] + j:
                            j += 1
                        if k == UNITS_BEFORE[j + 1] + j:
                            pe.wait_ge(max_rows, QB * g + j + 1)
                        else:
                            pe.wait_ge(unit_max, NU * g + k - j + 1)

                    def unit(j, i):
                        r, h, c, n, first_masked, masked = UNITS[j][i]
                        k = UNITS_BEFORE[j] + i + j
                        if i == 0:
                            pe.wait_ge(q_loaded[j % QBUFS], 48 * (q_uses[j % QBUFS] * g + j // QBUFS + 1))
                        if c == j and r == 0 and h == 0:
                            pe.wait_ge(k_loaded[c], 48 * (g + 1))
                        bank_free(k)
                        out = m_bank[k % 2]
                        mm = pe.matmul(out[:, 0:n], q_sb[j % QBUFS][0:R_MAX, h, r * P:(r + 1) * P],
                                       k_sb[0:R_MAX, h, c * BLK:c * BLK + n], start=True, stop=not masked)
                        if masked:
                            mm = pe.matmul(out[:, first_masked:n], ident_b[:, :], mask[:, 0:masked], start=False, stop=True)
                        mm.then_inc(unit_done, 1)

                    def transpose_max(j):
                        pe.wait_ge(neg_ready, 3 * (QB * g + j + 1))
                        n = UNITS_BEFORE[j + 1] + j
                        bank_free(n)
                        for r in range(4):
                            mm = pe.matmul(m_bank[n % 2][R_MAX:R_END, r * P:(r + 1) * P],
                                           neg_parts[:, r].rearrange("p h k -> p (h k)"), ident_b[:, :], start=True, stop=True)
                        mm.then_inc(maxT_done, 1)

                    def scores(s, p):
                        j, kt = STEPS[s]
                        q0 = max(0, kt - 4 * j) * P
                        if p == 0 and kt == 0:
                            pe.wait_ge(max_rows, QB * g + j + 1)
                        pe.wait_ge(exp_done, 2 * ST * g + (2 * s + p - 1 if s else 0))
                        for h in (2 * p, 2 * p + 1):
                            mm = pe.matmul(s_bank[:, h, q0:], k_sb[0:R_END, h, kt * P:(kt + 1) * P],
                                           q_sb[j % QBUFS][0:R_END, h, q0:], start=True, stop=kt < 4 * j)
                            if kt >= 4 * j:
                                mm = pe.matmul(s_bank[:, h, q0:q0 + P], ident_b[:, :], maskT[:, :], start=False, stop=True)
                        mm.then_inc(s_done, 1)

                    def weigh_values(s):
                        j, kt = STEPS[s]
                        q0 = max(0, kt - 4 * j) * P
                        rows = P if kt < KT - 1 else K_LAST
                        hold(pe, exp_done, 2 * ST * g + 2 * (s + 1), passed_pe)
                        if kt % 4 == 0 and kt // 4 == j:
                            pe.wait_ge(v_loaded[j], 16 * (g + 1))
                        if kt == 0:
                            pe.wait_ge(block_copied, 2 * (QB * g + j))
                        for h in range(HG):
                            mm = pe.matmul(o_bank[h * HD:(h + 1) * HD, q0:], v_sb[0:rows, kt, h * HD:(h + 1) * HD],
                                           pT[0:rows, s % SLOTS, h, q0:], start=kt == 0, stop=kt == key_tiles(j) - 1)
                        if pool_sums(j, kt):
                            mm.then_inc(p_used, 1)

                    def denominators(s):
                        j, kt = STEPS[s]
                        last = kt == key_tiles(j) - 1
                        if not pool_sums(j, kt):
                            q0 = max(0, kt - 4 * j) * P
                            rows = P if kt < KT - 1 else K_LAST
                            for h in range(HG):
                                mm = pe.matmul(den_bank[h * HD:(h + 1) * HD, q0:], ones[0:rows, :], pT[0:rows, s % SLOTS, h, q0:],
                                               start=kt == (2 if j else 0), stop=j == 0 and last)
                            mm.then_inc(p_used, 1)
                        if last and j > 0:
                            pe.wait_ge(pool_added, PO * g + PO_BEFORE[s + 1])
                            for h in range(HG):
                                mm = pe.matmul(den_bank[h * HD:(h + 1) * HD, :], ones[:, :], part_sum[:, j % 2, h], start=False, stop=True)
                            mm.then_inc(block_done, 1)

                    for i in range(len(UNITS[0])):
                        unit(0, i)
                    transpose_max(0)
                    for j in range(QB):
                        at = 0
                        plan = spread(j)
                        for kt in range(key_tiles(j)):
                            s = FIRST_STEP[j] + kt
                            work = [lambda: scores(s, 0), lambda: scores(s, 1), lambda: s and weigh_values(s - 1),
                                    lambda: s and denominators(s - 1)]
                            if kt == key_tiles(j) - 2 and j + 1 < QB:
                                transpose_max(j + 1)
                            for do, n in zip(work, plan[kt]):
                                do()
                                for _ in range(n):
                                    unit(j + 1, at)
                                    at += 1
                    weigh_values(ST - 1)
                    denominators(ST - 1)


def project_output(nc, x, aT, woT, bo, ident, neg_half, eps, x1_dram, xT_hi, xT_lo):
    ctx = ExitStack()
    with ctx:
        t = Tools(nc, ctx)
        w_in = t.sb("o_w_in", [P, DC, D])
        wo_hi, wo_lo = t.sb("wo_hi", [P, DC, D], F32R), t.sb("wo_lo", [P, DC, D], F32R)
        bo_all = t.sb("bo_all", [P, D])
        a_in = t.sb("a_in", [P, 2, DC, BLK])
        a_hi, a_lo = t.sb("a_hi", [P, 2, DC, BLK], F32R), t.sb("a_lo", [P, 2, DC, BLK], F32R)
        x_in = t.sb("o_x_in", [P, 2, 4, D])
        x1 = t.sb("x1", [P, 2, 4, D])
        xn = t.sb("o_xn", [P, 2, 4, D])
        stats = t.sb("o_stats", [P, 2, 4, 6])
        mean_var = t.sb("o_mean_var", [P, 2, 4, 2])
        var_eps = t.sb("o_var_eps", [P, 2, 4])
        rstd = t.sb("o_rstd", [P, 2, 4])
        t_hi, t_lo = t.sb("t_hi", [P, DC, BLK], F32R), t.sb("t_lo", [P, DC, BLK], F32R)
        bank, tbank = t.banks(4, "o_job_bank"), t.banks(4, "o_tbank")

        passed = t.sem("wo_loaded_sp_passed")
        w_loaded, bias_loaded = t.sem("wo_loaded"), t.sem("o_bias_loaded")
        w_hi_ready, w_lo_ready = t.sem("wo_hi_ready"), t.sem("wo_lo_ready")
        a_loaded = [t.sem("a_loaded0"), t.sem("a_loaded1")]
        x_loaded = [t.sem("o_x_loaded0"), t.sem("o_x_loaded1")]
        a_hi_ready, a_lo_ready, xb_ready = t.sem("a_hi_ready"), t.sem("a_lo_ready"), t.sem("o_xb_ready")
        job_done, x1_ready = t.sem("o_job_done"), t.sem("x1_ready")
        mv_ready, eps_ready, rstd_ready = t.sem("o_mv_ready"), t.sem("o_eps_ready"), t.sem("o_rstd_ready")
        stats_ready, passed_dve = t.sem("o_stats_ready"), t.sem("o_dve_passed")
        xn_ready, t_done = t.sem("o_xn_ready"), t.sem("o_t_done")
        t_hi_ready, t_lo_ready = t.sem("o_t_hi_ready"), t.sem("o_t_lo_ready")
        x1_stored = [t.sem("x1_stored0"), t.sem("x1_stored1")]
        t_stored = t.sem("t_stored")
        PAIRS = QB // 2 - 1

        def blocks(eng, ahead, process, behind):
            ahead(0, 0, 0)
            ahead(1, 1, 0)
            process(0, 0, 0)
            with eng.Fori(0, PAIRS) as i:
                for k in (1, 2):
                    u = k % 2
                    ahead(2 * i + k + 1, 1 - u, i + 1)
                    process(2 * i + k, u, i + k - 1)
                    behind(2 * i + k - 1, 1 - u, i)
            process(QB - 1, 1, PAIRS)
            behind(QB - 2, 0, PAIRS)
            behind(QB - 1, 1, PAIRS)

        def nothing(b, u, before):
            pass

        with nc.Block() as block:
            @block.sync
            def _(sp):
                sp.dma_start(w_in[:, :, :], woT.rearrange("(c p) n -> p c n", p=P)).then_inc(w_loaded, 16)
                sp.dma_start(bo_all[:, :], bo.partition_broadcast(P)).then_inc(bias_loaded, 16)

                def store(b, u, before):
                    rows = bass.ds(b * BLK, BLK)
                    hold(sp, x1_ready, 4 * (b + 1), passed)
                    sp.dma_start(x1_dram[rows, :].rearrange("(t p) n -> p t n", p=P), x1[:, u]).then_inc(x1_stored[u], 16)

                def store_t(b, u, before):
                    cols = bass.ds(b * BLK, BLK)
                    hold(sp, t_lo_ready, DC * (b + 1), passed)
                    sp.dma_start(xT_hi[:, cols].rearrange("(c p) n -> p c n", p=P), as_f32(t_hi[:, :, :])).then_inc(t_stored, 16)
                    sp.dma_start(xT_lo[:, cols].rearrange("(c p) n -> p c n", p=P), as_f32(t_lo[:, :, :])).then_inc(t_stored, 16)

                def load(b, u, before):
                    hold(sp, a_lo_ready, DC * (b - 1) if not isinstance(b, int) else DC * max(0, b - 1), passed)
                    hold(sp, x1_ready, 4 * (b - 1) if not isinstance(b, int) else 4 * max(0, b - 1), passed)
                    cols = bass.ds(b * BLK, BLK)
                    sp.dma_start(a_in[:, u], aT[:, cols].rearrange("(c p) n -> p c n", p=P)).then_inc(a_loaded[u], 16)
                    sp.dma_start(x_in[:, u], x[cols, :].rearrange("(t p) n -> p t n", p=P)).then_inc(x_loaded[u], 16)
                blocks(sp, load, store, store_t)
                for u in range(2):
                    hold(sp, x1_stored[u], 16 * (QB // 2), passed)
                hold(sp, t_stored, 32 * QB, passed)

            @block.scalar
            def _(act):
                act.wait_ge(w_loaded, 16)
                act.activation(wo_hi[:, :, :], w_in[:, :, :], ACT.Copy).then_inc(w_hi_ready, 1)

                def split(b, u, before):
                    act.wait_ge(a_loaded[u], 16 * (before + 1))
                    act.wait_ge(job_done, 4 * (b - 1) if not isinstance(b, int) else 0)
                    for c in range(DC):
                        act.activation(a_hi[:, u, c], a_in[:, u, c], ACT.Copy).then_inc(a_hi_ready, 1)

                def copy_t(b, u, before):
                    act.wait_ge(t_stored, 32 * b)
                    for c in range(DC):
                        act.wait_ge(t_done, DC * b + c + 1)
                        act.activation(t_hi[:, c], tbank[c][:, :], ACT.Copy).then_inc(t_hi_ready, 1)
                blocks(act, split, nothing, copy_t)

            @block.gpsimd
            def _(pool):
                pool.wait_ge(bias_loaded, 16)

                def split(b, u, before):
                    for c in range(DC):
                        pool.wait_ge(a_hi_ready, DC * b + c + 1)
                        pool.tensor_tensor(a_lo[:, u, c], a_in[:, u, c], as_f32(a_hi[:, u, c]), ALU.subtract).then_inc(a_lo_ready, 1)
                    pool.wait_ge(x_loaded[u], 16 * (before + 1))
                    for k in range(4):
                        pool.tensor_tensor(x_in[:, u, k], x_in[:, u, k], bo_all[:, :], ALU.add).then_inc(xb_ready, 1)

                def invert(b, u, before):
                    pool.wait_ge(mv_ready, 4 * (b + 1))
                    pool.tensor_tensor(var_eps[:, u], mean_var[:, u, :, 1], eps[:, :], ALU.add).then_inc(eps_ready, 1)
                    pool.wait_ge(eps_ready, b + 1)
                    pool.tensor_tensor(rstd[:, u], var_eps[:, u], neg_half[:, 0:4], ALU.pow).then_inc(rstd_ready, 1)
                blocks(pool, split, invert, nothing)

            @block.vector
            def _(dve):
                dve.wait_ge(w_hi_ready, 1)
                dve.tensor_tensor(wo_lo[:, :, :], w_in[:, :, :], as_f32(wo_hi[:, :, :]), ALU.subtract).then_inc(w_lo_ready, 1)

                def residual(b, u, before):
                    dve.wait_ge(x1_stored[u], 16 * before)
                    for k in range(4):
                        dve.wait_ge(job_done, 4 * b + k + 1)
                        dve.wait_ge(xb_ready, 4 * b + k + 1)
                        dve.tensor_tensor(x1[:, u, k], bank[k][:, :], x_in[:, u, k], ALU.add).then_inc(x1_ready, 1)
                        if k:
                            dve.wait_ge(x1_ready, 4 * b + k)
                            dve.bn_stats(stats[:, u, k - 1], x1[:, u, k - 1]).then_inc(stats_ready, 1)
                    dve.wait_ge(x1_ready, 4 * b + 4)
                    dve.bn_stats(stats[:, u, 3], x1[:, u, 3]).then_inc(stats_ready, 1)
                    hold(dve, stats_ready, 4 * (b + 1), passed_dve)
                    for k in range(4):
                        dve.bn_aggr(mean_var[:, u, k], stats[:, u, k]).then_inc(mv_ready, 1)
                    if isinstance(b, int) and b in (0, QB - 1):
                        normalise(b, u)

                def normalise(b, u):
                    dve.wait_ge(rstd_ready, b + 1)
                    for k in range(4):
                        dve.tensor_scalar(xn[:, u, k], x1[:, u, k], mean_var[:, u, k, 0:1], rstd[:, u, k:k + 1],
                                          ALU.subtract, ALU.mult).then_inc(xn_ready, 1)

                def behind(b, u, before):
                    for c in range(DC):
                        dve.wait_ge(t_hi_ready, DC * b + c + 1)
                        dve.tensor_tensor(t_lo[:, c], tbank[c][:, :], as_f32(t_hi[:, c]), ALU.subtract).then_inc(t_lo_ready, 1)
                    if not isinstance(b, int):
                        normalise(b + 1, 1 - u)
                blocks(dve, nothing, residual, behind)

            @block.tensor
            def _(pe):
                pe.wait_ge(w_lo_ready, 1)

                def project(b, u, before):
                    for n in range(4):
                        if n == 0:
                            pe.wait_ge(a_lo_ready, DC * (b + 1))
                        pe.wait_ge(x1_ready, 4 * b)
                        rows = slice(n * P, (n + 1) * P)
                        for c in range(DC):
                            for k, (a, w) in enumerate(((a_hi, wo_hi), (a_hi, wo_lo), (a_lo, wo_hi))):
                                mm = pe.matmul(bank[n][:, :], a[:, u, c, rows], w[:, c], start=(c == 0 and k == 0),
                                               stop=(c == DC - 1 and k == 2))
                        mm.then_inc(job_done, 1)

                def transpose(b, u, before):
                    pe.wait_ge(xn_ready, 4 * (b + 1))
                    pe.wait_ge(t_lo_ready, DC * b)
                    for c in range(DC):
                        for k in range(4):
                            mm = pe.transpose(tbank[c][:, k * P:(k + 1) * P], xn[:, u, k, c * P:(c + 1) * P], ident[:, :])
                        mm.then_inc(t_done, 1)
                blocks(pe, nothing, project, transpose)


PAIR = E // 2
GATE_AT = 2 * EC + 2
JOBS = FC + E * EC + PAIR + FC
RING = 4
JOB_W1 = [FC + k + (PAIR if k >= GATE_AT else 0) for k in range(E * EC)]
JOB_GATE = [FC + GATE_AT + p for p in range(PAIR)]
JOB_C2S = [FC + E * EC + PAIR + m for m in range(FC)]
assert JOBS % RING == 0


def feed_forward(nc, xT_hi, xT_lo, x1_dram, w, ident, neg_half, eps, out):
    ctx = ExitStack()
    with ctx:
        t = Tools(nc, ctx)
        we_hi, we_lo = t.sb("we_hi", [P, DC, FH], F32R), t.sb("we_lo", [P, DC, FH], F32R)
        wd_hi, wd_lo = t.sb("wd_hi", [P, FC, D], F32R), t.sb("wd_lo", [P, FC, D], F32R)
        w1_parts = t.sb("w1_parts", [P, E, EH], F32R)
        w2 = t.sb("w2", [P, E * EC, M])
        ws = t.sb("ws", [P, FC, 2, M])
        wc = t.sb("wc", [P, FH])
        wr = t.sb("wr", [M, E])
        be_col, bs_col, b1_col = t.sb("be_col", [P, FC]), t.sb("bs_col", [P, 1]), t.sb("b1_col", [P, E * EC])
        b2_col, bc_col = t.sb("b2_col", [P, PAIR]), t.sb("bc_col", [P, FC])
        br_all, bd_all = t.sb("br_all", [P, E]), t.sb("bd_all", [P, D])
        lng_all, lnb_all = t.sb("lng_all", [P, D]), t.sb("lnb_all", [P, D])
        select = t.sb("select", [P, PAIR, P], F32R)
        rank = t.sb("rank", [P, 4, E])
        base_e = t.sb("base_e", [P, 4, E])

        with ExitStack() as inner:
            s = Tools(nc, inner)
            e_in, d_in, w1_in = s.sb("e_in", [P, DC, FH]), s.sb("d_in", [P, FC, D]), s.sb("w1_in", [P, E, EH])
            sel_f = s.sb("sel_f", [P, PAIR, 2, M])
            e_loaded, d_loaded, w1_loaded = s.sem("e_loaded"), s.sem("d_loaded"), s.sem("w1_loaded")
            small_loaded = s.sem("small_loaded")
            hi_ready, lo_ready = s.sem("f_w_hi_ready"), s.sem("f_w_lo_ready")
            built = s.sem("f_built")
            with nc.Block() as block:
                @block.sync
                def _(sp):
                    sp.dma_start(e_in[:, :, :], w["W_enc"].rearrange("(c p) n -> p c n", p=P)).then_inc(e_loaded, 16)
                    sp.dma_start(d_in[:, :, :], w["W_dec"].rearrange("(c p) n -> p c n", p=P)).then_inc(d_loaded, 16)
                    loads = [(w2[:, :, :], w["W2"].rearrange("e (c p) m -> p (e c) m", p=P)),
                             (ws[:, :, 0, :], w["W_s2c"].rearrange("(c p) m -> p c m", p=P)),
                             (ws[:, :, 1, :], w["W_s2c"].rearrange("(c p) m -> p c m", p=P)),
                             (wc[0:M, :], w["W_c2s"]), (wc[M:P, :], w["W_c2s"]), (wr[:, :], w["Wr"]),
                             (bs_col[0:M, :], w["b_s2c"].rearrange("(p a) -> p a", a=1)),
                             (bs_col[M:P, :], w["b_s2c"].rearrange("(p a) -> p a", a=1))]
                    for dst, src in loads:
                        sp.dma_start(dst, src).then_inc(small_loaded, 16)
                    sp.wait_ge(small_loaded, 16 * 16)

                @block.scalar
                def _(act):
                    for half in range(2):
                        act.dma_start(w1_in[half * M:(half + 1) * M, :, :], w["W1"].rearrange("e m n -> m e n")).then_inc(w1_loaded, 16)
                    loads = [(be_col[:, :], w["b_enc"]),
                             (b1_col[:, :], w["b1"]),
                             (b2_col[:, :], w["b2"]),
                             (bc_col[:, :], w["b_c2s"]),
                             (br_all[:, :], w["br"].partition_broadcast(P)), (bd_all[:, :], w["b_dec"].partition_broadcast(P)),
                             (lng_all[:, :], w["ln_g"].partition_broadcast(P)), (lnb_all[:, :], w["ln_b"].partition_broadcast(P))]
                    for dst, src in loads:
                        act.dma_start(dst, src).then_inc(small_loaded, 16)
                    act.wait_ge(e_loaded, 16)
                    act.activation(we_hi[:, :, :], e_in[:, :, :], ACT.Copy).then_inc(hi_ready, 1)
                    act.wait_ge(d_loaded, 16)
                    act.activation(wd_hi[:, :, :], d_in[:, :, :], ACT.Copy).then_inc(hi_ready, 1)
                    act.wait_ge(w1_loaded, 32)
                    act.activation(w1_parts[:, :, :], w1_in[:, :, :], ACT.Copy).then_inc(hi_ready, 1)

                @block.vector
                def _(dve):
                    dve.wait_ge(hi_ready, 1)
                    dve.tensor_tensor(we_lo[:, :, :], e_in[:, :, :], as_f32(we_hi[:, :, :]), ALU.subtract).then_inc(lo_ready, 1)
                    dve.wait_ge(hi_ready, 2)
                    dve.tensor_tensor(wd_lo[:, :, :], d_in[:, :, :], as_f32(wd_hi[:, :, :]), ALU.subtract).then_inc(lo_ready, 1)
                    dve.wait_ge(hi_ready, 3)
                    dve.tensor_tensor(w1_parts[M:P, :, :], w1_in[M:P, :, :], as_f32(w1_parts[M:P, :, :]), ALU.subtract
                                      ).then_inc(lo_ready, 1)
                    dve.wait_ge(built, 3)
                    dve.tensor_copy(select[:, :, :], sel_f[:, :, :, :].rearrange("p a b c -> p a (b c)")).then_inc(lo_ready, 1)
                    dve.memset(base_e[:, :, :], 2.718281828459045).then_inc(lo_ready, 1)

                @block.gpsimd
                def _(pool):
                    pool.memset(sel_f[:, :, :, :], 0.0).then_inc(built, 1)
                    for n, row in enumerate((0, HD)):
                        pool.wait_ge(built, n + 1)
                        pool.affine_select(out=sel_f[:, :, :, :], in_=sel_f[:, :, :, :], compare_op=ALU.not_equal, fill=1.0,
                                           base=-row, pattern=[[-2, PAIR], [-1, 2], [0, M]], channel_multiplier=1).then_inc(built, 1)
                    for e in range(E):
                        pool.memset(rank[:, :, e:e + 1], float(E - e)).then_inc(built, 1)

        x_hi, x_lo = t.sb("f_x_hi", [P, 2, DC, BLK], F32R), t.sb("f_x_lo", [P, 2, DC, BLK], F32R)
        xb = t.sb("f_xb", [P, 4, D])
        sT = t.sb("sT", [P, 2, BLK])
        c_parts = t.sb("c_parts", [P, 2, BLK], F32R)
        c_f = t.sb("c_f", [M, BLK])
        logits, expd, prob = t.sb("logits", [P, 4, E]), t.sb("expd", [P, 4, E]), t.sb("prob", [P, 4, E])
        same, first1, first2, gate = (t.sb(n, [P, 4, E]) for n in ("same", "first1", "first2", "gate"))
        top = t.sb("top", [P, 8, 4])
        g_parts = t.sb("g_parts", [P, BLK], F32R)
        g_sb = t.sb("g_sb", [P, PAIR, BLK])
        hT = t.sb("hT", [P, RING, BLK])
        y_gated, moe = t.sb("y_gated", [P, BLK]), t.sb("moe", [P, BLK])
        sp_f = t.sb("sp_f", [P, 2, BLK])
        sp_hi, sp_lo = t.sb("sp_hi", [P, 2, BLK], F32R), t.sb("sp_lo", [P, 2, BLK], F32R)
        y = t.sb("y", [P, 4, D])
        stats, mean_var = t.sb("f_stats", [P, 4, 6]), t.sb("f_mean_var", [P, 4, 2])
        var_eps, rstd = t.sb("f_var_eps", [P, 4]), t.sb("f_rstd", [P, 4])
        ring, acc = t.banks(RING, "ring"), t.banks(4, "acc")

        x_loaded = [t.sem("f_x_loaded0"), t.sem("f_x_loaded1")]
        passed = t.sem("f_x1_loaded_sp_passed")
        x1_loaded, xb_ready = t.sem("f_x1_loaded"), t.sem("f_xb_ready")
        ring_done, ring_free = t.sem("ring_done"), t.sem("ring_free")
        s_used, h_used = t.sem("sT_used"), t.sem("hT_used")
        c_hi_ready, c_lo_ready, c_f_ready = t.sem("f_c_hi_ready"), t.sem("f_c_lo_ready"), t.sem("c_f_ready")
        logits_done, dist_ready, expd_ready = t.sem("logits_done"), t.sem("dist_ready"), t.sem("expd_ready")
        route = t.sem("route_step")
        gate_ready, gT_done, g_parts_ready = t.sem("gate_ready"), t.sem("gT_done"), t.sem("g_parts_ready")
        gated = t.sem("gated")
        gated_step, moe_ready = t.sem("gated_step"), t.sem("moe_ready")
        sp_hi_ready, sp_lo_ready, sp_used = t.sem("sp_hi_ready"), t.sem("sp_lo_ready"), t.sem("sp_used")
        y_ready = t.sem("y_ready")
        mv_ready, eps_ready, rstd_ready = t.sem("f_mv_ready"), t.sem("f_eps_ready"), t.sem("f_rstd_ready")
        stats_ready, scaled, passed_dve = t.sem("f_stats_ready"), t.sem("scaled"), t.sem("f_dve_passed")
        out_ready, out_stored = t.sem("out_ready"), t.sem("out_stored")

        def blocks(eng, body):
            with eng.Fori(0, QB // 2) as i:
                for u in range(2):
                    body(2 * i + u, u, i)

        ROUTE = 20

        with nc.Block() as block:
            @block.sync
            def _(sp):
                def load(b, u, before):
                    cols = bass.ds(b * BLK, BLK)
                    hold(sp, s_used, FC * (b + 1), passed)
                    sp.dma_start(as_f32(x_hi[:, u]), xT_hi[:, cols].rearrange("(c p) n -> p c n", p=P)).then_inc(x_loaded[u], 16)
                    sp.dma_start(as_f32(x_lo[:, u]), xT_lo[:, cols].rearrange("(c p) n -> p c n", p=P)).then_inc(x_loaded[u], 16)
                    hold(sp, out_ready, 4 * b, passed)
                    sp.dma_start(xb[:, :, :], x1_dram[cols, :].rearrange("(t p) n -> p t n", p=P)).then_inc(x1_loaded, 16)
                blocks(sp, load)

            @block.gpsimd
            def _(pool):
                def body(b, u, before):
                    pool.wait_ge(x1_loaded, 16 * (b + 1))
                    for k in range(4):
                        pool.tensor_tensor(xb[:, k], xb[:, k], lnb_all[:, :], ALU.add).then_inc(xb_ready, 1)
                    pool.wait_ge(dist_ready, b + 1)
                    pool.tensor_tensor(expd[:, :, :], base_e[:, :, :], logits[:, :, :], ALU.pow).then_inc(expd_ready, 1)
                    pool.wait_ge(mv_ready, 4 * (b + 1))
                    pool.tensor_tensor(var_eps[:, :], mean_var[:, :, 1], eps[:, :], ALU.add).then_inc(eps_ready, 1)
                    pool.wait_ge(eps_ready, b + 1)
                    pool.tensor_tensor(rstd[:, :], var_eps[:, :], neg_half[:, 0:4], ALU.pow).then_inc(rstd_ready, 1)
                    pool.wait_ge(out_ready, 4 * (b + 1))
                    pool.dma_start(out[bass.ds(b * BLK, BLK), :].rearrange("(t p) n -> p t n", p=P), y[:, :, :]).then_inc(out_stored, 16)
                blocks(pool, body)
                pool.wait_ge(out_stored, 16 * QB)

            @block.scalar
            def _(act):
                def body(b, u, before):
                    def take(n):
                        act.wait_ge(ring_done, JOBS * b + n + 1)
                        return ring[n % RING]

                    for m in range(FC):
                        src = take(m)
                        act.wait_ge(s_used, 2 * FC - 2 + FC * b + m + 1)
                        act.activation(sT[:, m % 2], src[:, :], ACT.Sigmoid, bias=be_col[:, m:m + 1]).then_inc(ring_free, 1)
                    act.wait_ge(s_used, FC * (b + 3))
                    act.activation(c_parts[:, 0], acc[0][:, :], ACT.Identity, bias=bs_col[:, 0:1]).then_inc(c_hi_ready, 1)
                    for k in range(E * EC):
                        if k == GATE_AT:
                            for p in range(PAIR):
                                src = take(JOB_GATE[p])
                                if p == 0:
                                    act.wait_ge(gated, PAIR * b)
                                act.activation(g_sb[:, p], src[:, :], ACT.Copy).then_inc(ring_free, 1)
                        p, c, half = k // (2 * EC), k % (2 * EC) // 2, k % 2
                        src = take(JOB_W1[k])
                        act.wait_ge(h_used, E * EC // 2 * b + k // 2 + 1)
                        col = (2 * p + half) * EC + c
                        act.activation(hT[:, k % RING], src[:, :], ACT.Relu, bias=b1_col[:, col:col + 1]).then_inc(ring_free, 1)
                    for m in range(FC):
                        src = take(JOB_C2S[m])
                        act.wait_ge(sp_lo_ready, FC * b + m + 1)
                        act.activation(sp_f[:, m % 2], src[:, :], ACT.Sigmoid, bias=bc_col[:, m:m + 1]).then_inc(ring_free, 1)
                blocks(act, body)

            @block.vector
            def _(dve):
                dve.memset(as_f32(g_parts[:, :]), 0.0)
                dve.sem_inc(sp_lo_ready, 2)

                def body(b, u, before):
                    dve.wait_ge(c_hi_ready, b + 1)
                    dve.scalar_tensor_tensor(c_parts[:, 1], acc[0][:, :], bs_col[:, 0:1], as_f32(c_parts[:, 0]),
                                             ALU.add, ALU.subtract).then_inc(c_lo_ready, 1)
                    dve.tensor_scalar(c_f[:, :], acc[0][0:M, :], bs_col[0:M, 0:1], None, ALU.add).then_inc(c_f_ready, 1)

                    steps = [0]

                    def step(ins):
                        steps[0] += 1
                        ins.then_inc(route, 1)
                        dve.wait_ge(route, ROUTE * b + steps[0])

                    def over(col):
                        return top[:, col].unsqueeze(2).to_broadcast([P, 4, E])

                    dve.wait_ge(logits_done, b + 1)
                    step(dve.tensor_tensor(logits[:, :, :], acc[1][:, 0:4 * E].rearrange("p (t e) -> p t e", e=E),
                                           br_all[:, :].unsqueeze(1).to_broadcast([P, 4, E]), ALU.add))
                    step(dve.tensor_reduce(top[:, 0], logits[:, :, :], AX_X, ALU.max))
                    dve.tensor_tensor(logits[:, :, :], logits[:, :, :], over(0), ALU.subtract).then_inc(dist_ready, 1)
                    dve.wait_ge(expd_ready, b + 1)
                    step(dve.tensor_reduce(top[:, 1], expd[:, :, :], AX_X, ALU.add))
                    step(dve.reciprocal(top[:, 2], top[:, 1]))
                    step(dve.tensor_tensor(prob[:, :, :], expd[:, :, :], over(2), ALU.mult))
                    step(dve.tensor_reduce(top[:, 3], prob[:, :, :], AX_X, ALU.max))
                    step(dve.tensor_tensor(same[:, :, :], prob[:, :, :], over(3), ALU.is_equal))
                    step(dve.tensor_tensor(same[:, :, :], same[:, :, :], rank[:, :, :], ALU.mult))
                    step(dve.tensor_reduce(top[:, 4], same[:, :, :], AX_X, ALU.max))
                    step(dve.tensor_tensor(first1[:, :, :], same[:, :, :], over(4), ALU.is_equal))
                    step(dve.scalar_tensor_tensor(prob[:, :, :], first1[:, :, :], -2.0, prob[:, :, :], ALU.mult, ALU.add))
                    step(dve.tensor_reduce(top[:, 5], prob[:, :, :], AX_X, ALU.max))
                    step(dve.tensor_tensor(same[:, :, :], prob[:, :, :], over(5), ALU.is_equal))
                    step(dve.tensor_tensor(same[:, :, :], same[:, :, :], rank[:, :, :], ALU.mult))
                    step(dve.tensor_reduce(top[:, 6], same[:, :, :], AX_X, ALU.max))
                    step(dve.tensor_tensor(top[:, 7], top[:, 3], top[:, 5], ALU.add))
                    step(dve.tensor_tensor(first2[:, :, :], same[:, :, :], over(6), ALU.is_equal))
                    step(dve.reciprocal(top[:, 7], top[:, 7]))
                    step(dve.tensor_tensor(first2[:, :, :], first2[:, :, :], over(5), ALU.mult))
                    step(dve.tensor_tensor(first1[:, :, :], first1[:, :, :], over(3), ALU.mult))
                    assert steps[0] == ROUTE
                    gather_gate(b)

                    dve.wait_ge(gT_done, b + 1)
                    dve.tensor_copy(g_parts[0:E, :], acc[1][0:E, :]).then_inc(g_parts_ready, 1)
                    dve.wait_ge(g_parts_ready, 2 * b + 1)
                    dve.tensor_tensor(g_parts[HD:HD + E, :], acc[1][0:E, :], as_f32(g_parts[0:E, :]), ALU.subtract
                                      ).then_inc(g_parts_ready, 1)

                    for p in range(PAIR):
                        dve.wait_ge(h_used, 2 + EC * (PAIR * b + p + 1))
                        dve.wait_ge(ring_free, 4 + JOBS * b + JOB_GATE[p] + 1)
                        dve.wait_ge(moe_ready, (PAIR - 1) * b + max(0, p - 1))
                        dst = moe if p == 0 else y_gated
                        dve.scalar_tensor_tensor(dst[:, :], acc[2 + p % 2][:, :], b2_col[:, p:p + 1], g_sb[:, p],
                                                 ALU.add, ALU.mult).then_inc(gated, 1)
                        if p:
                            dve.wait_ge(gated, PAIR * b + p + 1)
                            dve.tensor_tensor(moe[:, :], moe[:, :], y_gated[:, :], ALU.add).then_inc(moe_ready, 1)
                    for m in range(FC):
                        dve.wait_ge(ring_free, 4 + JOBS * b + JOB_C2S[m] + 1)
                        dve.wait_ge(sp_used, FC * b + m + 1)
                        dve.tensor_copy(sp_hi[:, m % 2], sp_f[:, m % 2]).then_inc(sp_hi_ready, 1)
                        dve.wait_ge(sp_hi_ready, FC * b + m + 1)
                        dve.tensor_tensor(sp_lo[:, m % 2], sp_f[:, m % 2], as_f32(sp_hi[:, m % 2]), ALU.subtract
                                          ).then_inc(sp_lo_ready, 1)
                    dve.wait_ge(sp_used, 2 + FC * (b + 1))
                    dve.wait_ge(out_stored, 16 * b)
                    for k in range(4):
                        dve.tensor_tensor(y[:, k], acc[k][:, :], bd_all[:, :], ALU.add).then_inc(y_ready, 1)
                    for k in range(4):
                        dve.wait_ge(y_ready, 4 * b + k + 1)
                        dve.bn_stats(stats[:, k], y[:, k]).then_inc(stats_ready, 1)
                    hold(dve, stats_ready, 4 * (b + 1), passed_dve)
                    for k in range(4):
                        dve.bn_aggr(mean_var[:, k], stats[:, k]).then_inc(mv_ready, 1)
                    dve.wait_ge(mv_ready, 4 * (b + 1))
                    for k in range(4):
                        dve.scalar_tensor_tensor(y[:, k], y[:, k], mean_var[:, k, 0:1], lng_all[:, :], ALU.subtract, ALU.mult
                                                 ).then_inc(scaled, 1)
                    dve.wait_ge(rstd_ready, b + 1)
                    dve.wait_ge(xb_ready, 4 * (b + 1))
                    dve.wait_ge(scaled, 4 * (b + 1))
                    for k in range(4):
                        dve.scalar_tensor_tensor(y[:, k], y[:, k], rstd[:, k:k + 1], xb[:, k], ALU.mult, ALU.add
                                                 ).then_inc(out_ready, 1)

                def gather_gate(b):
                    dve.tensor_tensor(gate[:, :, :], first1[:, :, :], first2[:, :, :], ALU.add).then_inc(gated_step, 1)
                    dve.wait_ge(gated_step, b + 1)
                    dve.tensor_tensor(gate[:, :, :], gate[:, :, :], top[:, 7].unsqueeze(2).to_broadcast([P, 4, E]), ALU.mult
                                      ).then_inc(gate_ready, 1)
                blocks(dve, body)

            @block.tensor
            def _(pe):
                pe.sem_inc(s_used, 2 * FC)
                pe.sem_inc(h_used, 2)
                pe.sem_inc(sp_used, 2)
                pe.sem_inc(ring_free, RING)

                def body(b, u, before):
                    def bank(n):
                        pe.wait_ge(ring_free, JOBS * b + n + 1)
                        return ring[n % RING]

                    def encode(m):
                        dst = bank(m)
                        cols = slice(m * P, (m + 1) * P)
                        for c in range(DC):
                            for k, (ww, xx) in enumerate(((we_hi, x_hi), (we_hi, x_lo), (we_lo, x_hi))):
                                mm = pe.matmul(dst[:, :], ww[:, c, cols], xx[:, u, c], start=(c == 0 and k == 0),
                                               stop=(c == DC - 1 and k == 2))
                        mm.then_inc(ring_done, 1)

                    def to_cont(m):
                        if m == 0:
                            pe.wait_ge(y_ready, 4 * b)
                        pe.wait_ge(ring_free, RING + JOBS * b + m + 1)
                        mm = pe.matmul(acc[0][:, :], ws[:, m].rearrange("p a b -> p (a b)"), sT[:, m % 2], start=m == 0, stop=m == FC - 1)
                        mm.then_inc(s_used, 1)

                    pe.wait_ge(x_loaded[u], 32 * (before + 1))
                    for m in range(FC):
                        encode(m)
                        if m:
                            to_cont(m - 1)
                    to_cont(FC - 1)

                    def hidden(k):
                        p, c, half = k // (2 * EC), k % (2 * EC) // 2, k % 2
                        dst = bank(JOB_W1[k])
                        if k == 0:
                            pe.wait_ge(c_lo_ready, b + 1)
                        for part in range(2):
                            mm = pe.matmul(dst[:, :], w1_parts[:, 2 * p + half, c * P:(c + 1) * P], c_parts[:, part],
                                           start=part == 0, stop=part == 1)
                        mm.then_inc(ring_done, 1)

                    def expert_out(q):
                        p, c = q // EC, q % EC
                        pe.wait_ge(ring_free, RING + JOBS * b + JOB_W1[2 * q + 1] + 1)
                        if c == 0:
                            pe.wait_ge(gated, PAIR * b + max(0, p - 1))
                        for half in range(2):
                            mm = pe.matmul(acc[2 + p % 2][half * M:(half + 1) * M, :], w2[:, (2 * p + half) * EC + c, :],
                                           hT[:, (2 * q + half) % RING], start=c == 0, stop=c == EC - 1)
                        mm.then_inc(h_used, 1)

                    def router():
                        pe.wait_ge(c_f_ready, b + 1)
                        for k in range(4):
                            mm = pe.matmul(acc[1][:, k * E:(k + 1) * E], c_f[:, k * P:(k + 1) * P], wr[:, :], start=True, stop=True)
                        mm.then_inc(logits_done, 1)

                    def spread_gates():
                        pe.wait_ge(gate_ready, b + 1)
                        for k in range(4):
                            mm = pe.transpose(acc[1][0:E, k * P:(k + 1) * P], gate[:, k], ident[:, :])
                        mm.then_inc(gT_done, 1)
                        for p in range(PAIR):
                            dst = bank(JOB_GATE[p])
                            pe.wait_ge(g_parts_ready, 2 * (b + 1))
                            pe.matmul(dst[:, :], select[:, p], g_parts[:, :], start=True, stop=True).then_inc(ring_done, 1)

                    for q in range(E * EC // 2):
                        if 2 * q == GATE_AT:
                            spread_gates()
                        hidden(2 * q)
                        hidden(2 * q + 1)
                        if q == 0:
                            router()
                        if q:
                            expert_out(q - 1)
                    expert_out(E * EC // 2 - 1)

                    def spikes(m):
                        dst = bank(JOB_C2S[m])
                        if m == 0:
                            pe.wait_ge(moe_ready, (PAIR - 1) * (b + 1))
                        pe.matmul(dst[:, :], wc[:, m * P:(m + 1) * P], moe[:, :], start=True, stop=True).then_inc(ring_done, 1)

                    def decode(m):
                        pe.wait_ge(sp_lo_ready, 2 + FC * b + m + 1)
                        for k in range(4):
                            rows = slice(k * P, (k + 1) * P)
                            for n, (a, ww) in enumerate(((sp_hi, wd_hi), (sp_hi, wd_lo), (sp_lo, wd_hi))):
                                mm = pe.matmul(acc[k][:, :], a[:, m % 2, rows], ww[:, m], start=(m == 0 and n == 0),
                                               stop=(m == FC - 1 and n == 2))
                        mm.then_inc(sp_used, 1)

                    spikes(0)
                    for m in range(FC):
                        if m + 1 < FC:
                            spikes(m + 1)
                        decode(m)
                blocks(pe, body)


def decoder_layer(nc, a):
    ctx = ExitStack()
    with ctx:
        t = Tools(nc, ctx)

        def scratch(name, shape, dt):
            return nc.dram_tensor(name, shape, dt, kind="Internal").ap()

        kT_hi, kT_lo = scratch("kT_hi", (D, NK_PAD), F32), scratch("kT_lo", (D, NK_PAD), F32)
        v_dram = scratch("v_dram", (NK_PAD, D), F32)
        qT_hi, qT_lo = scratch("qT_hi", (D, NQ), F32), scratch("qT_lo", (D, NQ), F32)
        aT = scratch("aT", (D, NQ), F32)
        x1 = scratch("x1_dram", (NQ, D), F32)
        nT_hi, nT_lo = scratch("nT_hi", (D, NQ), F32), scratch("nT_lo", (D, NQ), F32)

        ident, ident_b = t.sb("ident", [P, P]), t.sb("ident_b", [P, P], BF16)
        mask, maskT = t.sb("mask", [P, P], BF16), t.sb("maskT", [P, P], BF16)
        head_rows = t.sb("head_rows", [P, HG])
        neg_half, eps = t.sb("neg_half", [P, 4]), t.sb("eps", [P, 4])
        built = t.sem("const_built")
        with nc.Block() as block:
            @block.gpsimd
            def _(pool):
                for m in (ident, ident_b, mask, maskT):
                    pool.memset(m[:, :], 0.0).then_inc(built, 1)
                pool.memset(head_rows[:, :], 1.0).then_inc(built, 1)
                pool.memset(neg_half[:, :], -0.5).then_inc(built, 1)
                pool.memset(eps[:, :], EPS).then_inc(built, 1)
                pool.wait_ge(built, 7)
                for m in (ident, ident_b):
                    pool.affine_select(out=m[:, :], in_=m[:, :], compare_op=ALU.not_equal, fill=1.0, base=0,
                                       pattern=[[-1, P]], channel_multiplier=1).then_inc(built, 1)
                pool.affine_select(out=mask[:, :], in_=mask[:, :], compare_op=ALU.is_ge, fill=MASKED, base=0,
                                   pattern=[[-1, P]], channel_multiplier=1).then_inc(built, 1)
                pool.affine_select(out=maskT[:, :], in_=maskT[:, :], compare_op=ALU.is_ge, fill=MASKED, base=0,
                                   pattern=[[1, P]], channel_multiplier=-1).then_inc(built, 1)
                pool.affine_select(out=head_rows[:, :], in_=head_rows[:, :], compare_op=ALU.is_ge, fill=0.0, base=-R_MAX,
                                   pattern=[[-2, HG]], channel_multiplier=1).then_inc(built, 1)
                pool.wait_ge(built, 12)
                pool.affine_select(out=head_rows[:, :], in_=head_rows[:, :], compare_op=ALU.is_ge, fill=0.0, base=R_MAX + 1,
                                   pattern=[[2, HG]], channel_multiplier=-1).then_inc(built, 1)

        project_keys_values(nc, a["ctxT"], a["wkT"], a["wvT"], a["bk"], a["bv"], kT_hi, kT_lo, v_dram)
        project_queries(nc, a["x"], a["wqT"], a["bq"], ident, neg_half, eps, qT_hi, qT_lo)
        attend(nc, qT_hi, qT_lo, kT_hi, kT_lo, v_dram, aT, ident_b, mask, maskT, head_rows)
        project_output(nc, a["x"], aT, a["woT"], a["bo"], ident, neg_half, eps, x1, nT_hi, nT_lo)
        feed_forward(nc, nT_hi, nT_lo, x1, a, ident, neg_half, eps, a["out"])


def kernel(**inputs):
    import numpy as np
    import concourse.bacc as bacc
    from concourse.bass_utils import run_bass_kernel_spmd

    i = {name: np.asarray(value) for name, value in inputs.items()}
    ctxT = np.zeros((D, NK_PAD), i["ctx_1024"].dtype)
    ctxT[:, :NK] = i["ctx_1024"][0].T
    arrays = {"x": i["x"][0], "ctxT": ctxT}
    for n in "qkvo":
        arrays[f"w{n}T"] = i[f"L0_xattn_W{n}"].T
        arrays[f"b{n}"] = i[f"L0_xattn_b{n}"]
    for n in ("W_enc", "b_enc", "W_s2c", "b_s2c", "Wr", "br", "W1", "b1", "W2", "b2", "W_c2s", "b_c2s", "W_dec", "b_dec",
              "ln_g", "ln_b"):
        arrays[n] = i[f"L0_ffn_{n}"]
    for n in ("bq", "bk", "b_enc", "b1", "b2", "b_c2s"):
        arrays[n] = arrays[n].reshape(-1, P).T
    arrays = {n: np.ascontiguousarray(v) for n, v in arrays.items()}

    nc = bacc.Bacc("TRN2", target_bir_lowering=False, num_devices=1)
    dram = {n: nc.dram_tensor(f"in_{n}", v.shape, mybir.dt.from_np(v.dtype), kind="ExternalInput").ap() for n, v in arrays.items()}
    dram["out"] = nc.dram_tensor("out_rows", (NQ, D), F32, kind="ExternalOutput").ap()
    decoder_layer(nc, dram)
    r = run_bass_kernel_spmd(nc, [{f"in_{n}": v for n, v in arrays.items()}], core_ids=[0])
    return r.results[0]["out_rows"].reshape(1, NQ, D)
```

```python
from contextlib import ExitStack

import concourse.bass as bass
from concourse import mybir

F32 = mybir.dt.float32
F32R = mybir.dt.float32r
BF16 = mybir.dt.bfloat16
ALU = mybir.AluOpType
ACT = mybir.ActivationFunctionType
AX_X = mybir.AxisListType.X

P = 128
BLK = 512
NQ = 4096
NK = 3202
NK_PAD = 3584
D = 512
DC = D // P
H = 16
HD = 32
HG = P // HD
NG = H // HG
SCALE = HD ** -0.5
EPS = 1e-5
QB = NQ // BLK
KB = NK_PAD // BLK
KT = -(-NK // P)
K_LAST = NK - (KT - 1) * P
MASKED = -1e30
FH = 1024
FC = FH // P
M = 64
E = 8
EH = 512
EC = EH // P


def as_f32(ap):
    return ap.bitcast(F32)


def reach(eng, sem, n):
    if not isinstance(n, int) or n > 0:
        eng.wait_ge(sem, n)


def hold(eng, sem, n, passed):
    if not isinstance(n, int) or n > 0:
        eng.wait_ge(sem, n)
        eng.sem_inc(passed, 1)


class Tools:

    def __init__(self, nc, ctx):
        self.nc, self.ctx = nc, ctx

    def sb(self, name, shape, dt=F32):
        return self.ctx.enter_context(self.nc.sbuf_tensor(name, shape, dt))

    def banks(self, n, name):
        return [self.ctx.enter_context(self.nc.psum_tensor(f"{name}{i}", [P, BLK], F32)) for i in range(n)]

    def sem(self, name):
        return self.ctx.enter_context(self.nc.semaphore(name))


def project_keys_values(nc, ctxT, wkT, wvT, bk, bv, kT_hi, kT_lo, v_dram):
    ctx = ExitStack()
    with ctx:
        t = Tools(nc, ctx)
        w_in = t.sb("kv_w_in", [P, 2, DC, D])
        wk_hi, wk_lo = t.sb("wk_hi", [P, DC, D], F32R), t.sb("wk_lo", [P, DC, D], F32R)
        wv_hi, wv_lo = t.sb("wv_hi", [P, DC, D], F32R), t.sb("wv_lo", [P, DC, D], F32R)
        bk_col = t.sb("bk_col", [P, DC])
        bv_all = t.sb("bv_all", [P, D])
        c_in = t.sb("c_in", [P, 2, DC, BLK])
        c_hi, c_lo = t.sb("c_hi", [P, 2, DC, BLK], F32R), t.sb("c_lo", [P, 2, DC, BLK], F32R)
        k_hi, k_lo = t.sb("k_hi", [P, 2, DC, BLK], F32R), t.sb("k_lo", [P, 2, DC, BLK], F32R)
        v_out = t.sb("v_out", [P, 2, DC, D])
        bank = t.banks(4, "kv_bank")

        passed = t.sem("kv_bias_loaded_sp_passed")
        bias_loaded = t.sem("kv_bias_loaded")
        w_loaded = [t.sem("wk_loaded"), t.sem("wv_loaded")]
        w_hi_ready, w_lo_ready = t.sem("kv_w_hi_ready"), t.sem("kv_w_lo_ready")
        c_loaded = [t.sem("c_loaded0"), t.sem("c_loaded1")]
        c_hi_ready, c_lo_ready = t.sem("c_hi_ready"), t.sem("c_lo_ready")
        job_done = t.sem("kv_job_done")
        k_hi_ready = t.sem("k_hi_ready")
        bank_free = t.sem("kv_bank_free")
        k_stored = [t.sem("k_stored0"), t.sem("k_stored1")]
        v_stored = [t.sem("v_stored0"), t.sem("v_stored1")]

        JOBS = 2 * DC
        PAIRS = (KB - 1) // 2
        assert KB == 2 * PAIRS + 1

        def blocks(eng, body):
            body(0, 0, 0, True)
            body(1, 1, 0, True)
            with eng.Fori(1, PAIRS) as i:
                for u in range(2):
                    body(2 * i + u, u, i, True)
            body(2 * PAIRS, 0, PAIRS, False)

        with nc.Block() as block:
            @block.sync
            def _(sp):
                sp.dma_start(w_in[:, 0], wkT.rearrange("(c p) n -> p c n", p=P)).then_inc(w_loaded[0], 16)
                sp.dma_start(c_in[:, 0], ctxT[:, 0:BLK].rearrange("(c p) n -> p c n", p=P)).then_inc(c_loaded[0], 16)
                sp.dma_start(w_in[:, 1], wvT.rearrange("(c p) n -> p c n", p=P)).then_inc(w_loaded[1], 16)

                def load_next(b, u, before, more):
                    if more:
                        hold(sp, c_lo_ready, DC * b, passed)
                        sp.dma_start(c_in[:, 1 - u], ctxT[:, bass.ds((b + 1) * BLK, BLK)].rearrange(
                            "(c p) n -> p c n", p=P)).then_inc(c_loaded[1 - u], 16)
                blocks(sp, load_next)

            @block.gpsimd
            def _(pool):
                pool.dma_start(bk_col[:, :], bk).then_inc(bias_loaded, 16)
                pool.dma_start(bv_all[:, :], bv.partition_broadcast(P)).then_inc(bias_loaded, 16)

                def store(b, u, before, more):
                    cols = bass.ds(b * BLK, BLK)
                    pool.wait_ge(bank_free, 4 + JOBS * b + DC)
                    pool.dma_start(kT_hi[:, cols].rearrange("(c p) n -> p c n", p=P), as_f32(k_hi[:, u])).then_inc(k_stored[u], 16)
                    pool.dma_start(kT_lo[:, cols].rearrange("(c p) n -> p c n", p=P), as_f32(k_lo[:, u])).then_inc(k_stored[u], 16)
                    pool.wait_ge(bank_free, 4 + JOBS * b + 2 * DC)
                    pool.dma_start(v_dram[cols, :].rearrange("(t p) n -> p t n", p=P), v_out[:, u]).then_inc(v_stored[u], 16)
                blocks(pool, store)
                for u in range(2):
                    pool.wait_ge(k_stored[u], 32 * (PAIRS + 1 - u))
                    pool.wait_ge(v_stored[u], 16 * (PAIRS + 1 - u))

            @block.scalar
            def _(act):
                for w, hi in enumerate((wk_hi, wv_hi)):
                    act.wait_ge(w_loaded[w], 16)
                    act.activation(hi[:, :, :], w_in[:, w], ACT.Copy).then_inc(w_hi_ready, 1)
                    if w == 0:
                        act.wait_ge(c_loaded[0], 16)
                        for c in range(DC):
                            act.activation(c_hi[:, 0, c], c_in[:, 0, c], ACT.Copy).then_inc(c_hi_ready, 1)

                def body(b, u, before, more):
                    for n in range(DC):
                        act.wait_ge(job_done, JOBS * b + n + 1)
                        if n == 0:
                            act.wait_ge(bias_loaded, 32)
                            reach(act, k_stored[u], 32 * before)
                        act.activation(k_hi[:, u, n], bank[n][:, :], ACT.Identity, bias=bk_col[:, n:n + 1]).then_inc(k_hi_ready, 1)
                    if more:
                        act.wait_ge(c_loaded[1 - u], 16 * (before + 1 + u))
                        for c in range(DC):
                            act.activation(c_hi[:, 1 - u, c], c_in[:, 1 - u, c], ACT.Copy).then_inc(c_hi_ready, 1)
                blocks(act, body)

            @block.vector
            def _(dve):
                dve.sem_inc(bank_free, 4)
                for w, (hi, lo) in enumerate(((wk_hi, wk_lo), (wv_hi, wv_lo))):
                    dve.wait_ge(w_hi_ready, w + 1)
                    dve.tensor_tensor(lo[:, :, :], w_in[:, w], as_f32(hi[:, :, :]), ALU.subtract).then_inc(w_lo_ready, 1)
                    if w == 0:
                        for c in range(DC):
                            dve.wait_ge(c_hi_ready, c + 1)
                            dve.tensor_tensor(c_lo[:, 0, c], c_in[:, 0, c], as_f32(c_hi[:, 0, c]), ALU.subtract).then_inc(c_lo_ready, 1)

                def body(b, u, before, more):
                    dve.wait_ge(bias_loaded, 32)
                    for n in range(DC):
                        dve.wait_ge(k_hi_ready, DC * b + n + 1)
                        dve.scalar_tensor_tensor(k_lo[:, u, n], bank[n][:, :], bk_col[:, n:n + 1], as_f32(k_hi[:, u, n]),
                                                 ALU.add, ALU.subtract).then_inc(bank_free, 1)
                    for n in range(DC):
                        dve.wait_ge(job_done, JOBS * b + DC + n + 1)
                        if n == 0:
                            reach(dve, v_stored[u], 16 * before)
                        dve.tensor_tensor(v_out[:, u, n], bank[n][:, :], bv_all[:, :], ALU.add).then_inc(bank_free, 1)
                        if more:
                            dve.wait_ge(c_hi_ready, DC * (b + 1) + n + 1)
                            dve.tensor_tensor(c_lo[:, 1 - u, n], c_in[:, 1 - u, n], as_f32(c_hi[:, 1 - u, n]),
                                              ALU.subtract).then_inc(c_lo_ready, 1)
                blocks(dve, body)

            @block.tensor
            def _(pe):
                pe.wait_ge(w_lo_ready, 1)

                def body(b, u, before, more):
                    pe.wait_ge(c_lo_ready, DC * (b + 1))
                    for n in range(JOBS):
                        pe.wait_ge(bank_free, JOBS * b + n + 1)
                        if n == DC:
                            pe.wait_ge(w_lo_ready, 2)
                        first = True
                        for c in range(DC):
                            if n < DC:
                                cols = slice(n * P, (n + 1) * P)
                                terms = [(wk_hi[:, c, cols], c_hi[:, u, c]), (wk_hi[:, c, cols], c_lo[:, u, c]),
                                         (wk_lo[:, c, cols], c_hi[:, u, c])]
                            else:
                                cols = slice((n - DC) * P, (n - DC + 1) * P)
                                terms = [(c_hi[:, u, c, cols], wv_hi[:, c]), (c_hi[:, u, c, cols], wv_lo[:, c]),
                                         (c_lo[:, u, c, cols], wv_hi[:, c])]
                            for k, (lhsT, rhs) in enumerate(terms):
                                mm = pe.matmul(bank[n % DC][:, :], lhsT, rhs, start=first, stop=(c == DC - 1 and k == 2))
                                first = False
                        mm.then_inc(job_done, 1)
                blocks(pe, body)


def project_queries(nc, x, wqT, bq, ident, neg_half, eps, qT_hi, qT_lo):
    ctx = ExitStack()
    with ctx:
        t = Tools(nc, ctx)
        w_in = t.sb("q_w_in", [P, DC, D])
        wq_hi, wq_lo = t.sb("wq_hi", [P, DC, D], F32R), t.sb("wq_lo", [P, DC, D], F32R)
        bq_col = t.sb("bq_col", [P, DC])
        x_in = t.sb("x_in", [P, 2, 4, D])
        xn = t.sb("xn", [P, 2, 4, D])
        stats = t.sb("q_stats", [P, 2, 4, 6])
        mean_var = t.sb("q_mean_var", [P, 2, 4, 2])
        var_eps = t.sb("q_var_eps", [P, 2, 4])
        rstd = t.sb("q_rstd", [P, 2, 4])
        xT_hi, xT_lo = t.sb("xT_hi", [P, 2, DC, BLK], F32R), t.sb("xT_lo", [P, 2, DC, BLK], F32R)
        q_hi, q_lo = t.sb("q_hi", [P, 2, DC, BLK], F32R), t.sb("q_lo", [P, 2, DC, BLK], F32R)
        bank = t.banks(4, "q_bank")
        tbank = t.banks(4, "q_tbank")

        passed = t.sem("q_bias_loaded_sp_passed")
        bias_loaded, w_loaded = t.sem("q_bias_loaded"), t.sem("wq_loaded")
        w_hi_ready, w_lo_ready = t.sem("wq_hi_ready"), t.sem("wq_lo_ready")
        x_loaded = [t.sem("x_loaded0"), t.sem("x_loaded1")]
        stats_ready, mv_ready, eps_ready = t.sem("q_stats_ready"), t.sem("q_mv_ready"), t.sem("q_eps_ready")
        passed_dve = t.sem("q_dve_passed")
        rstd_ready, xn_ready = t.sem("q_rstd_ready"), t.sem("xn_ready")
        xT_done = t.sem("xT_done")
        xT_hi_ready, xT_lo_ready = t.sem("xT_hi_ready"), t.sem("xT_lo_ready")
        job_done, q_hi_ready, q_lo_ready = t.sem("q_job_done"), t.sem("q_hi_ready"), t.sem("q_lo_ready")
        q_stored = [t.sem("q_stored0"), t.sem("q_stored1")]
        PAIRS = QB // 2 - 1

        def blocks(eng, prepare, process):
            prepare(0, 0, 0)

            def pair(i):
                for u in range(2):
                    process(2 * i + u, u, i, lambda: prepare(2 * i + u + 1, 1 - u, i + u))
            pair(0)
            with eng.Fori(1, PAIRS) as i:
                pair(i)
            process(2 * PAIRS, 0, PAIRS, lambda: prepare(2 * PAIRS + 1, 1, PAIRS))
            process(2 * PAIRS + 1, 1, PAIRS, None)

        with nc.Block() as block:
            @block.sync
            def _(sp):
                sp.dma_start(w_in[:, :, :], wqT.rearrange("(c p) n -> p c n", p=P)).then_inc(w_loaded, 16)

                def process(b, u, before, prepare_next):
                    if prepare_next:
                        hold(sp, xn_ready, 4 * b, passed)
                        sp.dma_start(x_in[:, 1 - u], x[bass.ds((b + 1) * BLK, BLK), :].rearrange(
                            "(t p) n -> p t n", p=P)).then_inc(x_loaded[1 - u], 16)

                def first(b, u, before):
                    sp.dma_start(x_in[:, 0], x[0:BLK, :].rearrange("(t p) n -> p t n", p=P)).then_inc(x_loaded[0], 16)
                blocks(sp, first, process)

            @block.gpsimd
            def _(pool):
                pool.dma_start(bq_col[:, :], bq).then_inc(bias_loaded, 16)

                def prepare(b, u, before):
                    pool.wait_ge(mv_ready, 4 * (b + 1))
                    pool.tensor_tensor(var_eps[:, u], mean_var[:, u, :, 1], eps[:, :], ALU.add).then_inc(eps_ready, 1)
                    pool.wait_ge(eps_ready, b + 1)
                    pool.tensor_tensor(rstd[:, u], var_eps[:, u], neg_half[:, 0:4], ALU.pow).then_inc(rstd_ready, 1)

                def process(b, u, before, prepare_next):
                    if prepare_next:
                        prepare_next()
                    cols = bass.ds(b * BLK, BLK)
                    pool.wait_ge(q_lo_ready, 4 + DC * (b + 1))
                    pool.dma_start(qT_hi[:, cols].rearrange("(c p) n -> p c n", p=P), as_f32(q_hi[:, u])).then_inc(q_stored[u], 16)
                    pool.dma_start(qT_lo[:, cols].rearrange("(c p) n -> p c n", p=P), as_f32(q_lo[:, u])).then_inc(q_stored[u], 16)
                blocks(pool, prepare, process)
                for u in range(2):
                    pool.wait_ge(q_stored[u], 32 * (QB // 2))

            @block.scalar
            def _(act):
                act.wait_ge(w_loaded, 16)
                act.activation(wq_hi[:, :, :], w_in[:, :, :], ACT.Copy).then_inc(w_hi_ready, 1)

                def prepare(b, u, before):
                    for c in range(DC):
                        act.wait_ge(xT_done, DC * b + c + 1)
                        act.activation(xT_hi[:, u, c], tbank[c][:, :], ACT.Copy).then_inc(xT_hi_ready, 1)

                def process(b, u, before, prepare_next):
                    for n in range(DC):
                        if n == 2 and prepare_next:
                            prepare_next()
                        act.wait_ge(job_done, DC * b + n + 1)
                        if n == 0:
                            act.wait_ge(bias_loaded, 16)
                            reach(act, q_stored[u], 32 * before)
                        act.activation(q_hi[:, u, n], bank[n][:, :], ACT.Identity, bias=bq_col[:, n:n + 1]).then_inc(q_hi_ready, 1)
                blocks(act, prepare, process)

            @block.vector
            def _(dve):
                def normalise_stats(b, u):
                    for k in range(4):
                        dve.bn_stats(stats[:, u, k], x_in[:, u, k]).then_inc(stats_ready, 1)
                    hold(dve, stats_ready, 4 * (b + 1), passed_dve)
                    for k in range(4):
                        dve.bn_aggr(mean_var[:, u, k], stats[:, u, k]).then_inc(mv_ready, 1)

                def normalise(b, u):
                    dve.wait_ge(rstd_ready, b + 1)
                    for k in range(4):
                        dve.tensor_scalar(xn[:, u, k], x_in[:, u, k], mean_var[:, u, k, 0:1], rstd[:, u, k:k + 1],
                                          ALU.subtract, ALU.mult).then_inc(xn_ready, 1)

                def low_parts(b, u):
                    for c in range(DC):
                        dve.wait_ge(xT_hi_ready, DC * b + c + 1)
                        dve.tensor_tensor(xT_lo[:, u, c], tbank[c][:, :], as_f32(xT_hi[:, u, c]), ALU.subtract).then_inc(xT_lo_ready, 1)

                def q_low(b, u, n):
                    dve.wait_ge(q_hi_ready, DC * b + n + 1)
                    dve.scalar_tensor_tensor(q_lo[:, u, n], bank[n][:, :], bq_col[:, n:n + 1], as_f32(q_hi[:, u, n]),
                                             ALU.add, ALU.subtract).then_inc(q_lo_ready, 1)

                def first(b, u, before):
                    dve.sem_inc(q_lo_ready, 4)
                    dve.wait_ge(x_loaded[0], 16)
                    normalise_stats(0, 0)
                    normalise(0, 0)
                    low_parts(0, 0)
                    dve.wait_ge(w_hi_ready, 1)
                    dve.tensor_tensor(wq_lo[:, :, :], w_in[:, :, :], as_f32(wq_hi[:, :, :]), ALU.subtract).then_inc(w_lo_ready, 1)
                    dve.wait_ge(bias_loaded, 16)

                def process(b, u, before, prepare_next):
                    if prepare_next:
                        dve.wait_ge(x_loaded[1 - u], 16 * (before + 1 + u))
                        normalise_stats(b + 1, 1 - u)
                    q_low(b, u, 0)
                    if prepare_next:
                        normalise(b + 1, 1 - u)
                    q_low(b, u, 1)
                    if prepare_next:
                        low_parts(b + 1, 1 - u)
                    q_low(b, u, 2)
                    q_low(b, u, 3)
                blocks(dve, first, process)

            @block.tensor
            def _(pe):
                def prepare(b, u, before):
                    pe.wait_ge(xn_ready, 4 * (b + 1))
                    reach(pe, xT_lo_ready, DC * b)
                    for c in range(DC):
                        for k in range(4):
                            mm = pe.transpose(tbank[c][:, k * P:(k + 1) * P], xn[:, u, k, c * P:(c + 1) * P], ident[:, :])
                        mm.then_inc(xT_done, 1)

                def process(b, u, before, prepare_next):
                    for n in range(DC):
                        if n == 2 and prepare_next:
                            prepare_next()
                        if n == 0:
                            pe.wait_ge(xT_lo_ready, DC * (b + 1))
                            pe.wait_ge(w_lo_ready, 1)
                        pe.wait_ge(q_lo_ready, DC * b + n + 1)
                        for c in range(DC):
                            cols = slice(n * P, (n + 1) * P)
                            for k, (w, xx) in enumerate(((wq_hi, xT_hi), (wq_hi, xT_lo), (wq_lo, xT_hi))):
                                mm = pe.matmul(bank[n][:, :], w[:, c, cols], xx[:, u, c],
                                               start=(c == 0 and k == 0), stop=(c == DC - 1 and k == 2))
                        mm.then_inc(job_done, 1)
                blocks(pe, prepare, process)


R_HI, R_MID, R_LO, R_MAX = 0, HD, 2 * HD, 3 * HD
R_END = R_MAX + 2 * HG
SLOTS = 6
QBUFS = 4
S_RING, M_RING = 3, 3


def key_tiles(j):
    return min(4 * j + 4, KT)


def key_chunks(j):
    return min(j + 1, KB)


STEPS = [(j, kt) for j in range(QB) for kt in range(key_tiles(j))]
ST = len(STEPS)
FIRST_STEP = [STEPS.index((j, 0)) for j in range(QB)] + [ST]


def pool_sums(j, kt):
    if j == 0 or kt >= key_tiles(j) - 2:
        return False
    return kt % 3 != 2 if j < QB - 1 else kt % 2 == 1 or kt == 0


def pool_adds(j, kt):
    return pool_sums(j, kt) and kt != 0


PO = sum(pool_adds(j, kt) for j, kt in STEPS)
PO_BEFORE = [sum(pool_adds(j, kt) for j, kt in STEPS[:s]) for s in range(ST + 1)]


def max_units(j):
    units = []
    for r in range(4):
        seen = min((4 * j + r + 1) * P, NK)
        for h in range(HG):
            for c in range(key_chunks(j)):
                n = min(BLK, seen - c * BLK)
                first_masked = (4 * j + r) * P - c * BLK
                masked = min(P, n - first_masked) if first_masked < n else 0
                units.append((r, h, c, n, first_masked, masked))
    return units


UNITS = [max_units(j) for j in range(QB)]
NU = sum(map(len, UNITS))
UNITS_BEFORE = [sum(map(len, UNITS[:j])) for j in range(QB + 1)]


LEAD_BLOCKS = 3


def max_jobs():
    jobs = []
    for j in range(QB):
        for i in range(len(UNITS[j])):
            if j > 0 and i == (0 if j == LEAD_BLOCKS else 3):
                jobs.append((j - 1, None))
            jobs.append((j, i))
    return jobs + [(QB - 1, None)]


MAX_JOBS = max_jobs()
FIRST_LEAD = MAX_JOBS.index((0, None)) + 1
LEAD = MAX_JOBS.index((LEAD_BLOCKS - 1, None))
W_SCORES, W_VALUES = 1, 1.5

PIECES = (0, 1, 2, "values", 3, "denominators")


def plan(first, last):
    t, at = 0, []
    for j, kt in STEPS:
        width = (BLK - max(0, kt - 4 * j) * P) / BLK
        at.append([])
        for piece in PIECES:
            at[-1].append(t)
            if isinstance(piece, int):
                t += W_SCORES * width
            elif piece == "values" or not pool_sums(j, kt):
                t += W_VALUES * width
    jobs = []
    for q in range(FIRST_LEAD if first else LEAD, len(MAX_JOBS)):
        j = MAX_JOBS[q][0]
        release = at[min(FIRST_STEP[j - QBUFS + 1] + 3, ST - 1)][0] if j >= QBUFS - 1 and MAX_JOBS[q][1] is not None else 0
        jobs.append((0, q, release, at[max(0, FIRST_STEP[j] - 3)][0]))
    if not last:
        for q in range(LEAD):
            j = MAX_JOBS[q][0]
            jobs.append((1, q, at[FIRST_STEP[QB - 1] + 4 * j + 7][0], t))
    when, now = [], 0
    for n, (_, _, release, _) in enumerate(jobs):
        pace = min([(t - now) / (len(jobs) - n)] + [(due - now) / (i + 1) for i, (_, _, _, due) in enumerate(jobs[n:])])
        now = max(now + max(pace, 0), release)
        when.append(now)
    n, steps = 0, []
    for s in range(ST):
        steps.append([])
        for piece in range(len(PIECES)):
            steps[-1].append([])
            while n < len(jobs) and (when[n] <= at[s][piece] or (s == ST - 1 and piece == len(PIECES) - 1)):
                steps[-1][-1].append(jobs[n][:2])
                n += 1
    return steps


PLANS = {(first, last): plan(first, last) for first, last in ((True, False), (False, False), (False, True))}


def attend(nc, qT_hi, qT_lo, kT_hi, kT_lo, v_dram, aT, ident_b, mask, maskT, head_rows):
    ctx = ExitStack()
    with ctx:
        t = Tools(nc, ctx)
        k_sb = t.sb("k_sb", [P, HG, KT * P], F32R)
        v_sb = t.sb("v_sb", [P, KT, P])
        q_sb = [t.sb(f"q_sb{i}", [P, HG, BLK], F32R) for i in range(QBUFS)]
        pT = t.sb("pT", [P, SLOTS, HG, BLK])
        ones = t.sb("ones", [P, HD])
        part_sum = t.sb("part_sum", [P, 2, HG, BLK])
        row_max = t.sb("row_max", [P, 2, 4, HG, KB])
        neg_max = t.sb("neg_max", [P, 4, HG])
        neg_parts = t.sb("neg_parts", [P, 4, HG, 2], BF16)
        o_sb, den_sb = t.sb("o_sb", [P, 2, BLK]), t.sb("den_sb", [P, 2, BLK])
        rden, a_out = t.sb("rden", [P, BLK]), t.sb("a_out", [P, 2, BLK])
        s_bank, m_bank = t.banks(S_RING, "s_bank"), t.banks(M_RING, "m_bank")
        [o_bank] = t.banks(1, "o_bank")
        [den_bank] = t.banks(1, "den_bank")

        passed, passed_pe = t.sem("att_sp_passed"), t.sem("att_pe_passed")
        const_ready = t.sem("att_const_ready")
        q_loaded = [t.sem(f"q_loaded{i}") for i in range(QBUFS)]
        k_loaded = [t.sem(f"k_loaded{c}") for c in range(KB)]
        v_loaded = [t.sem(f"v_loaded{c}") for c in range(KB)]
        unit_done, unit_max = t.sem("unit_done"), t.sem("unit_max")
        neg_ready = t.sem("neg_ready")
        maxT_done, max_rows = t.sem("maxT_done"), t.sem("max_rows")
        s_done = t.sem("s_done")
        exp_done = t.sem("exp_done")
        p_used = t.sem("p_used")
        pool_added = t.sem("pool_added")
        block_done, block_copied = t.sem("block_done"), t.sem("block_copied")
        rden_ready, a_ready = t.sem("rden_ready"), t.sem("a_ready")
        a_stored = [t.sem("a_stored0"), t.sem("a_stored1")]
        TILES = HG * ST

        def groups(eng, body):
            body(0, True, False)
            with eng.Fori(1, NG - 1) as g:
                body(g, False, False)
            body(NG - 1, False, True)

        with nc.Block() as block:
            @block.sync
            def _(sp):
                def load_q(g, j):
                    for row, src in ((R_HI, qT_hi), (R_MID, qT_lo), (R_LO, qT_hi)):
                        sp.dma_start(as_f32(q_sb[j % QBUFS][row:row + HD, :, :]),
                                     src[bass.ds(g * P, P), j * BLK:(j + 1) * BLK].rearrange("(h d) n -> d h n", d=HD)
                                     ).then_inc(q_loaded[j % QBUFS], 16)

                def load_k(g, c):
                    n = min(BLK, KT * P - c * BLK)
                    for row, src in ((R_HI, kT_hi), (R_MID, kT_hi), (R_LO, kT_lo)):
                        sp.dma_start(as_f32(k_sb[row:row + HD, :, c * BLK:c * BLK + n]),
                                     src[bass.ds(g * P, P), c * BLK:c * BLK + n].rearrange("(h d) n -> d h n", d=HD)
                                     ).then_inc(k_loaded[c], 16)

                def load_v(g, c):
                    n = min(BLK, KT * P - c * BLK)
                    sp.dma_start(v_sb[:, 4 * c:4 * c + n // P, :],
                                 v_dram[c * BLK:c * BLK + n, bass.ds(g * P, P)].rearrange("(t p) n -> p t n", p=P)
                                 ).then_inc(v_loaded[c], 16)

                def body(g, first, last):
                    if first:
                        for c in range(KB):
                            if c < QBUFS:
                                load_q(0, c)
                            load_k(0, c)
                            load_v(0, c)
                    else:
                        hold(sp, s_done, TILES * g, passed)
                        load_q(g, QBUFS - 1)
                    for j in range(QBUFS, QB):
                        hold(sp, s_done, TILES * g + HG * FIRST_STEP[j - QBUFS + 1], passed)
                        load_q(g, j)
                    if not last:
                        for c in range(KB):
                            if c < QBUFS - 1:
                                hold(sp, s_done, TILES * g + HG * FIRST_STEP[c + QBUFS + 1], passed)
                                load_q(g + 1, c)
                            through = FIRST_STEP[QB - 1] + min(4 * c + 4, KT)
                            hold(sp, s_done, TILES * g + HG * through, passed)
                            load_k(g + 1, c)
                            hold(sp, p_used, ST * g + through, passed)
                            load_v(g + 1, c)
                groups(sp, body)

            @block.gpsimd
            def _(pool):
                pool.memset(ones[:, :], 1.0).then_inc(const_ready, 1)

                def body(g, first, last):
                    for s, (j, kt) in enumerate(STEPS):
                        if not pool_adds(j, kt):
                            continue
                        if kt == 1:
                            reach(pool, block_done, (QB - 1) * g + max(0, j - 2))
                        reach(pool, exp_done, TILES * g + HG * (s + 1))
                        reach(pool, pool_added, PO * g + PO_BEFORE[s])
                        q0 = max(0, kt - 4 * j) * P
                        total = part_sum[:, j % 2, :, q0:]
                        pool.tensor_tensor(total, pT[:, (s - 1) % SLOTS, :, q0:] if kt == 1 else total,
                                           pT[:, s % SLOTS, :, q0:], ALU.add).then_inc(pool_added, 1)
                groups(pool, body)

            @block.scalar
            def _(act):
                def body(g, first, last):
                    def copy_block(j):
                        if j == 0:
                            reach(act, p_used, ST * g + key_tiles(0))
                        else:
                            reach(act, block_done, (QB - 1) * g + j)
                        reach(act, a_ready, QB * g + j - 1)
                        act.activation(o_sb[:, j % 2], o_bank[:, :], ACT.Copy).then_inc(block_copied, 1)
                        act.activation(den_sb[:, j % 2], den_bank[:, :], ACT.Copy).then_inc(block_copied, 1)

                    def store_block(j):
                        reach(act, a_ready, QB * g + j + 1)
                        act.dma_start(aT[bass.ds(g * P, P), j * BLK:(j + 1) * BLK], a_out[:, j % 2]).then_inc(a_stored[j % 2], 16)

                    def max_to_rows(ahead, j):
                        reach(act, maxT_done, QB * (g + ahead) + j + 1)
                        rows = slice(R_MAX, R_END)
                        bank = m_bank[MAX_JOBS.index((j, None)) % M_RING]
                        src = bank[rows, :].unsqueeze(1).to_broadcast([R_END - R_MAX, HG, BLK])
                        act.activation(q_sb[j % QBUFS][rows, :, :], src, ACT.Copy).then_inc(max_rows, 1)

                    def transposed_maxima(jobs):
                        for ahead, q in jobs:
                            if MAX_JOBS[q][1] is None:
                                max_to_rows(ahead, MAX_JOBS[q][0])

                    steps = PLANS[first, last]
                    if first:
                        max_to_rows(0, 0)
                    for s, (j, kt) in enumerate(STEPS):
                        q0 = max(0, kt - 4 * j) * P
                        rows = P if kt < KT - 1 else K_LAST
                        reach(act, p_used, ST * g + s + 1 - SLOTS)
                        reach(act, pool_added, PO * g + (PO_BEFORE[s - SLOTS + 1 + (STEPS[s - SLOTS][1] == 0)] if s >= SLOTS else 0))
                        for jobs, h in zip(steps[s], PIECES):
                            transposed_maxima(jobs)
                            if not isinstance(h, int):
                                continue
                            reach(act, s_done, TILES * g + HG * s + h + 1)
                            act.activation(pT[0:rows, s % SLOTS, h, q0:], s_bank[(HG * s + h) % S_RING][0:rows, q0:],
                                           ACT.Exp, scale=SCALE).then_inc(exp_done, 1)
                        if kt == 0 and j > 0:
                            copy_block(j - 1)
                        if kt == 7:
                            store_block(j - 1)
                    copy_block(QB - 1)
                    store_block(QB - 1)
                groups(act, body)
                for i in range(2):
                    act.wait_ge(a_stored[i], 16 * NG * QB // 2)

            @block.vector
            def _(dve):
                for h in range(HG):
                    dve.tensor_copy(k_sb[R_MAX:R_END, h, :], head_rows[R_MAX:R_END, h:h + 1].to_broadcast([R_END - R_MAX, KT * P])
                                    ).then_inc(const_ready, 1)

                def body(g, first, last):
                    def take_max(ahead, q):
                        j, i = MAX_JOBS[q]
                        if i is None:
                            return
                        r, h, c, n, _, _ = UNITS[j][i]
                        reach(dve, unit_done, NU * (g + ahead) + UNITS_BEFORE[j] + i + 1)
                        dve.tensor_reduce(row_max[:, j % 2, r, h, c:c + 1], m_bank[q % M_RING][:, 0:n], AX_X, ALU.max
                                          ).then_inc(unit_max, 1)
                        if i == len(UNITS[j]) - 1:
                            negate(ahead, j)

                    def negate(ahead, j):
                        before = QB * (g + ahead) + j
                        reach(dve, unit_max, NU * (g + ahead) + UNITS_BEFORE[j + 1])
                        dve.tensor_reduce(neg_max[:, :, :], row_max[:, j % 2, :, :, 0:key_chunks(j)], AX_X, ALU.max,
                                          negate=True).then_inc(neg_ready, 1)
                        reach(dve, neg_ready, 3 * before + 1)
                        reach(dve, maxT_done, before)
                        dve.tensor_copy(neg_parts[:, :, :, 0], neg_max[:, :, :]).then_inc(neg_ready, 1)
                        reach(dve, neg_ready, 3 * before + 2)
                        dve.tensor_tensor(neg_parts[:, :, :, 1], neg_max[:, :, :], neg_parts[:, :, :, 0], ALU.subtract
                                          ).then_inc(neg_ready, 1)

                    def invert(j, quarter):
                        if quarter == 0:
                            reach(dve, block_copied, 2 * (QB * g + j + 1))
                        cols = slice(quarter * P, (quarter + 1) * P)
                        dve.reciprocal(rden[:, cols], den_sb[:, j % 2, cols]).then_inc(rden_ready, 1)

                    def normalise(j):
                        reach(dve, rden_ready, 4 * (QB * g + j + 1))
                        reach(dve, a_stored[j % 2], 16 * (QB // 2 * g + j // 2))
                        dve.tensor_tensor(a_out[:, j % 2], o_sb[:, j % 2], rden[:, :], ALU.mult).then_inc(a_ready, 1)

                    if first:
                        for q in range(FIRST_LEAD):
                            take_max(0, q)
                    steps = PLANS[first, last]
                    for s, (j, kt) in enumerate(STEPS):
                        for ahead, q in sum(steps[s], []):
                            take_max(ahead, q)
                        if j > 0 and 0 < kt < 5:
                            invert(j - 1, kt - 1)
                        if j > 0 and kt == 5:
                            normalise(j - 1)
                    for quarter in range(4):
                        invert(QB - 1, quarter)
                    normalise(QB - 1)
                groups(dve, body)

            @block.tensor
            def _(pe):
                pe.wait_ge(const_ready, 1 + HG)

                def body(g, first, last):
                    def bank_free(ahead, q):
                        if q < M_RING:
                            reach(pe, unit_max, NU * (g + ahead))
                            reach(pe, max_rows, QB * (g + ahead))
                            return
                        j, i = MAX_JOBS[q - M_RING]
                        if i is None:
                            reach(pe, max_rows, QB * (g + ahead) + j + 1)
                        else:
                            reach(pe, unit_max, NU * (g + ahead) + UNITS_BEFORE[j] + i + 1)

                    def job(ahead, q):
                        j, i = MAX_JOBS[q]
                        if i is None:
                            transpose_max(ahead, q, j)
                        else:
                            unit(ahead, q, j, i)

                    def unit(ahead, q, j, i):
                        r, h, c, n, first_masked, masked = UNITS[j][i]
                        if i == 0:
                            reach(pe, q_loaded[j % QBUFS], 48 * (QB // QBUFS * (g + ahead) + j // QBUFS + 1))
                        if c == j and r == 0 and h == 0:
                            reach(pe, k_loaded[c], 48 * (g + ahead + 1))
                        bank_free(ahead, q)
                        out = m_bank[q % M_RING]
                        mm = pe.matmul(out[:, 0:n], q_sb[j % QBUFS][0:R_MAX, h, r * P:(r + 1) * P],
                                       k_sb[0:R_MAX, h, c * BLK:c * BLK + n], start=True, stop=not masked)
                        if masked:
                            mm = pe.matmul(out[:, first_masked:n], ident_b[:, :], mask[:, 0:masked], start=False, stop=True)
                        mm.then_inc(unit_done, 1)

                    def transpose_max(ahead, q, j):
                        reach(pe, neg_ready, 3 * (QB * (g + ahead) + j + 1))
                        bank_free(ahead, q)
                        for r in range(4):
                            mm = pe.matmul(m_bank[q % M_RING][R_MAX:R_END, r * P:(r + 1) * P],
                                           neg_parts[:, r].rearrange("p h k -> p (h k)"), ident_b[:, :], start=True, stop=True)
                        mm.then_inc(maxT_done, 1)

                    def scores(s, h):
                        j, kt = STEPS[s]
                        q0 = max(0, kt - 4 * j) * P
                        if h == 0 and kt == 0:
                            reach(pe, max_rows, QB * g + j + 1)
                        n = HG * s + h
                        reach(pe, exp_done, TILES * g + max(0, n - S_RING + 1))
                        out = s_bank[n % S_RING]
                        mm = pe.matmul(out[:, q0:], k_sb[0:R_END, h, kt * P:(kt + 1) * P],
                                       q_sb[j % QBUFS][0:R_END, h, q0:], start=True, stop=kt < 4 * j)
                        if kt >= 4 * j:
                            mm = pe.matmul(out[:, q0:q0 + P], ident_b[:, :], maskT[:, :], start=False, stop=True)
                        mm.then_inc(s_done, 1)

                    def weigh_values(s):
                        j, kt = STEPS[s]
                        q0 = max(0, kt - 4 * j) * P
                        rows = P if kt < KT - 1 else K_LAST
                        if kt < KT - 1:
                            reach(pe, exp_done, TILES * g + HG * (s + 1))
                        else:
                            hold(pe, exp_done, TILES * g + HG * (s + 1), passed_pe)
                        if kt % 4 == 0 and kt // 4 == j:
                            reach(pe, v_loaded[j], 16 * (g + 1))
                        if kt == 0:
                            reach(pe, block_copied, 2 * (QB * g + j) - 1)
                        for h in range(HG):
                            mm = pe.matmul(o_bank[h * HD:(h + 1) * HD, q0:], v_sb[0:rows, kt, h * HD:(h + 1) * HD],
                                           pT[0:rows, s % SLOTS, h, q0:], start=kt == 0, stop=kt == key_tiles(j) - 1)
                        if pool_sums(j, kt):
                            mm.then_inc(p_used, 1)

                    def denominators(s):
                        j, kt = STEPS[s]
                        last_tile = kt == key_tiles(j) - 1
                        if not pool_sums(j, kt):
                            q0 = max(0, kt - 4 * j) * P
                            rows = P if kt < KT - 1 else K_LAST
                            if kt == (2 if j else 0):
                                reach(pe, block_copied, 2 * (QB * g + j))
                            for h in range(HG):
                                mm = pe.matmul(den_bank[h * HD:(h + 1) * HD, q0:], ones[0:rows, :], pT[0:rows, s % SLOTS, h, q0:],
                                               start=kt == (2 if j else 0), stop=j == 0 and last_tile)
                            mm.then_inc(p_used, 1)
                        if last_tile and j > 0:
                            reach(pe, pool_added, PO * g + PO_BEFORE[s + 1])
                            for h in range(HG):
                                mm = pe.matmul(den_bank[h * HD:(h + 1) * HD, :], ones[:, :], part_sum[:, j % 2, h], start=False, stop=True)
                            mm.then_inc(block_done, 1)

                    if first:
                        for q in range(FIRST_LEAD):
                            job(0, q)
                    steps = PLANS[first, last]
                    for s in range(ST):
                        for jobs, piece in zip(steps[s], PIECES):
                            for ahead, q in jobs:
                                job(ahead, q)
                            if isinstance(piece, int):
                                scores(s, piece)
                            elif s and piece == "values":
                                weigh_values(s - 1)
                            elif s:
                                denominators(s - 1)
                    weigh_values(ST - 1)
                    denominators(ST - 1)
                groups(pe, body)


def project_output(nc, x, aT, woT, bo, ident, neg_half, eps, x1_dram, xT_hi, xT_lo):
    ctx = ExitStack()
    with ctx:
        t = Tools(nc, ctx)
        w_in = t.sb("o_w_in", [P, DC, D])
        wo_hi, wo_lo = t.sb("wo_hi", [P, DC, D], F32R), t.sb("wo_lo", [P, DC, D], F32R)
        bo_all = t.sb("bo_all", [P, D])
        a_in = t.sb("a_in", [P, 2, DC, BLK])
        a_hi, a_lo = t.sb("a_hi", [P, 2, DC, BLK], F32R), t.sb("a_lo", [P, 2, DC, BLK], F32R)
        x_in = t.sb("o_x_in", [P, 2, 4, D])
        x1 = t.sb("x1", [P, 2, 4, D])
        xn = t.sb("o_xn", [P, 2, 4, D])
        stats = t.sb("o_stats", [P, 2, 4, 6])
        mean_var = t.sb("o_mean_var", [P, 2, 4, 2])
        var_eps = t.sb("o_var_eps", [P, 2, 4])
        rstd = t.sb("o_rstd", [P, 2, 4])
        t_hi, t_lo = t.sb("t_hi", [P, DC, BLK], F32R), t.sb("t_lo", [P, DC, BLK], F32R)
        bank, tbank = t.banks(4, "o_job_bank"), t.banks(4, "o_tbank")

        passed = t.sem("wo_loaded_sp_passed")
        w_loaded, bias_loaded = t.sem("wo_loaded"), t.sem("o_bias_loaded")
        w_hi_ready, w_lo_ready = t.sem("wo_hi_ready"), t.sem("wo_lo_ready")
        a_loaded = [t.sem("a_loaded0"), t.sem("a_loaded1")]
        x_loaded = [t.sem("o_x_loaded0"), t.sem("o_x_loaded1")]
        a_hi_ready, a_lo_ready, xb_ready = t.sem("a_hi_ready"), t.sem("a_lo_ready"), t.sem("o_xb_ready")
        job_done, x1_ready = t.sem("o_job_done"), t.sem("x1_ready")
        mv_ready, eps_ready, rstd_ready = t.sem("o_mv_ready"), t.sem("o_eps_ready"), t.sem("o_rstd_ready")
        stats_ready, passed_dve = t.sem("o_stats_ready"), t.sem("o_dve_passed")
        xn_ready, t_done = t.sem("o_xn_ready"), t.sem("o_t_done")
        t_hi_ready, t_lo_ready = t.sem("o_t_hi_ready"), t.sem("o_t_lo_ready")
        x1_stored = [t.sem("x1_stored0"), t.sem("x1_stored1")]
        t_stored = t.sem("t_stored")
        PAIRS = QB // 2 - 1

        def blocks(eng, ahead, process, behind):
            ahead(0, 0, 0)
            ahead(1, 1, 0)
            process(0, 0, 0)

            def pair(i):
                for k in (1, 2):
                    u = k % 2
                    ahead(2 * i + k + 1, 1 - u, i + 1)
                    process(2 * i + k, u, i + k - 1)
                    behind(2 * i + k - 1, 1 - u, i)
            pair(0)
            with eng.Fori(1, PAIRS) as i:
                pair(i)
            process(QB - 1, 1, PAIRS)
            behind(QB - 2, 0, PAIRS)
            behind(QB - 1, 1, PAIRS)

        def nothing(b, u, before):
            pass

        with nc.Block() as block:
            @block.sync
            def _(sp):
                sp.dma_start(w_in[:, :, :], woT.rearrange("(c p) n -> p c n", p=P)).then_inc(w_loaded, 16)
                sp.dma_start(bo_all[:, :], bo.partition_broadcast(P)).then_inc(bias_loaded, 16)

                def store(b, u, before):
                    rows = bass.ds(b * BLK, BLK)
                    hold(sp, x1_ready, 4 * (b + 1), passed)
                    sp.dma_start(x1_dram[rows, :].rearrange("(t p) n -> p t n", p=P), x1[:, u]).then_inc(x1_stored[u], 16)

                def store_t(b, u, before):
                    cols = bass.ds(b * BLK, BLK)
                    hold(sp, t_lo_ready, DC * (b + 1), passed)
                    sp.dma_start(xT_hi[:, cols].rearrange("(c p) n -> p c n", p=P), as_f32(t_hi[:, :, :])).then_inc(t_stored, 16)
                    sp.dma_start(xT_lo[:, cols].rearrange("(c p) n -> p c n", p=P), as_f32(t_lo[:, :, :])).then_inc(t_stored, 16)

                def load(b, u, before):
                    hold(sp, a_lo_ready, DC * (b - 1), passed)
                    hold(sp, x1_ready, 4 * (b - 1), passed)
                    cols = bass.ds(b * BLK, BLK)
                    sp.dma_start(a_in[:, u], aT[:, cols].rearrange("(c p) n -> p c n", p=P)).then_inc(a_loaded[u], 16)
                    sp.dma_start(x_in[:, u], x[cols, :].rearrange("(t p) n -> p t n", p=P)).then_inc(x_loaded[u], 16)
                blocks(sp, load, store, store_t)
                for u in range(2):
                    hold(sp, x1_stored[u], 16 * (QB // 2), passed)
                hold(sp, t_stored, 32 * QB, passed)

            @block.scalar
            def _(act):
                act.wait_ge(w_loaded, 16)
                act.activation(wo_hi[:, :, :], w_in[:, :, :], ACT.Copy).then_inc(w_hi_ready, 1)

                def split(b, u, before):
                    act.wait_ge(a_loaded[u], 16 * (before + 1))
                    reach(act, job_done, 4 * (b - 1))
                    for c in range(DC):
                        act.activation(a_hi[:, u, c], a_in[:, u, c], ACT.Copy).then_inc(a_hi_ready, 1)

                def copy_t(b, u, before):
                    reach(act, t_stored, 32 * b)
                    for c in range(DC):
                        act.wait_ge(t_done, DC * b + c + 1)
                        act.activation(t_hi[:, c], tbank[c][:, :], ACT.Copy).then_inc(t_hi_ready, 1)
                blocks(act, split, nothing, copy_t)

            @block.gpsimd
            def _(pool):
                pool.wait_ge(bias_loaded, 16)

                def split(b, u, before):
                    for c in range(DC):
                        pool.wait_ge(a_hi_ready, DC * b + c + 1)
                        pool.tensor_tensor(a_lo[:, u, c], a_in[:, u, c], as_f32(a_hi[:, u, c]), ALU.subtract).then_inc(a_lo_ready, 1)
                    pool.wait_ge(x_loaded[u], 16 * (before + 1))
                    for k in range(4):
                        pool.tensor_tensor(x_in[:, u, k], x_in[:, u, k], bo_all[:, :], ALU.add).then_inc(xb_ready, 1)

                def invert(b, u, before):
                    pool.wait_ge(mv_ready, 4 * (b + 1))
                    pool.tensor_tensor(var_eps[:, u], mean_var[:, u, :, 1], eps[:, :], ALU.add).then_inc(eps_ready, 1)
                    pool.wait_ge(eps_ready, b + 1)
                    pool.tensor_tensor(rstd[:, u], var_eps[:, u], neg_half[:, 0:4], ALU.pow).then_inc(rstd_ready, 1)
                blocks(pool, split, invert, nothing)

            @block.vector
            def _(dve):
                dve.wait_ge(w_hi_ready, 1)
                dve.tensor_tensor(wo_lo[:, :, :], w_in[:, :, :], as_f32(wo_hi[:, :, :]), ALU.subtract).then_inc(w_lo_ready, 1)

                def residual(b, u, before):
                    reach(dve, x1_stored[u], 16 * before)
                    for k in range(4):
                        dve.wait_ge(job_done, 4 * b + k + 1)
                        dve.wait_ge(xb_ready, 4 * b + k + 1)
                        dve.tensor_tensor(x1[:, u, k], bank[k][:, :], x_in[:, u, k], ALU.add).then_inc(x1_ready, 1)
                        if k:
                            dve.wait_ge(x1_ready, 4 * b + k)
                            dve.bn_stats(stats[:, u, k - 1], x1[:, u, k - 1]).then_inc(stats_ready, 1)
                    dve.wait_ge(x1_ready, 4 * b + 4)
                    dve.bn_stats(stats[:, u, 3], x1[:, u, 3]).then_inc(stats_ready, 1)
                    hold(dve, stats_ready, 4 * (b + 1), passed_dve)
                    for k in range(4):
                        dve.bn_aggr(mean_var[:, u, k], stats[:, u, k]).then_inc(mv_ready, 1)
                    if isinstance(b, int) and b in (0, QB - 1):
                        normalise(b, u)

                def normalise(b, u):
                    dve.wait_ge(rstd_ready, b + 1)
                    for k in range(4):
                        dve.tensor_scalar(xn[:, u, k], x1[:, u, k], mean_var[:, u, k, 0:1], rstd[:, u, k:k + 1],
                                          ALU.subtract, ALU.mult).then_inc(xn_ready, 1)

                def behind(b, u, before):
                    for c in range(DC):
                        dve.wait_ge(t_hi_ready, DC * b + c + 1)
                        dve.tensor_tensor(t_lo[:, c], tbank[c][:, :], as_f32(t_hi[:, c]), ALU.subtract).then_inc(t_lo_ready, 1)
                    if not isinstance(b, int) or b < QB - 2:
                        normalise(b + 1, 1 - u)
                blocks(dve, nothing, residual, behind)

            @block.tensor
            def _(pe):
                pe.wait_ge(w_lo_ready, 1)

                def project(b, u, before):
                    for n in range(4):
                        if n == 0:
                            pe.wait_ge(a_lo_ready, DC * (b + 1))
                        reach(pe, x1_ready, 4 * b)
                        rows = slice(n * P, (n + 1) * P)
                        for c in range(DC):
                            for k, (a, w) in enumerate(((a_hi, wo_hi), (a_hi, wo_lo), (a_lo, wo_hi))):
                                mm = pe.matmul(bank[n][:, :], a[:, u, c, rows], w[:, c], start=(c == 0 and k == 0),
                                               stop=(c == DC - 1 and k == 2))
                        mm.then_inc(job_done, 1)

                def transpose(b, u, before):
                    pe.wait_ge(xn_ready, 4 * (b + 1))
                    reach(pe, t_lo_ready, DC * b)
                    for c in range(DC):
                        for k in range(4):
                            mm = pe.transpose(tbank[c][:, k * P:(k + 1) * P], xn[:, u, k, c * P:(c + 1) * P], ident[:, :])
                        mm.then_inc(t_done, 1)
                blocks(pe, nothing, project, transpose)


PAIR = E // 2
GATE_AT = 2 * EC + 2
JOBS = FC + E * EC + PAIR + FC
RING = 4
JOB_W1 = [FC + k + (PAIR if k >= GATE_AT else 0) for k in range(E * EC)]
JOB_GATE = [FC + GATE_AT + p for p in range(PAIR)]
JOB_C2S = [FC + E * EC + PAIR + m for m in range(FC)]
assert JOBS % RING == 0


def feed_forward(nc, xT_hi, xT_lo, x1_dram, w, ident, neg_half, eps, out):
    ctx = ExitStack()
    with ctx:
        t = Tools(nc, ctx)
        we_hi, we_lo = t.sb("we_hi", [P, DC, FH], F32R), t.sb("we_lo", [P, DC, FH], F32R)
        wd_hi, wd_lo = t.sb("wd_hi", [P, FC, D], F32R), t.sb("wd_lo", [P, FC, D], F32R)
        w1_parts = t.sb("w1_parts", [P, E, EH], F32R)
        w2 = t.sb("w2", [P, E * EC, M])
        ws = t.sb("ws", [P, FC, 2, M])
        wc = t.sb("wc", [P, FH])
        wr = t.sb("wr", [M, E])
        be_col, bs_col, b1_col = t.sb("be_col", [P, FC]), t.sb("bs_col", [P, 1]), t.sb("b1_col", [P, E * EC])
        b2_col, bc_col = t.sb("b2_col", [P, PAIR]), t.sb("bc_col", [P, FC])
        br_all, bd_all = t.sb("br_all", [P, E]), t.sb("bd_all", [P, D])
        lng_all, lnb_all = t.sb("lng_all", [P, D]), t.sb("lnb_all", [P, D])
        select = t.sb("select", [P, PAIR, P], F32R)
        rank = t.sb("rank", [P, 4, E])
        base_e = t.sb("base_e", [P, 4, E])

        with ExitStack() as inner:
            s = Tools(nc, inner)
            e_in, d_in, w1_in = s.sb("e_in", [P, DC, FH]), s.sb("d_in", [P, FC, D]), s.sb("w1_in", [P, E, EH])
            sel_f = s.sb("sel_f", [P, PAIR, 2, M])
            e_loaded, d_loaded, w1_loaded = s.sem("e_loaded"), s.sem("d_loaded"), s.sem("w1_loaded")
            small_loaded = s.sem("small_loaded")
            hi_ready, lo_ready = s.sem("f_w_hi_ready"), s.sem("f_w_lo_ready")
            built = s.sem("f_built")
            with nc.Block() as block:
                @block.sync
                def _(sp):
                    sp.dma_start(e_in[:, :, :], w["W_enc"].rearrange("(c p) n -> p c n", p=P)).then_inc(e_loaded, 16)
                    sp.dma_start(d_in[:, :, :], w["W_dec"].rearrange("(c p) n -> p c n", p=P)).then_inc(d_loaded, 16)
                    loads = [(w2[:, :, :], w["W2"].rearrange("e (c p) m -> p (e c) m", p=P)),
                             (ws[:, :, 0, :], w["W_s2c"].rearrange("(c p) m -> p c m", p=P)),
                             (ws[:, :, 1, :], w["W_s2c"].rearrange("(c p) m -> p c m", p=P)),
                             (wc[0:M, :], w["W_c2s"]), (wc[M:P, :], w["W_c2s"]), (wr[:, :], w["Wr"]),
                             (bs_col[0:M, :], w["b_s2c"].rearrange("(p a) -> p a", a=1)),
                             (bs_col[M:P, :], w["b_s2c"].rearrange("(p a) -> p a", a=1))]
                    for dst, src in loads:
                        sp.dma_start(dst, src).then_inc(small_loaded, 16)
                    sp.wait_ge(small_loaded, 16 * 16)

                @block.scalar
                def _(act):
                    for half in range(2):
                        act.dma_start(w1_in[half * M:(half + 1) * M, :, :], w["W1"].rearrange("e m n -> m e n")).then_inc(w1_loaded, 16)
                    loads = [(be_col[:, :], w["b_enc"]),
                             (b1_col[:, :], w["b1"]),
                             (b2_col[:, :], w["b2"]),
                             (bc_col[:, :], w["b_c2s"]),
                             (br_all[:, :], w["br"].partition_broadcast(P)), (bd_all[:, :], w["b_dec"].partition_broadcast(P)),
                             (lng_all[:, :], w["ln_g"].partition_broadcast(P)), (lnb_all[:, :], w["ln_b"].partition_broadcast(P))]
                    for dst, src in loads:
                        act.dma_start(dst, src).then_inc(small_loaded, 16)
                    act.wait_ge(e_loaded, 16)
                    act.activation(we_hi[:, :, :], e_in[:, :, :], ACT.Copy).then_inc(hi_ready, 1)
                    act.wait_ge(d_loaded, 16)
                    act.activation(wd_hi[:, :, :], d_in[:, :, :], ACT.Copy).then_inc(hi_ready, 1)
                    act.wait_ge(w1_loaded, 32)
                    act.activation(w1_parts[:, :, :], w1_in[:, :, :], ACT.Copy).then_inc(hi_ready, 1)

                @block.vector
                def _(dve):
                    dve.wait_ge(hi_ready, 1)
                    dve.tensor_tensor(we_lo[:, :, :], e_in[:, :, :], as_f32(we_hi[:, :, :]), ALU.subtract).then_inc(lo_ready, 1)
                    dve.wait_ge(hi_ready, 2)
                    dve.tensor_tensor(wd_lo[:, :, :], d_in[:, :, :], as_f32(wd_hi[:, :, :]), ALU.subtract).then_inc(lo_ready, 1)
                    dve.wait_ge(hi_ready, 3)
                    dve.tensor_tensor(w1_parts[M:P, :, :], w1_in[M:P, :, :], as_f32(w1_parts[M:P, :, :]), ALU.subtract
                                      ).then_inc(lo_ready, 1)
                    dve.wait_ge(built, 3)
                    dve.tensor_copy(select[:, :, :], sel_f[:, :, :, :].rearrange("p a b c -> p a (b c)")).then_inc(lo_ready, 1)
                    dve.memset(base_e[:, :, :], 2.718281828459045).then_inc(lo_ready, 1)

                @block.gpsimd
                def _(pool):
                    pool.memset(sel_f[:, :, :, :], 0.0).then_inc(built, 1)
                    for n, row in enumerate((0, HD)):
                        pool.wait_ge(built, n + 1)
                        pool.affine_select(out=sel_f[:, :, :, :], in_=sel_f[:, :, :, :], compare_op=ALU.not_equal, fill=1.0,
                                           base=-row, pattern=[[-2, PAIR], [-1, 2], [0, M]], channel_multiplier=1).then_inc(built, 1)
                    for e in range(E):
                        pool.memset(rank[:, :, e:e + 1], float(E - e)).then_inc(built, 1)

        x_hi, x_lo = t.sb("f_x_hi", [P, 2, DC, BLK], F32R), t.sb("f_x_lo", [P, 2, DC, BLK], F32R)
        xb = t.sb("f_xb", [P, 4, D])
        sT = t.sb("sT", [P, 2, BLK])
        c_parts = t.sb("c_parts", [P, 2, BLK], F32R)
        c_f = t.sb("c_f", [M, BLK])
        logits, expd, prob = t.sb("logits", [P, 4, E]), t.sb("expd", [P, 4, E]), t.sb("prob", [P, 4, E])
        same, first1, first2, gate = (t.sb(n, [P, 4, E]) for n in ("same", "first1", "first2", "gate"))
        top = t.sb("top", [P, 8, 4])
        g_parts = t.sb("g_parts", [P, BLK], F32R)
        g_sb = t.sb("g_sb", [P, PAIR, BLK])
        hT = t.sb("hT", [P, RING, BLK])
        y_gated, moe = t.sb("y_gated", [P, BLK]), t.sb("moe", [P, BLK])
        sp_f = t.sb("sp_f", [P, 2, BLK])
        sp_hi, sp_lo = t.sb("sp_hi", [P, 2, BLK], F32R), t.sb("sp_lo", [P, 2, BLK], F32R)
        y = t.sb("y", [P, 4, D])
        stats, mean_var = t.sb("f_stats", [P, 4, 6]), t.sb("f_mean_var", [P, 4, 2])
        var_eps, rstd = t.sb("f_var_eps", [P, 4]), t.sb("f_rstd", [P, 4])
        ring, acc = t.banks(RING, "ring"), t.banks(4, "acc")

        x_loaded = [t.sem("f_x_loaded0"), t.sem("f_x_loaded1")]
        passed = t.sem("f_x1_loaded_sp_passed")
        x1_loaded, xb_ready = t.sem("f_x1_loaded"), t.sem("f_xb_ready")
        ring_done, ring_free = t.sem("ring_done"), t.sem("ring_free")
        s_used, h_used = t.sem("sT_used"), t.sem("hT_used")
        c_hi_ready, c_lo_ready, c_f_ready = t.sem("f_c_hi_ready"), t.sem("f_c_lo_ready"), t.sem("c_f_ready")
        logits_done, dist_ready, expd_ready = t.sem("logits_done"), t.sem("dist_ready"), t.sem("expd_ready")
        route = t.sem("route_step")
        gate_ready, gT_done, g_parts_ready = t.sem("gate_ready"), t.sem("gT_done"), t.sem("g_parts_ready")
        gated = t.sem("gated")
        gated_step, moe_ready = t.sem("gated_step"), t.sem("moe_ready")
        sp_hi_ready, sp_lo_ready, sp_used = t.sem("sp_hi_ready"), t.sem("sp_lo_ready"), t.sem("sp_used")
        y_ready = t.sem("y_ready")
        mv_ready, eps_ready, rstd_ready = t.sem("f_mv_ready"), t.sem("f_eps_ready"), t.sem("f_rstd_ready")
        stats_ready, scaled, passed_dve = t.sem("f_stats_ready"), t.sem("scaled"), t.sem("f_dve_passed")
        out_ready, out_stored = t.sem("out_ready"), t.sem("out_stored")

        def blocks(eng, body):
            body(0, 0, 0)
            body(1, 1, 0)
            with eng.Fori(1, QB // 2) as i:
                for u in range(2):
                    body(2 * i + u, u, i)

        ROUTE = 20

        with nc.Block() as block:
            @block.sync
            def _(sp):
                def load(b, u, before):
                    cols = bass.ds(b * BLK, BLK)
                    hold(sp, s_used, FC * (b + 1), passed)
                    sp.dma_start(as_f32(x_hi[:, u]), xT_hi[:, cols].rearrange("(c p) n -> p c n", p=P)).then_inc(x_loaded[u], 16)
                    sp.dma_start(as_f32(x_lo[:, u]), xT_lo[:, cols].rearrange("(c p) n -> p c n", p=P)).then_inc(x_loaded[u], 16)
                    hold(sp, out_ready, 4 * b, passed)
                    sp.dma_start(xb[:, :, :], x1_dram[cols, :].rearrange("(t p) n -> p t n", p=P)).then_inc(x1_loaded, 16)
                blocks(sp, load)

            @block.gpsimd
            def _(pool):
                def body(b, u, before):
                    pool.wait_ge(x1_loaded, 16 * (b + 1))
                    for k in range(4):
                        pool.tensor_tensor(xb[:, k], xb[:, k], lnb_all[:, :], ALU.add).then_inc(xb_ready, 1)
                    pool.wait_ge(dist_ready, b + 1)
                    pool.tensor_tensor(expd[:, :, :], base_e[:, :, :], logits[:, :, :], ALU.pow).then_inc(expd_ready, 1)
                    pool.wait_ge(mv_ready, 4 * (b + 1))
                    pool.tensor_tensor(var_eps[:, :], mean_var[:, :, 1], eps[:, :], ALU.add).then_inc(eps_ready, 1)
                    pool.wait_ge(eps_ready, b + 1)
                    pool.tensor_tensor(rstd[:, :], var_eps[:, :], neg_half[:, 0:4], ALU.pow).then_inc(rstd_ready, 1)
                    pool.wait_ge(out_ready, 4 * (b + 1))
                    pool.dma_start(out[bass.ds(b * BLK, BLK), :].rearrange("(t p) n -> p t n", p=P), y[:, :, :]).then_inc(out_stored, 16)
                blocks(pool, body)
                pool.wait_ge(out_stored, 16 * QB)

            @block.scalar
            def _(act):
                def body(b, u, before):
                    def take(n):
                        act.wait_ge(ring_done, JOBS * b + n + 1)
                        return ring[n % RING]

                    for m in range(FC):
                        src = take(m)
                        act.wait_ge(s_used, 2 * FC - 2 + FC * b + m + 1)
                        act.activation(sT[:, m % 2], src[:, :], ACT.Sigmoid, bias=be_col[:, m:m + 1]).then_inc(ring_free, 1)
                    act.wait_ge(s_used, FC * (b + 3))
                    act.activation(c_parts[:, 0], acc[0][:, :], ACT.Identity, bias=bs_col[:, 0:1]).then_inc(c_hi_ready, 1)
                    for k in range(E * EC):
                        if k == GATE_AT:
                            for p in range(PAIR):
                                src = take(JOB_GATE[p])
                                if p == 0:
                                    reach(act, gated, PAIR * b)
                                act.activation(g_sb[:, p], src[:, :], ACT.Copy).then_inc(ring_free, 1)
                        p, c, half = k // (2 * EC), k % (2 * EC) // 2, k % 2
                        src = take(JOB_W1[k])
                        act.wait_ge(h_used, E * EC // 2 * b + k // 2 + 1)
                        col = (2 * p + half) * EC + c
                        act.activation(hT[:, k % RING], src[:, :], ACT.Relu, bias=b1_col[:, col:col + 1]).then_inc(ring_free, 1)
                    for m in range(FC):
                        src = take(JOB_C2S[m])
                        act.wait_ge(sp_lo_ready, FC * b + m + 1)
                        act.activation(sp_f[:, m % 2], src[:, :], ACT.Sigmoid, bias=bc_col[:, m:m + 1]).then_inc(ring_free, 1)
                blocks(act, body)

            @block.vector
            def _(dve):
                dve.memset(as_f32(g_parts[:, :]), 0.0)
                dve.sem_inc(sp_lo_ready, 2)

                def body(b, u, before):
                    dve.wait_ge(c_hi_ready, b + 1)
                    dve.scalar_tensor_tensor(c_parts[:, 1], acc[0][:, :], bs_col[:, 0:1], as_f32(c_parts[:, 0]),
                                             ALU.add, ALU.subtract).then_inc(c_lo_ready, 1)
                    dve.tensor_scalar(c_f[:, :], acc[0][0:M, :], bs_col[0:M, 0:1], None, ALU.add).then_inc(c_f_ready, 1)

                    steps = [0]

                    def step(ins):
                        steps[0] += 1
                        ins.then_inc(route, 1)
                        dve.wait_ge(route, ROUTE * b + steps[0])

                    def over(col):
                        return top[:, col].unsqueeze(2).to_broadcast([P, 4, E])

                    dve.wait_ge(logits_done, b + 1)
                    step(dve.tensor_tensor(logits[:, :, :], acc[1][:, 0:4 * E].rearrange("p (t e) -> p t e", e=E),
                                           br_all[:, :].unsqueeze(1).to_broadcast([P, 4, E]), ALU.add))
                    step(dve.tensor_reduce(top[:, 0], logits[:, :, :], AX_X, ALU.max))
                    dve.tensor_tensor(logits[:, :, :], logits[:, :, :], over(0), ALU.subtract).then_inc(dist_ready, 1)
                    dve.wait_ge(expd_ready, b + 1)
                    step(dve.tensor_reduce(top[:, 1], expd[:, :, :], AX_X, ALU.add))
                    step(dve.reciprocal(top[:, 2], top[:, 1]))
                    step(dve.tensor_tensor(prob[:, :, :], expd[:, :, :], over(2), ALU.mult))
                    step(dve.tensor_reduce(top[:, 3], prob[:, :, :], AX_X, ALU.max))
                    step(dve.tensor_tensor(same[:, :, :], prob[:, :, :], over(3), ALU.is_equal))
                    step(dve.tensor_tensor(same[:, :, :], same[:, :, :], rank[:, :, :], ALU.mult))
                    step(dve.tensor_reduce(top[:, 4], same[:, :, :], AX_X, ALU.max))
                    step(dve.tensor_tensor(first1[:, :, :], same[:, :, :], over(4), ALU.is_equal))
                    step(dve.scalar_tensor_tensor(prob[:, :, :], first1[:, :, :], -2.0, prob[:, :, :], ALU.mult, ALU.add))
                    step(dve.tensor_reduce(top[:, 5], prob[:, :, :], AX_X, ALU.max))
                    step(dve.tensor_tensor(same[:, :, :], prob[:, :, :], over(5), ALU.is_equal))
                    step(dve.tensor_tensor(same[:, :, :], same[:, :, :], rank[:, :, :], ALU.mult))
                    step(dve.tensor_reduce(top[:, 6], same[:, :, :], AX_X, ALU.max))
                    step(dve.tensor_tensor(top[:, 7], top[:, 3], top[:, 5], ALU.add))
                    step(dve.tensor_tensor(first2[:, :, :], same[:, :, :], over(6), ALU.is_equal))
                    step(dve.reciprocal(top[:, 7], top[:, 7]))
                    step(dve.tensor_tensor(first2[:, :, :], first2[:, :, :], over(5), ALU.mult))
                    step(dve.tensor_tensor(first1[:, :, :], first1[:, :, :], over(3), ALU.mult))
                    assert steps[0] == ROUTE
                    gather_gate(b)

                    dve.wait_ge(gT_done, b + 1)
                    dve.tensor_copy(g_parts[0:E, :], acc[1][0:E, :]).then_inc(g_parts_ready, 1)
                    dve.wait_ge(g_parts_ready, 2 * b + 1)
                    dve.tensor_tensor(g_parts[HD:HD + E, :], acc[1][0:E, :], as_f32(g_parts[0:E, :]), ALU.subtract
                                      ).then_inc(g_parts_ready, 1)

                    for p in range(PAIR):
                        dve.wait_ge(h_used, 2 + EC * (PAIR * b + p + 1))
                        dve.wait_ge(ring_free, 4 + JOBS * b + JOB_GATE[p] + 1)
                        reach(dve, moe_ready, (PAIR - 1) * b + max(0, p - 1))
                        dst = moe if p == 0 else y_gated
                        dve.scalar_tensor_tensor(dst[:, :], acc[2 + p % 2][:, :], b2_col[:, p:p + 1], g_sb[:, p],
                                                 ALU.add, ALU.mult).then_inc(gated, 1)
                        if p:
                            dve.wait_ge(gated, PAIR * b + p + 1)
                            dve.tensor_tensor(moe[:, :], moe[:, :], y_gated[:, :], ALU.add).then_inc(moe_ready, 1)
                    for m in range(FC):
                        dve.wait_ge(ring_free, 4 + JOBS * b + JOB_C2S[m] + 1)
                        dve.wait_ge(sp_used, FC * b + m + 1)
                        dve.tensor_copy(sp_hi[:, m % 2], sp_f[:, m % 2]).then_inc(sp_hi_ready, 1)
                        dve.wait_ge(sp_hi_ready, FC * b + m + 1)
                        dve.tensor_tensor(sp_lo[:, m % 2], sp_f[:, m % 2], as_f32(sp_hi[:, m % 2]), ALU.subtract
                                          ).then_inc(sp_lo_ready, 1)
                    dve.wait_ge(sp_used, 2 + FC * (b + 1))
                    reach(dve, out_stored, 16 * b)
                    for k in range(4):
                        dve.tensor_tensor(y[:, k], acc[k][:, :], bd_all[:, :], ALU.add).then_inc(y_ready, 1)
                    for k in range(4):
                        dve.wait_ge(y_ready, 4 * b + k + 1)
                        dve.bn_stats(stats[:, k], y[:, k]).then_inc(stats_ready, 1)
                    hold(dve, stats_ready, 4 * (b + 1), passed_dve)
                    for k in range(4):
                        dve.bn_aggr(mean_var[:, k], stats[:, k]).then_inc(mv_ready, 1)
                    dve.wait_ge(mv_ready, 4 * (b + 1))
                    for k in range(4):
                        dve.scalar_tensor_tensor(y[:, k], y[:, k], mean_var[:, k, 0:1], lng_all[:, :], ALU.subtract, ALU.mult
                                                 ).then_inc(scaled, 1)
                    dve.wait_ge(rstd_ready, b + 1)
                    dve.wait_ge(xb_ready, 4 * (b + 1))
                    dve.wait_ge(scaled, 4 * (b + 1))
                    for k in range(4):
                        dve.scalar_tensor_tensor(y[:, k], y[:, k], rstd[:, k:k + 1], xb[:, k], ALU.mult, ALU.add
                                                 ).then_inc(out_ready, 1)

                def gather_gate(b):
                    dve.tensor_tensor(gate[:, :, :], first1[:, :, :], first2[:, :, :], ALU.add).then_inc(gated_step, 1)
                    dve.wait_ge(gated_step, b + 1)
                    dve.tensor_tensor(gate[:, :, :], gate[:, :, :], top[:, 7].unsqueeze(2).to_broadcast([P, 4, E]), ALU.mult
                                      ).then_inc(gate_ready, 1)
                blocks(dve, body)

            @block.tensor
            def _(pe):
                pe.sem_inc(s_used, 2 * FC)
                pe.sem_inc(h_used, 2)
                pe.sem_inc(sp_used, 2)
                pe.sem_inc(ring_free, RING)

                def body(b, u, before):
                    def bank(n):
                        pe.wait_ge(ring_free, JOBS * b + n + 1)
                        return ring[n % RING]

                    def encode(m):
                        dst = bank(m)
                        cols = slice(m * P, (m + 1) * P)
                        for c in range(DC):
                            for k, (ww, xx) in enumerate(((we_hi, x_hi), (we_hi, x_lo), (we_lo, x_hi))):
                                mm = pe.matmul(dst[:, :], ww[:, c, cols], xx[:, u, c], start=(c == 0 and k == 0),
                                               stop=(c == DC - 1 and k == 2))
                        mm.then_inc(ring_done, 1)

                    def to_cont(m):
                        if m == 0:
                            reach(pe, y_ready, 4 * b)
                        pe.wait_ge(ring_free, RING + JOBS * b + m + 1)
                        mm = pe.matmul(acc[0][:, :], ws[:, m].rearrange("p a b -> p (a b)"), sT[:, m % 2], start=m == 0, stop=m == FC - 1)
                        mm.then_inc(s_used, 1)

                    pe.wait_ge(x_loaded[u], 32 * (before + 1))
                    for m in range(FC):
                        encode(m)
                        if m:
                            to_cont(m - 1)
                    to_cont(FC - 1)

                    def hidden(k):
                        p, c, half = k // (2 * EC), k % (2 * EC) // 2, k % 2
                        dst = bank(JOB_W1[k])
                        if k == 0:
                            pe.wait_ge(c_lo_ready, b + 1)
                        for part in range(2):
                            mm = pe.matmul(dst[:, :], w1_parts[:, 2 * p + half, c * P:(c + 1) * P], c_parts[:, part],
                                           start=part == 0, stop=part == 1)
                        mm.then_inc(ring_done, 1)

                    def expert_out(q):
                        p, c = q // EC, q % EC
                        pe.wait_ge(ring_free, RING + JOBS * b + JOB_W1[2 * q + 1] + 1)
                        if c == 0:
                            reach(pe, gated, PAIR * b + max(0, p - 1))
                        for half in range(2):
                            mm = pe.matmul(acc[2 + p % 2][half * M:(half + 1) * M, :], w2[:, (2 * p + half) * EC + c, :],
                                           hT[:, (2 * q + half) % RING], start=c == 0, stop=c == EC - 1)
                        mm.then_inc(h_used, 1)

                    def router():
                        pe.wait_ge(c_f_ready, b + 1)
                        for k in range(4):
                            mm = pe.matmul(acc[1][:, k * E:(k + 1) * E], c_f[:, k * P:(k + 1) * P], wr[:, :], start=True, stop=True)
                        mm.then_inc(logits_done, 1)

                    def spread_gates():
                        pe.wait_ge(gate_ready, b + 1)
                        for k in range(4):
                            mm = pe.transpose(acc[1][0:E, k * P:(k + 1) * P], gate[:, k], ident[:, :])
                        mm.then_inc(gT_done, 1)
                        for p in range(PAIR):
                            dst = bank(JOB_GATE[p])
                            pe.wait_ge(g_parts_ready, 2 * (b + 1))
                            pe.matmul(dst[:, :], select[:, p], g_parts[:, :], start=True, stop=True).then_inc(ring_done, 1)

                    for q in range(E * EC // 2):
                        if 2 * q == GATE_AT:
                            spread_gates()
                        hidden(2 * q)
                        hidden(2 * q + 1)
                        if q == 0:
                            router()
                        if q:
                            expert_out(q - 1)
                    expert_out(E * EC // 2 - 1)

                    def spikes(m):
                        dst = bank(JOB_C2S[m])
                        if m == 0:
                            pe.wait_ge(moe_ready, (PAIR - 1) * (b + 1))
                        pe.matmul(dst[:, :], wc[:, m * P:(m + 1) * P], moe[:, :], start=True, stop=True).then_inc(ring_done, 1)

                    def decode(m):
                        pe.wait_ge(sp_lo_ready, 2 + FC * b + m + 1)
                        for k in range(4):
                            rows = slice(k * P, (k + 1) * P)
                            for n, (a, ww) in enumerate(((sp_hi, wd_hi), (sp_hi, wd_lo), (sp_lo, wd_hi))):
                                mm = pe.matmul(acc[k][:, :], a[:, m % 2, rows], ww[:, m], start=(m == 0 and n == 0),
                                               stop=(m == FC - 1 and n == 2))
                        mm.then_inc(sp_used, 1)

                    spikes(0)
                    for m in range(FC):
                        if m + 1 < FC:
                            spikes(m + 1)
                        decode(m)
                blocks(pe, body)


def decoder_layer(nc, a):
    ctx = ExitStack()
    with ctx:
        t = Tools(nc, ctx)

        def scratch(name, shape, dt):
            return nc.dram_tensor(name, shape, dt, kind="Internal").ap()

        kT_hi, kT_lo = scratch("kT_hi", (D, NK_PAD), F32), scratch("kT_lo", (D, NK_PAD), F32)
        v_dram = scratch("v_dram", (NK_PAD, D), F32)
        qT_hi, qT_lo = scratch("qT_hi", (D, NQ), F32), scratch("qT_lo", (D, NQ), F32)
        aT = scratch("aT", (D, NQ), F32)
        x1 = scratch("x1_dram", (NQ, D), F32)
        nT_hi, nT_lo = scratch("nT_hi", (D, NQ), F32), scratch("nT_lo", (D, NQ), F32)

        ident, ident_b = t.sb("ident", [P, P]), t.sb("ident_b", [P, P], BF16)
        mask, maskT = t.sb("mask", [P, P], BF16), t.sb("maskT", [P, P], BF16)
        head_rows = t.sb("head_rows", [P, HG])
        neg_half, eps = t.sb("neg_half", [P, 4]), t.sb("eps", [P, 4])
        built = t.sem("const_built")
        with nc.Block() as block:
            @block.gpsimd
            def _(pool):
                for m in (ident, ident_b, mask, maskT):
                    pool.memset(m[:, :], 0.0).then_inc(built, 1)
                pool.memset(head_rows[:, :], 1.0).then_inc(built, 1)
                pool.memset(neg_half[:, :], -0.5).then_inc(built, 1)
                pool.memset(eps[:, :], EPS).then_inc(built, 1)
                pool.wait_ge(built, 7)
                for m in (ident, ident_b):
                    pool.affine_select(out=m[:, :], in_=m[:, :], compare_op=ALU.not_equal, fill=1.0, base=0,
                                       pattern=[[-1, P]], channel_multiplier=1).then_inc(built, 1)
                pool.affine_select(out=mask[:, :], in_=mask[:, :], compare_op=ALU.is_ge, fill=MASKED, base=0,
                                   pattern=[[-1, P]], channel_multiplier=1).then_inc(built, 1)
                pool.affine_select(out=maskT[:, :], in_=maskT[:, :], compare_op=ALU.is_ge, fill=MASKED, base=0,
                                   pattern=[[1, P]], channel_multiplier=-1).then_inc(built, 1)
                pool.affine_select(out=head_rows[:, :], in_=head_rows[:, :], compare_op=ALU.is_ge, fill=0.0, base=-R_MAX,
                                   pattern=[[-2, HG]], channel_multiplier=1).then_inc(built, 1)
                pool.wait_ge(built, 12)
                pool.affine_select(out=head_rows[:, :], in_=head_rows[:, :], compare_op=ALU.is_ge, fill=0.0, base=R_MAX + 1,
                                   pattern=[[2, HG]], channel_multiplier=-1).then_inc(built, 1)

        project_keys_values(nc, a["ctxT"], a["wkT"], a["wvT"], a["bk"], a["bv"], kT_hi, kT_lo, v_dram)
        project_queries(nc, a["x"], a["wqT"], a["bq"], ident, neg_half, eps, qT_hi, qT_lo)
        attend(nc, qT_hi, qT_lo, kT_hi, kT_lo, v_dram, aT, ident_b, mask, maskT, head_rows)
        project_output(nc, a["x"], aT, a["woT"], a["bo"], ident, neg_half, eps, x1, nT_hi, nT_lo)
        feed_forward(nc, nT_hi, nT_lo, x1, a, ident, neg_half, eps, a["out"])


def kernel(**inputs):
    import numpy as np
    import concourse.bacc as bacc
    from concourse.bass_utils import run_bass_kernel_spmd

    i = {name: np.asarray(value) for name, value in inputs.items()}
    ctxT = np.zeros((D, NK_PAD), i["ctx_1024"].dtype)
    ctxT[:, :NK] = i["ctx_1024"][0].T
    arrays = {"x": i["x"][0], "ctxT": ctxT}
    for n in "qkvo":
        arrays[f"w{n}T"] = i[f"L0_xattn_W{n}"].T
        arrays[f"b{n}"] = i[f"L0_xattn_b{n}"]
    for n in ("W_enc", "b_enc", "W_s2c", "b_s2c", "Wr", "br", "W1", "b1", "W2", "b2", "W_c2s", "b_c2s", "W_dec", "b_dec",
              "ln_g", "ln_b"):
        arrays[n] = i[f"L0_ffn_{n}"]
    for n in ("bq", "bk", "b_enc", "b1", "b2", "b_c2s"):
        arrays[n] = arrays[n].reshape(-1, P).T
    arrays = {n: np.ascontiguousarray(v) for n, v in arrays.items()}

    nc = bacc.Bacc("TRN2", target_bir_lowering=False, num_devices=1)
    dram = {n: nc.dram_tensor(f"in_{n}", v.shape, mybir.dt.from_np(v.dtype), kind="ExternalInput").ap() for n, v in arrays.items()}
    dram["out"] = nc.dram_tensor("out_rows", (NQ, D), F32, kind="ExternalOutput").ap()
    decoder_layer(nc, dram)
    r = run_bass_kernel_spmd(nc, [{f"in_{n}": v for n, v in arrays.items()}], core_ids=[0])
    return r.results[0]["out_rows"].reshape(1, NQ, D)
```

```python
from contextlib import ExitStack

import concourse.bass as bass
from concourse import mybir

F32 = mybir.dt.float32
F32R = mybir.dt.float32r
BF16 = mybir.dt.bfloat16
ALU = mybir.AluOpType
ACT = mybir.ActivationFunctionType
AX_X = mybir.AxisListType.X

P = 128
BLK = 512
NQ = 4096
NK = 3202
NK_PAD = 3584
D = 512
DC = D // P
H = 16
HD = 32
HG = P // HD
NG = H // HG
SCALE = HD ** -0.5
EPS = 1e-5
QB = NQ // BLK
KB = NK_PAD // BLK
KT = -(-NK // P)
K_LAST = NK - (KT - 1) * P
MASKED = -1e30
FH = 1024
FC = FH // P
M = 64
E = 8
EH = 512
EC = EH // P


def as_f32(ap):
    return ap.bitcast(F32)


def reach(eng, sem, n):
    if not isinstance(n, int) or n > 0:
        eng.wait_ge(sem, n)


def hold(eng, sem, n, passed):
    if not isinstance(n, int) or n > 0:
        eng.wait_ge(sem, n)
        eng.sem_inc(passed, 1)


class Tools:

    def __init__(self, nc, ctx):
        self.nc, self.ctx = nc, ctx

    def sb(self, name, shape, dt=F32):
        return self.ctx.enter_context(self.nc.sbuf_tensor(name, shape, dt))

    def banks(self, n, name):
        return [self.ctx.enter_context(self.nc.psum_tensor(f"{name}{i}", [P, BLK], F32)) for i in range(n)]

    def sem(self, name):
        return self.ctx.enter_context(self.nc.semaphore(name))


def project_keys_values(nc, ctxT, wkT, wvT, bk, bv, kT_hi, kT_lo, v_dram):
    ctx = ExitStack()
    with ctx:
        t = Tools(nc, ctx)
        w_in = t.sb("kv_w_in", [P, 2, DC, D])
        wk_hi, wk_lo = t.sb("wk_hi", [P, DC, D], F32R), t.sb("wk_lo", [P, DC, D], F32R)
        wv_hi, wv_lo = t.sb("wv_hi", [P, DC, D], F32R), t.sb("wv_lo", [P, DC, D], F32R)
        bk_col = t.sb("bk_col", [P, DC])
        bv_all = t.sb("bv_all", [P, D])
        c_in = t.sb("c_in", [P, 2, DC, BLK])
        c_hi, c_lo = t.sb("c_hi", [P, 2, DC, BLK], F32R), t.sb("c_lo", [P, 2, DC, BLK], F32R)
        k_hi, k_lo = t.sb("k_hi", [P, 2, DC, BLK], F32R), t.sb("k_lo", [P, 2, DC, BLK], F32R)
        v_out = t.sb("v_out", [P, 2, DC, D])
        bank = t.banks(4, "kv_bank")

        passed = t.sem("kv_bias_loaded_sp_passed")
        bias_loaded = t.sem("kv_bias_loaded")
        w_loaded = [t.sem("wk_loaded"), t.sem("wv_loaded")]
        w_hi_ready, w_lo_ready = t.sem("kv_w_hi_ready"), t.sem("kv_w_lo_ready")
        c_loaded = [t.sem("c_loaded0"), t.sem("c_loaded1")]
        c_hi_ready, c_lo_ready = t.sem("c_hi_ready"), t.sem("c_lo_ready")
        job_done = t.sem("kv_job_done")
        k_hi_ready = t.sem("k_hi_ready")
        bank_free = t.sem("kv_bank_free")
        k_stored = [t.sem("k_stored0"), t.sem("k_stored1")]
        v_stored = [t.sem("v_stored0"), t.sem("v_stored1")]

        JOBS = 2 * DC
        PAIRS = (KB - 1) // 2
        assert KB == 2 * PAIRS + 1

        def blocks(eng, body):
            body(0, 0, 0, True)
            body(1, 1, 0, True)
            with eng.Fori(1, PAIRS) as i:
                for u in range(2):
                    body(2 * i + u, u, i, True)
            body(2 * PAIRS, 0, PAIRS, False)

        with nc.Block() as block:
            @block.sync
            def _(sp):
                sp.dma_start(w_in[:, 0], wkT.rearrange("(c p) n -> p c n", p=P)).then_inc(w_loaded[0], 16)
                sp.dma_start(c_in[:, 0], ctxT[:, 0:BLK].rearrange("(c p) n -> p c n", p=P)).then_inc(c_loaded[0], 16)
                sp.dma_start(w_in[:, 1], wvT.rearrange("(c p) n -> p c n", p=P)).then_inc(w_loaded[1], 16)

                def load_next(b, u, before, more):
                    if more:
                        hold(sp, c_lo_ready, DC * b, passed)
                        sp.dma_start(c_in[:, 1 - u], ctxT[:, bass.ds((b + 1) * BLK, BLK)].rearrange(
                            "(c p) n -> p c n", p=P)).then_inc(c_loaded[1 - u], 16)
                blocks(sp, load_next)

            @block.gpsimd
            def _(pool):
                pool.dma_start(bk_col[:, :], bk).then_inc(bias_loaded, 16)
                pool.dma_start(bv_all[:, :], bv.partition_broadcast(P)).then_inc(bias_loaded, 16)

                def store(b, u, before, more):
                    cols = bass.ds(b * BLK, BLK)
                    pool.wait_ge(bank_free, 4 + JOBS * b + DC)
                    pool.dma_start(kT_hi[:, cols].rearrange("(c p) n -> p c n", p=P), as_f32(k_hi[:, u])).then_inc(k_stored[u], 16)
                    pool.dma_start(kT_lo[:, cols].rearrange("(c p) n -> p c n", p=P), as_f32(k_lo[:, u])).then_inc(k_stored[u], 16)
                    pool.wait_ge(bank_free, 4 + JOBS * b + 2 * DC)
                    pool.dma_start(v_dram[cols, :].rearrange("(t p) n -> p t n", p=P), v_out[:, u]).then_inc(v_stored[u], 16)
                blocks(pool, store)
                for u in range(2):
                    pool.wait_ge(k_stored[u], 32 * (PAIRS + 1 - u))
                    pool.wait_ge(v_stored[u], 16 * (PAIRS + 1 - u))

            @block.scalar
            def _(act):
                for w, hi in enumerate((wk_hi, wv_hi)):
                    act.wait_ge(w_loaded[w], 16)
                    act.activation(hi[:, :, :], w_in[:, w], ACT.Copy).then_inc(w_hi_ready, 1)
                    if w == 0:
                        act.wait_ge(c_loaded[0], 16)
                        for c in range(DC):
                            act.activation(c_hi[:, 0, c], c_in[:, 0, c], ACT.Copy).then_inc(c_hi_ready, 1)

                def body(b, u, before, more):
                    for n in range(DC):
                        act.wait_ge(job_done, JOBS * b + n + 1)
                        if n == 0:
                            act.wait_ge(bias_loaded, 32)
                            reach(act, k_stored[u], 32 * before)
                        act.activation(k_hi[:, u, n], bank[n][:, :], ACT.Identity, bias=bk_col[:, n:n + 1]).then_inc(k_hi_ready, 1)
                    if more:
                        act.wait_ge(c_loaded[1 - u], 16 * (before + 1 + u))
                        for c in range(DC):
                            act.activation(c_hi[:, 1 - u, c], c_in[:, 1 - u, c], ACT.Copy).then_inc(c_hi_ready, 1)
                blocks(act, body)

            @block.vector
            def _(dve):
                dve.sem_inc(bank_free, 4)
                for w, (hi, lo) in enumerate(((wk_hi, wk_lo), (wv_hi, wv_lo))):
                    dve.wait_ge(w_hi_ready, w + 1)
                    dve.tensor_tensor(lo[:, :, :], w_in[:, w], as_f32(hi[:, :, :]), ALU.subtract).then_inc(w_lo_ready, 1)
                    if w == 0:
                        for c in range(DC):
                            dve.wait_ge(c_hi_ready, c + 1)
                            dve.tensor_tensor(c_lo[:, 0, c], c_in[:, 0, c], as_f32(c_hi[:, 0, c]), ALU.subtract).then_inc(c_lo_ready, 1)

                def body(b, u, before, more):
                    dve.wait_ge(bias_loaded, 32)
                    for n in range(DC):
                        dve.wait_ge(k_hi_ready, DC * b + n + 1)
                        dve.scalar_tensor_tensor(k_lo[:, u, n], bank[n][:, :], bk_col[:, n:n + 1], as_f32(k_hi[:, u, n]),
                                                 ALU.add, ALU.subtract).then_inc(bank_free, 1)
                    for n in range(DC):
                        dve.wait_ge(job_done, JOBS * b + DC + n + 1)
                        if n == 0:
                            reach(dve, v_stored[u], 16 * before)
                        dve.tensor_tensor(v_out[:, u, n], bank[n][:, :], bv_all[:, :], ALU.add).then_inc(bank_free, 1)
                        for c in range(2 * n, 2 * n + 2) if more and n < DC // 2 else ():
                            dve.wait_ge(c_hi_ready, DC * (b + 1) + c + 1)
                            dve.tensor_tensor(c_lo[:, 1 - u, c], c_in[:, 1 - u, c], as_f32(c_hi[:, 1 - u, c]),
                                              ALU.subtract).then_inc(c_lo_ready, 1)
                blocks(dve, body)

            @block.tensor
            def _(pe):
                pe.wait_ge(w_lo_ready, 1)

                def body(b, u, before, more):
                    pe.wait_ge(c_lo_ready, DC * (b + 1))
                    for n in range(JOBS):
                        pe.wait_ge(bank_free, JOBS * b + n + 1)
                        if n == DC:
                            pe.wait_ge(w_lo_ready, 2)
                        first = True
                        for c in range(DC):
                            if n < DC:
                                cols = slice(n * P, (n + 1) * P)
                                terms = [(wk_hi[:, c, cols], c_hi[:, u, c]), (wk_hi[:, c, cols], c_lo[:, u, c]),
                                         (wk_lo[:, c, cols], c_hi[:, u, c])]
                            else:
                                cols = slice((n - DC) * P, (n - DC + 1) * P)
                                terms = [(c_hi[:, u, c, cols], wv_hi[:, c]), (c_hi[:, u, c, cols], wv_lo[:, c]),
                                         (c_lo[:, u, c, cols], wv_hi[:, c])]
                            for k, (lhsT, rhs) in enumerate(terms):
                                mm = pe.matmul(bank[n % DC][:, :], lhsT, rhs, start=first, stop=(c == DC - 1 and k == 2))
                                first = False
                        mm.then_inc(job_done, 1)
                blocks(pe, body)


def project_queries(nc, x, wqT, bq, ident, neg_half, eps, qT_hi, qT_lo):
    ctx = ExitStack()
    with ctx:
        t = Tools(nc, ctx)
        w_in = t.sb("q_w_in", [P, DC, D])
        wq_hi, wq_lo = t.sb("wq_hi", [P, DC, D], F32R), t.sb("wq_lo", [P, DC, D], F32R)
        bq_col = t.sb("bq_col", [P, DC])
        x_in = t.sb("x_in", [P, 2, 4, D])
        xn = t.sb("xn", [P, 2, 4, D])
        stats = t.sb("q_stats", [P, 2, 4, 6])
        mean_var = t.sb("q_mean_var", [P, 2, 4, 2])
        var_eps = t.sb("q_var_eps", [P, 2, 4])
        rstd = t.sb("q_rstd", [P, 2, 4])
        xT_hi, xT_lo = t.sb("xT_hi", [P, 2, DC, BLK], F32R), t.sb("xT_lo", [P, 2, DC, BLK], F32R)
        q_hi, q_lo = t.sb("q_hi", [P, 2, DC, BLK], F32R), t.sb("q_lo", [P, 2, DC, BLK], F32R)
        bank = t.banks(4, "q_bank")
        tbank = t.banks(4, "q_tbank")

        passed = t.sem("q_bias_loaded_sp_passed")
        bias_loaded, w_loaded = t.sem("q_bias_loaded"), t.sem("wq_loaded")
        w_hi_ready, w_lo_ready = t.sem("wq_hi_ready"), t.sem("wq_lo_ready")
        x_loaded = [t.sem("x_loaded0"), t.sem("x_loaded1")]
        stats_ready, mv_ready, eps_ready = t.sem("q_stats_ready"), t.sem("q_mv_ready"), t.sem("q_eps_ready")
        passed_dve = t.sem("q_dve_passed")
        rstd_ready, xn_ready = t.sem("q_rstd_ready"), t.sem("xn_ready")
        xT_done = t.sem("xT_done")
        xT_hi_ready, xT_lo_ready = t.sem("xT_hi_ready"), t.sem("xT_lo_ready")
        job_done, q_hi_ready, q_lo_ready = t.sem("q_job_done"), t.sem("q_hi_ready"), t.sem("q_lo_ready")
        q_stored = [t.sem("q_stored0"), t.sem("q_stored1")]
        PAIRS = QB // 2 - 1

        def blocks(eng, prepare, process):
            prepare(0, 0, 0)

            def pair(i):
                for u in range(2):
                    process(2 * i + u, u, i, lambda: prepare(2 * i + u + 1, 1 - u, i + u))
            pair(0)
            with eng.Fori(1, PAIRS) as i:
                pair(i)
            process(2 * PAIRS, 0, PAIRS, lambda: prepare(2 * PAIRS + 1, 1, PAIRS))
            process(2 * PAIRS + 1, 1, PAIRS, None)

        with nc.Block() as block:
            @block.sync
            def _(sp):
                sp.dma_start(w_in[:, :, :], wqT.rearrange("(c p) n -> p c n", p=P)).then_inc(w_loaded, 16)

                def process(b, u, before, prepare_next):
                    if prepare_next:
                        hold(sp, xn_ready, 4 * b, passed)
                        sp.dma_start(x_in[:, 1 - u], x[bass.ds((b + 1) * BLK, BLK), :].rearrange(
                            "(t p) n -> p t n", p=P)).then_inc(x_loaded[1 - u], 16)

                def first(b, u, before):
                    sp.dma_start(x_in[:, 0], x[0:BLK, :].rearrange("(t p) n -> p t n", p=P)).then_inc(x_loaded[0], 16)
                blocks(sp, first, process)

            @block.gpsimd
            def _(pool):
                pool.dma_start(bq_col[:, :], bq).then_inc(bias_loaded, 16)

                def prepare(b, u, before):
                    pool.wait_ge(mv_ready, 4 * (b + 1))
                    pool.tensor_tensor(var_eps[:, u], mean_var[:, u, :, 1], eps[:, :], ALU.add).then_inc(eps_ready, 1)
                    pool.wait_ge(eps_ready, b + 1)
                    pool.tensor_tensor(rstd[:, u], var_eps[:, u], neg_half[:, 0:4], ALU.pow).then_inc(rstd_ready, 1)

                def process(b, u, before, prepare_next):
                    if prepare_next:
                        prepare_next()
                    cols = bass.ds(b * BLK, BLK)
                    pool.wait_ge(q_lo_ready, 4 + DC * (b + 1))
                    pool.dma_start(qT_hi[:, cols].rearrange("(c p) n -> p c n", p=P), as_f32(q_hi[:, u])).then_inc(q_stored[u], 16)
                    pool.dma_start(qT_lo[:, cols].rearrange("(c p) n -> p c n", p=P), as_f32(q_lo[:, u])).then_inc(q_stored[u], 16)
                blocks(pool, prepare, process)
                for u in range(2):
                    pool.wait_ge(q_stored[u], 32 * (QB // 2))

            @block.scalar
            def _(act):
                act.wait_ge(w_loaded, 16)
                act.activation(wq_hi[:, :, :], w_in[:, :, :], ACT.Copy).then_inc(w_hi_ready, 1)

                def prepare(b, u, before):
                    for c in range(DC):
                        act.wait_ge(xT_done, DC * b + c + 1)
                        act.activation(xT_hi[:, u, c], tbank[c][:, :], ACT.Copy).then_inc(xT_hi_ready, 1)

                def process(b, u, before, prepare_next):
                    for n in range(DC):
                        if n == DC - 1 and prepare_next:
                            prepare_next()
                        act.wait_ge(job_done, DC * b + n + 1)
                        if n == 0:
                            act.wait_ge(bias_loaded, 16)
                            reach(act, q_stored[u], 32 * before)
                        act.activation(q_hi[:, u, n], bank[n][:, :], ACT.Identity, bias=bq_col[:, n:n + 1]).then_inc(q_hi_ready, 1)
                blocks(act, prepare, process)

            @block.vector
            def _(dve):
                def normalise_stats(b, u):
                    for k in range(4):
                        dve.bn_stats(stats[:, u, k], x_in[:, u, k]).then_inc(stats_ready, 1)
                    hold(dve, stats_ready, 4 * (b + 1), passed_dve)
                    for k in range(4):
                        dve.bn_aggr(mean_var[:, u, k], stats[:, u, k]).then_inc(mv_ready, 1)

                def normalise(b, u):
                    dve.wait_ge(rstd_ready, b + 1)
                    for k in range(4):
                        dve.tensor_scalar(xn[:, u, k], x_in[:, u, k], mean_var[:, u, k, 0:1], rstd[:, u, k:k + 1],
                                          ALU.subtract, ALU.mult).then_inc(xn_ready, 1)

                def low_parts(b, u):
                    for c in range(DC):
                        dve.wait_ge(xT_hi_ready, DC * b + c + 1)
                        dve.tensor_tensor(xT_lo[:, u, c], tbank[c][:, :], as_f32(xT_hi[:, u, c]), ALU.subtract).then_inc(xT_lo_ready, 1)

                def q_low(b, u, n):
                    dve.wait_ge(q_hi_ready, DC * b + n + 1)
                    dve.scalar_tensor_tensor(q_lo[:, u, n], bank[n][:, :], bq_col[:, n:n + 1], as_f32(q_hi[:, u, n]),
                                             ALU.add, ALU.subtract).then_inc(q_lo_ready, 1)

                def first(b, u, before):
                    dve.sem_inc(q_lo_ready, 4)
                    dve.wait_ge(x_loaded[0], 16)
                    normalise_stats(0, 0)
                    normalise(0, 0)
                    low_parts(0, 0)
                    dve.wait_ge(w_hi_ready, 1)
                    dve.tensor_tensor(wq_lo[:, :, :], w_in[:, :, :], as_f32(wq_hi[:, :, :]), ALU.subtract).then_inc(w_lo_ready, 1)
                    dve.wait_ge(bias_loaded, 16)

                def process(b, u, before, prepare_next):
                    if prepare_next:
                        dve.wait_ge(x_loaded[1 - u], 16 * (before + 1 + u))
                        normalise_stats(b + 1, 1 - u)
                    q_low(b, u, 0)
                    if prepare_next:
                        normalise(b + 1, 1 - u)
                    q_low(b, u, 1)
                    q_low(b, u, 2)
                    if prepare_next:
                        low_parts(b + 1, 1 - u)
                    q_low(b, u, 3)
                blocks(dve, first, process)

            @block.tensor
            def _(pe):
                def prepare(b, u, before):
                    pe.wait_ge(xn_ready, 4 * (b + 1))
                    reach(pe, xT_lo_ready, DC * b)
                    for c in range(DC):
                        for k in range(4):
                            mm = pe.transpose(tbank[c][:, k * P:(k + 1) * P], xn[:, u, k, c * P:(c + 1) * P], ident[:, :])
                        mm.then_inc(xT_done, 1)

                def process(b, u, before, prepare_next):
                    for n in range(DC):
                        if n == DC - 1 and prepare_next:
                            prepare_next()
                        if n == 0:
                            pe.wait_ge(xT_lo_ready, DC * (b + 1))
                            pe.wait_ge(w_lo_ready, 1)
                        pe.wait_ge(q_lo_ready, DC * b + n + 1)
                        for c in range(DC):
                            cols = slice(n * P, (n + 1) * P)
                            for k, (w, xx) in enumerate(((wq_hi, xT_hi), (wq_hi, xT_lo), (wq_lo, xT_hi))):
                                mm = pe.matmul(bank[n][:, :], w[:, c, cols], xx[:, u, c],
                                               start=(c == 0 and k == 0), stop=(c == DC - 1 and k == 2))
                        mm.then_inc(job_done, 1)
                blocks(pe, prepare, process)


R_HI, R_MID, R_LO, R_MAX = 0, HD, 2 * HD, 3 * HD
R_END = R_MAX + 2 * HG
SLOTS = 5
QBUFS = 4
S_RING, M_RING = 3, 3
PARTS = 8


def key_tiles(j):
    return min(4 * j + 4, KT)


def key_chunks(j):
    return min(j + 1, KB)


STEPS = [(j, kt) for j in range(QB) for kt in range(key_tiles(j))]
ST = len(STEPS)
FIRST_STEP = [STEPS.index((j, 0)) for j in range(QB)] + [ST]


def pool_sums(j, kt):
    if j == 0 or kt >= key_tiles(j) - 2:
        return False
    return kt % 3 != 2 if j < QB - 1 else kt % 2 == 1 or kt == 0


def pool_adds(j, kt):
    return pool_sums(j, kt) and kt != 0


PO = sum(pool_adds(j, kt) for j, kt in STEPS)
PO_BEFORE = [sum(pool_adds(j, kt) for j, kt in STEPS[:s]) for s in range(ST + 1)]


def max_units(j):
    units = []
    for r in range(4):
        seen = min((4 * j + r + 1) * P, NK)
        for h in range(HG):
            for c in range(key_chunks(j)):
                n = min(BLK, seen - c * BLK)
                first_masked = (4 * j + r) * P - c * BLK
                masked = min(P, n - first_masked) if first_masked < n else 0
                units.append((r, h, c, n, first_masked, masked))
    return units


UNITS = [max_units(j) for j in range(QB)]
NU = sum(map(len, UNITS))
UNITS_BEFORE = [sum(map(len, UNITS[:j])) for j in range(QB + 1)]


LEAD_BLOCKS = 3


def max_jobs():
    jobs = []
    for j in range(QB):
        for i in range(len(UNITS[j])):
            if j > 0 and i == (0 if j == LEAD_BLOCKS else 3):
                jobs.append((j - 1, None))
            jobs.append((j, i))
    return jobs + [(QB - 1, None)]


MAX_JOBS = max_jobs()
FIRST_LEAD = MAX_JOBS.index((0, None)) + 1
LEAD = MAX_JOBS.index((LEAD_BLOCKS - 1, None))
W_SCORES, W_VALUES = 1, 0.8

PIECES = (0, 1, 2, "values", 3, "denominators")


def plan(first, last):
    t, at = 0, []
    for j, kt in STEPS:
        width = (BLK - max(0, kt - 4 * j) * P) / BLK
        at.append([])
        for piece in PIECES:
            at[-1].append(t)
            if isinstance(piece, int):
                t += W_SCORES * width
            elif piece == "values" or not pool_sums(j, kt):
                t += W_VALUES * width
    jobs = []
    for q in range(FIRST_LEAD if first else LEAD, len(MAX_JOBS)):
        j = MAX_JOBS[q][0]
        release = at[min(FIRST_STEP[j - QBUFS + 1] + 3, ST - 1)][0] if j >= QBUFS - 1 and MAX_JOBS[q][1] is not None else 0
        jobs.append((0, q, release, at[max(0, FIRST_STEP[j] - 3)][0]))
    if not last:
        for q in range(LEAD):
            j = MAX_JOBS[q][0]
            jobs.append((1, q, at[FIRST_STEP[QB - 1] + 4 * j + 7][0], t))
    when, now = [], 0
    for n, (_, _, release, _) in enumerate(jobs):
        pace = min([(t - now) / (len(jobs) - n)] + [(due - now) / (i + 1) for i, (_, _, _, due) in enumerate(jobs[n:])])
        now = max(now + max(pace, 0), release)
        when.append(now)
    n, steps = 0, []
    for s in range(ST):
        steps.append([])
        for piece in range(len(PIECES)):
            steps[-1].append([])
            while n < len(jobs) and (when[n] <= at[s][piece] or (s == ST - 1 and piece == len(PIECES) - 1)):
                steps[-1][-1].append(jobs[n][:2])
                n += 1
    return steps


PLANS = {(first, last): plan(first, last) for first, last in ((True, False), (False, False), (False, True))}


def attend(nc, qT_hi, qT_lo, kT_hi, kT_lo, v_dram, aT, ident_b, mask, maskT, head_rows, load_weights):
    ctx = ExitStack()
    with ctx:
        t = Tools(nc, ctx)
        k_sb = t.sb("k_sb", [P, HG, KT * P], F32R)
        v_sb = t.sb("v_sb", [P, KT, P])
        q_sb = [t.sb(f"q_sb{i}", [P, HG, BLK], F32R) for i in range(QBUFS)]
        pT = t.sb("pT", [P, SLOTS, HG, BLK])
        ones = t.sb("ones", [P, HD])
        part_sum = t.sb("part_sum", [P, 2, HG, BLK])
        row_max = t.sb("row_max", [P, 2, 4, HG, KB])
        neg_max = t.sb("neg_max", [P, 4, HG])
        neg_parts = t.sb("neg_parts", [P, 4, HG, 2], BF16)
        o_sb, den_sb = t.sb("o_sb", [P, 2, BLK]), t.sb("den_sb", [P, 2, BLK])
        rden, a_out = t.sb("rden", [P, BLK]), t.sb("a_out", [P, 2, BLK])
        s_bank, m_bank = t.banks(S_RING, "s_bank"), t.banks(M_RING, "m_bank")
        [o_bank] = t.banks(1, "o_bank")
        [den_bank] = t.banks(1, "den_bank")

        passed, passed_pe = t.sem("att_sp_passed"), t.sem("att_pe_passed")
        const_ready = t.sem("att_const_ready")
        q_loaded = [t.sem(f"q_loaded{i}") for i in range(QBUFS)]
        k_loaded = [t.sem(f"k_loaded{c}") for c in range(KB)]
        v_loaded = [t.sem(f"v_loaded{c}") for c in range(KB)]
        unit_done, unit_max = t.sem("unit_done"), t.sem("unit_max")
        neg_ready = t.sem("neg_ready")
        maxT_done, max_rows = t.sem("maxT_done"), t.sem("max_rows")
        s_done = t.sem("s_done")
        exp_done = t.sem("exp_done")
        p_used = t.sem("p_used")
        pool_added = t.sem("pool_added")
        block_done, block_copied = t.sem("block_done"), t.sem("block_copied")
        rden_ready, a_ready = t.sem("rden_ready"), t.sem("a_ready")
        a_stored = [t.sem("a_stored0"), t.sem("a_stored1")]
        TILES = HG * ST

        def groups(eng, body):
            body(0, True, False)
            with eng.Fori(1, NG - 1) as g:
                body(g, False, False)
            body(NG - 1, False, True)

        with nc.Block() as block:
            @block.sync
            def _(sp):
                def load_q(g, j):
                    for row, src in ((R_HI, qT_hi), (R_MID, qT_lo), (R_LO, qT_hi)):
                        sp.dma_start(as_f32(q_sb[j % QBUFS][row:row + HD, :, :]),
                                     src[bass.ds(g * P, P), j * BLK:(j + 1) * BLK].rearrange("(h d) n -> d h n", d=HD)
                                     ).then_inc(q_loaded[j % QBUFS], 16)

                def load_k(g, c):
                    n = min(BLK, KT * P - c * BLK)
                    for row, src in ((R_HI, kT_hi), (R_MID, kT_hi), (R_LO, kT_lo)):
                        sp.dma_start(as_f32(k_sb[row:row + HD, :, c * BLK:c * BLK + n]),
                                     src[bass.ds(g * P, P), c * BLK:c * BLK + n].rearrange("(h d) n -> d h n", d=HD)
                                     ).then_inc(k_loaded[c], 16)

                def load_v(g, c):
                    n = min(BLK, KT * P - c * BLK)
                    sp.dma_start(v_sb[:, 4 * c:4 * c + n // P, :],
                                 v_dram[c * BLK:c * BLK + n, bass.ds(g * P, P)].rearrange("(t p) n -> p t n", p=P)
                                 ).then_inc(v_loaded[c], 16)

                def body(g, first, last):
                    if first:
                        for c in range(KB):
                            if c < QBUFS:
                                load_q(0, c)
                            load_k(0, c)
                            load_v(0, c)
                        load_weights(sp)
                    else:
                        hold(sp, s_done, TILES * g, passed)
                        load_q(g, QBUFS - 1)
                    for j in range(QBUFS, QB):
                        hold(sp, s_done, TILES * g + HG * FIRST_STEP[j - QBUFS + 1], passed)
                        load_q(g, j)
                    if not last:
                        for c in range(KB):
                            if c < QBUFS - 1:
                                hold(sp, s_done, TILES * g + HG * FIRST_STEP[c + QBUFS + 1], passed)
                                load_q(g + 1, c)
                            through = FIRST_STEP[QB - 1] + min(4 * c + 4, KT)
                            hold(sp, s_done, TILES * g + HG * through, passed)
                            load_k(g + 1, c)
                            hold(sp, p_used, ST * g + through, passed)
                            load_v(g + 1, c)
                groups(sp, body)

            @block.gpsimd
            def _(pool):
                pool.memset(ones[:, :], 1.0).then_inc(const_ready, 1)

                def body(g, first, last):
                    for s, (j, kt) in enumerate(STEPS):
                        if not pool_adds(j, kt):
                            continue
                        if kt == 1:
                            reach(pool, block_done, (QB - 1) * g + max(0, j - 2))
                        reach(pool, exp_done, TILES * g + HG * (s + 1))
                        reach(pool, pool_added, PO * g + PO_BEFORE[s])
                        q0 = max(0, kt - 4 * j) * P
                        total = part_sum[:, j % 2, :, q0:]
                        pool.tensor_tensor(total, pT[:, (s - 1) % SLOTS, :, q0:] if kt == 1 else total,
                                           pT[:, s % SLOTS, :, q0:], ALU.add).then_inc(pool_added, 1)
                groups(pool, body)

            @block.scalar
            def _(act):
                def body(g, first, last):
                    def copy_block(j):
                        if j < 0:
                            reach(act, block_done, (QB - 1) * g)
                        elif j == 0:
                            reach(act, p_used, ST * g + key_tiles(0))
                        else:
                            reach(act, block_done, (QB - 1) * g + j)
                        reach(act, a_ready, QB * g + j - 1)
                        act.activation(o_sb[:, j % 2], o_bank[:, :], ACT.Copy).then_inc(block_copied, 1)
                        act.activation(den_sb[:, j % 2], den_bank[:, :], ACT.Copy).then_inc(block_copied, 1)

                    def store_block(j):
                        reach(act, a_ready, QB * g + j + 1)
                        rows, cols = (g if j >= 0 else g - 1) * P, slice(j % QB * BLK, (j % QB + 1) * BLK)
                        act.dma_start(aT[bass.ds(rows, P), cols], a_out[:, j % 2]).then_inc(a_stored[j % 2], 16)

                    def max_to_rows(ahead, j):
                        reach(act, maxT_done, QB * (g + ahead) + j + 1)
                        rows = slice(R_MAX, R_END)
                        bank = m_bank[MAX_JOBS.index((j, None)) % M_RING]
                        src = bank[rows, :].unsqueeze(1).to_broadcast([R_END - R_MAX, HG, BLK])
                        act.activation(q_sb[j % QBUFS][rows, :, :], src, ACT.Copy).then_inc(max_rows, 1)

                    def transposed_maxima(jobs):
                        for ahead, q in jobs:
                            if MAX_JOBS[q][1] is None:
                                max_to_rows(ahead, MAX_JOBS[q][0])

                    steps = PLANS[first, last]
                    if first:
                        max_to_rows(0, 0)
                    for s, (j, kt) in enumerate(STEPS):
                        q0 = max(0, kt - 4 * j) * P
                        rows = P if kt < KT - 1 else K_LAST
                        reach(act, p_used, ST * g + s + 1 - SLOTS)
                        reach(act, pool_added, PO * g + (PO_BEFORE[s - SLOTS + 1 + (STEPS[s - SLOTS][1] == 0)] if s >= SLOTS else 0))
                        for jobs, h in zip(steps[s], PIECES):
                            transposed_maxima(jobs)
                            if not isinstance(h, int):
                                continue
                            reach(act, s_done, TILES * g + HG * s + h + 1)
                            act.activation(pT[0:rows, s % SLOTS, h, q0:], s_bank[(HG * s + h) % S_RING][0:rows, q0:],
                                           ACT.Exp, scale=SCALE).then_inc(exp_done, 1)
                        if kt == 0 and (j > 0 or not first):
                            copy_block(j - 1)
                        if kt == 7 or (j == 1 and kt == 2 and not first):
                            store_block(j - 1 if kt == 7 else -1)
                    if last:
                        copy_block(QB - 1)
                        store_block(QB - 1)
                groups(act, body)
                for i in range(2):
                    act.wait_ge(a_stored[i], 16 * NG * QB // 2)

            @block.vector
            def _(dve):
                for h in range(HG):
                    dve.tensor_copy(k_sb[R_MAX:R_END, h, :], head_rows[R_MAX:R_END, h:h + 1].to_broadcast([R_END - R_MAX, KT * P])
                                    ).then_inc(const_ready, 1)

                def body(g, first, last):
                    def take_max(ahead, q):
                        j, i = MAX_JOBS[q]
                        if i is None:
                            return
                        r, h, c, n, _, _ = UNITS[j][i]
                        reach(dve, unit_done, NU * (g + ahead) + UNITS_BEFORE[j] + i + 1)
                        dve.tensor_reduce(row_max[:, j % 2, r, h, c:c + 1], m_bank[q % M_RING][:, 0:n], AX_X, ALU.max
                                          ).then_inc(unit_max, 1)
                        if i == len(UNITS[j]) - 1:
                            negate(ahead, j)

                    def negate(ahead, j):
                        before = QB * (g + ahead) + j
                        reach(dve, unit_max, NU * (g + ahead) + UNITS_BEFORE[j + 1])
                        dve.tensor_reduce(neg_max[:, :, :], row_max[:, j % 2, :, :, 0:key_chunks(j)], AX_X, ALU.max,
                                          negate=True).then_inc(neg_ready, 1)
                        reach(dve, neg_ready, 3 * before + 1)
                        reach(dve, maxT_done, before)
                        dve.tensor_copy(neg_parts[:, :, :, 0], neg_max[:, :, :]).then_inc(neg_ready, 1)
                        reach(dve, neg_ready, 3 * before + 2)
                        dve.tensor_tensor(neg_parts[:, :, :, 1], neg_max[:, :, :], neg_parts[:, :, :, 0], ALU.subtract
                                          ).then_inc(neg_ready, 1)

                    def invert(j, part):
                        if part == 0:
                            reach(dve, block_copied, 2 * (QB * g + j + 1))
                            reach(dve, a_ready, QB * g + j)
                        cols = slice(part * BLK // PARTS, (part + 1) * BLK // PARTS)
                        dve.reciprocal(rden[:, cols], den_sb[:, j % 2, cols]).then_inc(rden_ready, 1)

                    def normalise(j):
                        reach(dve, rden_ready, PARTS * (QB * g + j + 1))
                        reach(dve, a_stored[j % 2], 16 * (QB // 2 * g + j // 2))
                        dve.tensor_tensor(a_out[:, j % 2], o_sb[:, j % 2], rden[:, :], ALU.mult).then_inc(a_ready, 1)

                    if first:
                        for q in range(FIRST_LEAD):
                            take_max(0, q)
                    steps = PLANS[first, last]
                    for s, (j, kt) in enumerate(STEPS):
                        for n, jobs in enumerate(steps[s]):
                            for ahead, q in jobs:
                                take_max(ahead, q)
                            if j > 0 and 0 < kt < 5 and n in (1, 4):
                                invert(j - 1, 2 * (kt - 1) + n // 4)
                            if j == 0 and kt > 0 and not first and n in (0, 2, 4) and 3 * (kt - 1) + n // 2 < PARTS:
                                invert(-1, 3 * (kt - 1) + n // 2)
                        if j > 0 and kt == 5:
                            normalise(j - 1)
                        if j == 1 and kt == 0 and not first:
                            normalise(-1)
                    if last:
                        for part in range(PARTS):
                            invert(QB - 1, part)
                        normalise(QB - 1)
                groups(dve, body)

            @block.tensor
            def _(pe):
                pe.wait_ge(const_ready, 1 + HG)

                def body(g, first, last):
                    def bank_free(ahead, q):
                        if q < M_RING:
                            reach(pe, unit_max, NU * (g + ahead))
                            reach(pe, max_rows, QB * (g + ahead))
                            return
                        j, i = MAX_JOBS[q - M_RING]
                        if i is None:
                            reach(pe, max_rows, QB * (g + ahead) + j + 1)
                        else:
                            reach(pe, unit_max, NU * (g + ahead) + UNITS_BEFORE[j] + i + 1)

                    def job(ahead, q):
                        j, i = MAX_JOBS[q]
                        if i is None:
                            transpose_max(ahead, q, j)
                        else:
                            unit(ahead, q, j, i)

                    def unit(ahead, q, j, i):
                        r, h, c, n, first_masked, masked = UNITS[j][i]
                        if i == 0:
                            reach(pe, q_loaded[j % QBUFS], 48 * (QB // QBUFS * (g + ahead) + j // QBUFS + 1))
                        if c == j and r == 0 and h == 0:
                            reach(pe, k_loaded[c], 48 * (g + ahead + 1))
                        bank_free(ahead, q)
                        out = m_bank[q % M_RING]
                        mm = pe.matmul(out[:, 0:n], q_sb[j % QBUFS][0:R_MAX, h, r * P:(r + 1) * P],
                                       k_sb[0:R_MAX, h, c * BLK:c * BLK + n], start=True, stop=not masked)
                        if masked:
                            mm = pe.matmul(out[:, first_masked:n], ident_b[:, :], mask[:, 0:masked], start=False, stop=True)
                        mm.then_inc(unit_done, 1)

                    def transpose_max(ahead, q, j):
                        reach(pe, neg_ready, 3 * (QB * (g + ahead) + j + 1))
                        bank_free(ahead, q)
                        for r in range(4):
                            mm = pe.matmul(m_bank[q % M_RING][R_MAX:R_END, r * P:(r + 1) * P],
                                           neg_parts[:, r].rearrange("p h k -> p (h k)"), ident_b[:, :], start=True, stop=True)
                        mm.then_inc(maxT_done, 1)

                    def scores(s, h):
                        j, kt = STEPS[s]
                        q0 = max(0, kt - 4 * j) * P
                        if h == 0 and kt == 0:
                            reach(pe, max_rows, QB * g + j + 1)
                        n = HG * s + h
                        reach(pe, exp_done, TILES * g + max(0, n - S_RING + 1))
                        out = s_bank[n % S_RING]
                        mm = pe.matmul(out[:, q0:], k_sb[0:R_END, h, kt * P:(kt + 1) * P],
                                       q_sb[j % QBUFS][0:R_END, h, q0:], start=True, stop=kt < 4 * j)
                        if kt >= 4 * j:
                            mm = pe.matmul(out[:, q0:q0 + P], ident_b[:, :], maskT[:, :], start=False, stop=True)
                        mm.then_inc(s_done, 1)

                    def weigh_values(s):
                        j, kt = STEPS[s]
                        q0 = max(0, kt - 4 * j) * P
                        rows = P if kt < KT - 1 else K_LAST
                        if kt < KT - 1:
                            reach(pe, exp_done, TILES * g + HG * (s + 1))
                        else:
                            hold(pe, exp_done, TILES * g + HG * (s + 1), passed_pe)
                        if kt % 4 == 0 and kt // 4 == j:
                            reach(pe, v_loaded[j], 16 * (g + 1))
                        if kt == 0:
                            reach(pe, block_copied, 2 * (QB * g + j) - 1)
                        for h in range(HG):
                            mm = pe.matmul(o_bank[h * HD:(h + 1) * HD, q0:], v_sb[0:rows, kt, h * HD:(h + 1) * HD],
                                           pT[0:rows, s % SLOTS, h, q0:], start=kt == 0, stop=kt == key_tiles(j) - 1)
                        if pool_sums(j, kt):
                            mm.then_inc(p_used, 1)

                    def denominators(s):
                        j, kt = STEPS[s]
                        last_tile = kt == key_tiles(j) - 1
                        if not pool_sums(j, kt):
                            q0 = max(0, kt - 4 * j) * P
                            rows = P if kt < KT - 1 else K_LAST
                            if kt == (2 if j else 0):
                                reach(pe, block_copied, 2 * (QB * g + j))
                            for h in range(HG):
                                mm = pe.matmul(den_bank[h * HD:(h + 1) * HD, q0:], ones[0:rows, :], pT[0:rows, s % SLOTS, h, q0:],
                                               start=kt == (2 if j else 0), stop=j == 0 and last_tile)
                            mm.then_inc(p_used, 1)
                        if last_tile and j > 0:
                            reach(pe, pool_added, PO * g + PO_BEFORE[s + 1])
                            for h in range(HG):
                                mm = pe.matmul(den_bank[h * HD:(h + 1) * HD, :], ones[:, :], part_sum[:, j % 2, h], start=False, stop=True)
                            mm.then_inc(block_done, 1)

                    if first:
                        for q in range(FIRST_LEAD):
                            job(0, q)
                    steps = PLANS[first, last]
                    for s in range(ST):
                        for jobs, piece in zip(steps[s], PIECES):
                            for ahead, q in jobs:
                                job(ahead, q)
                            if isinstance(piece, int):
                                scores(s, piece)
                            elif s and piece == "values":
                                weigh_values(s - 1)
                            elif s:
                                denominators(s - 1)
                    weigh_values(ST - 1)
                    denominators(ST - 1)
                groups(pe, body)


def project_output(nc, x, aT, wo, wo_loaded, bo, ident, neg_half, eps, x1_dram, xT_hi, xT_lo, raw, later_weights):
    ctx = ExitStack()
    with ctx:
        t = Tools(nc, ctx)
        bo_all = t.sb("bo_all", [P, D])
        a_in = t.sb("a_in", [P, 2, DC, BLK])
        a_hi, a_lo = t.sb("a_hi", [P, 2, DC, BLK], F32R), t.sb("a_lo", [P, 2, DC, BLK], F32R)
        x_in = t.sb("o_x_in", [P, 2, 4, D])
        x1 = t.sb("x1", [P, 4, D])
        xn = t.sb("o_xn", [P, 2, 4, D])
        stats = t.sb("o_stats", [P, 2, 4, 6])
        mean_var = t.sb("o_mean_var", [P, 2, 4, 2])
        var_eps = t.sb("o_var_eps", [P, 2, 4])
        rstd = t.sb("o_rstd", [P, 2, 4])
        t_hi, t_lo = t.sb("t_hi", [P, DC, BLK], F32R), t.sb("t_lo", [P, DC, BLK], F32R)
        bank, tbank = t.banks(4, "o_job_bank"), t.banks(4, "o_tbank")

        passed = t.sem("wo_loaded_sp_passed")
        bias_loaded, piece_loaded = t.sem("o_bias_loaded"), t.sem("piece_loaded")
        w_hi_ready, w_lo_ready = t.sem("wo_hi_ready"), t.sem("wo_lo_ready")
        a_loaded = [t.sem("a_loaded0"), t.sem("a_loaded1")]
        x_loaded = [t.sem("o_x_loaded0"), t.sem("o_x_loaded1")]
        a_hi_ready, a_lo_ready, xb_ready = t.sem("a_hi_ready"), t.sem("a_lo_ready"), t.sem("o_xb_ready")
        job_done, x1_ready = t.sem("o_job_done"), t.sem("x1_ready")
        mv_ready, eps_ready, rstd_ready = t.sem("o_mv_ready"), t.sem("o_eps_ready"), t.sem("o_rstd_ready")
        stats_ready, passed_dve = t.sem("o_stats_ready"), t.sem("o_dve_passed")
        xn_ready, t_done = t.sem("o_xn_ready"), t.sem("o_t_done")
        t_hi_ready, t_lo_ready = t.sem("o_t_hi_ready"), t.sem("o_t_lo_ready")
        x1_stored = t.sem("x1_stored")
        t_stored = t.sem("t_stored")
        PAIRS = QB // 2 - 1

        def blocks(eng, ahead, process, behind):
            ahead(0, 0, 0)
            ahead(1, 1, 0)
            process(0, 0, 0)

            def pair(i):
                for k in (1, 2):
                    u = k % 2
                    ahead(2 * i + k + 1, 1 - u, i + 1)
                    process(2 * i + k, u, i + k - 1)
                    behind(2 * i + k - 1, 1 - u, i)
            pair(0)
            with eng.Fori(1, PAIRS) as i:
                pair(i)
            process(QB - 1, 1, PAIRS)
            behind(QB - 2, 0, PAIRS)
            behind(QB - 1, 1, PAIRS)

        PIECE_AFTER = (0, 1, QB - 2, QB - 1)
        assert len(later_weights) == len(PIECE_AFTER)

        def nothing(b, u, before):
            pass

        with nc.Block() as block:
            @block.sync
            def _(sp):
                def load_piece(n):
                    hold(sp, w_lo_ready, n + 1, passed)
                    stage, src, _, _ = later_weights[n]
                    sp.dma_start(stage, src).then_inc(piece_loaded, 16)

                sp.dma_start(bo_all[:, :], bo.partition_broadcast(P)).then_inc(bias_loaded, 16)

                def store(b, u, before):
                    rows = bass.ds(b * BLK, BLK)
                    hold(sp, x1_ready, 4 * (b + 1), passed)
                    sp.dma_start(x1_dram[rows, :].rearrange("(t p) n -> p t n", p=P), x1[:, :, :]).then_inc(x1_stored, 16)
                    if isinstance(b, int) and b in (2, QB - 1):
                        load_piece(1 if b == 2 else 2)

                def store_t(b, u, before):
                    cols = bass.ds(b * BLK, BLK)
                    hold(sp, t_lo_ready, DC * (b + 1), passed)
                    sp.dma_start(xT_hi[:, cols].rearrange("(c p) n -> p c n", p=P), as_f32(t_hi[:, :, :])).then_inc(t_stored, 16)
                    sp.dma_start(xT_lo[:, cols].rearrange("(c p) n -> p c n", p=P), as_f32(t_lo[:, :, :])).then_inc(t_stored, 16)
                    if isinstance(b, int) and b == QB - 2:
                        load_piece(3)

                def load(b, u, before):
                    hold(sp, a_lo_ready, DC * (b - 1), passed)
                    cols = bass.ds(b * BLK, BLK)
                    sp.dma_start(a_in[:, u], aT[:, cols].rearrange("(c p) n -> p c n", p=P)).then_inc(a_loaded[u], 16)
                    hold(sp, x1_ready, 4 * (b - 1), passed)
                    sp.dma_start(x_in[:, u], x[cols, :].rearrange("(t p) n -> p t n", p=P)).then_inc(x_loaded[u], 16)
                    if isinstance(b, int) and b == 2:
                        load_piece(0)
                blocks(sp, load, store, store_t)
                hold(sp, x1_stored, 16 * QB, passed)
                hold(sp, t_stored, 32 * QB, passed)

            @block.scalar
            def _(act):
                act.wait_ge(wo_loaded, 16)
                act.activation(wo[:, 0:DC, :], raw[:, :, :], ACT.Copy).then_inc(w_hi_ready, 1)

                def split(b, u, before):
                    act.wait_ge(a_loaded[u], 16 * (before + 1))
                    reach(act, job_done, 4 * (b - 1))
                    for c in range(DC):
                        act.activation(a_hi[:, u, c], a_in[:, u, c], ACT.Copy).then_inc(a_hi_ready, 1)

                def copy_t(b, u, before):
                    reach(act, t_stored, 32 * b)
                    for c in range(DC):
                        act.wait_ge(t_done, DC * b + c + 1)
                        act.activation(t_hi[:, c], tbank[c][:, :], ACT.Copy).then_inc(t_hi_ready, 1)
                    if isinstance(b, int) and b in PIECE_AFTER:
                        n = PIECE_AFTER.index(b)
                        act.wait_ge(piece_loaded, 16 * (n + 1))
                        stage, _, hi, _ = later_weights[n]
                        act.activation(hi, stage, ACT.Copy).then_inc(w_hi_ready, 1)
                blocks(act, split, nothing, copy_t)

            @block.gpsimd
            def _(pool):
                pool.wait_ge(bias_loaded, 16)

                def split(b, u, before):
                    for c in range(DC):
                        pool.wait_ge(a_hi_ready, DC * b + c + 1)
                        pool.tensor_tensor(a_lo[:, u, c], a_in[:, u, c], as_f32(a_hi[:, u, c]), ALU.subtract).then_inc(a_lo_ready, 1)
                    pool.wait_ge(x_loaded[u], 16 * (before + 1))
                    for k in range(4):
                        pool.tensor_tensor(x_in[:, u, k], x_in[:, u, k], bo_all[:, :], ALU.add).then_inc(xb_ready, 1)

                def invert(b, u, before):
                    pool.wait_ge(mv_ready, 4 * (b + 1))
                    pool.tensor_tensor(var_eps[:, u], mean_var[:, u, :, 1], eps[:, :], ALU.add).then_inc(eps_ready, 1)
                    pool.wait_ge(eps_ready, b + 1)
                    pool.tensor_tensor(rstd[:, u], var_eps[:, u], neg_half[:, 0:4], ALU.pow).then_inc(rstd_ready, 1)
                blocks(pool, split, invert, nothing)

            @block.vector
            def _(dve):
                dve.wait_ge(w_hi_ready, 1)
                dve.tensor_tensor(wo[:, DC:2 * DC, :], raw[:, :, :], as_f32(wo[:, 0:DC, :]), ALU.subtract).then_inc(w_lo_ready, 1)

                def residual(b, u, before):
                    reach(dve, xn_ready, 4 * b)
                    reach(dve, x1_stored, 16 * b)
                    for k in range(4):
                        dve.wait_ge(job_done, 4 * b + k + 1)
                        dve.wait_ge(xb_ready, 4 * b + k + 1)
                        dve.tensor_tensor(x1[:, k], bank[k][:, :], x_in[:, u, k], ALU.add).then_inc(x1_ready, 1)
                        if k:
                            dve.wait_ge(x1_ready, 4 * b + k)
                            dve.bn_stats(stats[:, u, k - 1], x1[:, k - 1]).then_inc(stats_ready, 1)
                    dve.wait_ge(x1_ready, 4 * b + 4)
                    dve.bn_stats(stats[:, u, 3], x1[:, 3]).then_inc(stats_ready, 1)
                    hold(dve, stats_ready, 4 * (b + 1), passed_dve)
                    for k in range(4):
                        dve.bn_aggr(mean_var[:, u, k], stats[:, u, k]).then_inc(mv_ready, 1)
                    if isinstance(b, int) and b in (0, QB - 1):
                        normalise(b, u)

                def normalise(b, u):
                    dve.wait_ge(rstd_ready, b + 1)
                    for k in range(4):
                        dve.tensor_scalar(xn[:, u, k], x1[:, k], mean_var[:, u, k, 0:1], rstd[:, u, k:k + 1],
                                          ALU.subtract, ALU.mult).then_inc(xn_ready, 1)

                def behind(b, u, before):
                    for c in range(DC):
                        dve.wait_ge(t_hi_ready, DC * b + c + 1)
                        dve.tensor_tensor(t_lo[:, c], tbank[c][:, :], as_f32(t_hi[:, c]), ALU.subtract).then_inc(t_lo_ready, 1)
                    if not isinstance(b, int) or b < QB - 2:
                        normalise(b + 1, 1 - u)
                    if isinstance(b, int) and b in PIECE_AFTER:
                        n = PIECE_AFTER.index(b)
                        stage, _, hi, lo = later_weights[n]
                        dve.wait_ge(w_hi_ready, n + 2)
                        dve.tensor_tensor(lo, stage, as_f32(hi), ALU.subtract).then_inc(w_lo_ready, 1)
                blocks(dve, nothing, residual, behind)

            @block.tensor
            def _(pe):
                pe.wait_ge(w_lo_ready, 1)

                def project(b, u, before):
                    for n in range(4):
                        if n == 0:
                            pe.wait_ge(a_lo_ready, DC * (b + 1))
                        reach(pe, x1_ready, 4 * b)
                        rows = slice(n * P, (n + 1) * P)
                        for c in range(DC):
                            for k, (a, w) in enumerate(((a_hi, c), (a_hi, DC + c), (a_lo, c))):
                                mm = pe.matmul(bank[n][:, :], a[:, u, c, rows], wo[:, w], start=(c == 0 and k == 0),
                                               stop=(c == DC - 1 and k == 2))
                        mm.then_inc(job_done, 1)

                def transpose(b, u, before):
                    pe.wait_ge(xn_ready, 4 * (b + 1))
                    reach(pe, t_lo_ready, DC * b)
                    for c in range(DC):
                        for k in range(4):
                            mm = pe.transpose(tbank[c][:, k * P:(k + 1) * P], xn[:, u, k, c * P:(c + 1) * P], ident[:, :])
                        mm.then_inc(t_done, 1)
                blocks(pe, nothing, project, transpose)


PAIR = E // 2
GATE_AT = 2 * EC + 4
JOBS = FC + E * EC + PAIR + FC
RING = 4
AHEAD = 5
assert JOBS % RING == 0


def ring_jobs(last):
    jobs = [("enc", m) for m in range(AHEAD, FC)] + [("next", 0)]
    for k in range(E * EC):
        if k == GATE_AT:
            jobs += [("next", 1), ("next", 2)] + [("gate", p) for p in range(PAIR)]
        jobs.append(("w1", k))
    jobs += [("next", 3), ("c2s", 0), ("c2s", 1), ("next", 4)] + [("c2s", m) for m in range(2, FC)]
    return [job for job in jobs if not (last and job[0] == "next")]


RING_JOBS = {last: ring_jobs(last) for last in (False, True)}
PLACE = {last: {job: AHEAD + n for n, job in enumerate(jobs)} for last, jobs in RING_JOBS.items()}
assert len(RING_JOBS[False]) == JOBS


def feed_forward(nc, xT_hi, xT_lo, x1_dram, w, we_hi, we_lo, wd_hi, wd_lo, w1_parts, hT, ident, neg_half, eps, out):
    ctx = ExitStack()
    with ctx:
        t = Tools(nc, ctx)
        w2 = t.sb("w2", [P, E * EC, M])
        ws = t.sb("ws", [P, FC, 2, M])
        wc = t.sb("wc", [P, FH])
        wr = t.sb("wr", [M, E])
        be_col, bs_col, b1_col = t.sb("be_col", [P, FC]), t.sb("bs_col", [P, 1]), t.sb("b1_col", [P, E * EC])
        b2_col, bc_col = t.sb("b2_col", [P, PAIR]), t.sb("bc_col", [P, FC])
        br_all, bd_all = t.sb("br_all", [P, E]), t.sb("bd_all", [P, D])
        lng_all, lnb_all = t.sb("lng_all", [P, D]), t.sb("lnb_all", [P, D])
        sel_f, select = t.sb("sel_f", [P, PAIR, 2, M]), t.sb("select", [P, PAIR, P], F32R)
        rank = t.sb("rank", [P, 4, E])
        base_e = t.sb("base_e", [P, 4, E])

        x_hi, x_lo = t.sb("f_x_hi", [P, 2, DC, BLK], F32R), t.sb("f_x_lo", [P, 2, DC, BLK], F32R)
        xb = t.sb("f_xb", [P, 4, D])
        sT = t.sb("sT", [P, FC, BLK])
        c_parts = t.sb("c_parts", [P, 2, BLK], F32R)
        c_f = t.sb("c_f", [M, BLK])
        logits, expd, prob = t.sb("logits", [P, 4, E]), t.sb("expd", [P, 4, E]), t.sb("prob", [P, 4, E])
        same, first1, first2, gate = (t.sb(n, [P, 4, E]) for n in ("same", "first1", "first2", "gate"))
        top = t.sb("top", [P, 8, 4])
        g_parts = t.sb("g_parts", [P, BLK], F32R)
        y_gated, moe = t.sb("y_gated", [P, BLK]), t.sb("moe", [P, BLK])
        sp_f = t.sb("sp_f", [P, 2, BLK])
        sp_hi, sp_lo = t.sb("sp_hi", [P, 2, BLK], F32R), t.sb("sp_lo", [P, 2, BLK], F32R)
        y = t.sb("y", [P, 4, D])
        g_sb = y
        stats, mean_var = t.sb("f_stats", [P, 4, 6]), t.sb("f_mean_var", [P, 4, 2])
        var_eps, rstd = t.sb("f_var_eps", [P, 4]), t.sb("f_rstd", [P, 4])
        ring, acc = t.banks(RING, "ring"), t.banks(4, "acc")

        small_loaded, w1_loaded = t.sem("small_loaded"), [t.sem("w1_loaded0"), t.sem("w1_loaded1")]
        built, const_ready = t.sem("f_built"), t.sem("f_const_ready")
        w1_hi_ready, w1_lo_ready = t.sem("w1_hi_ready"), t.sem("w1_lo_ready")
        x_loaded = [t.sem("f_x_loaded0"), t.sem("f_x_loaded1")]
        passed = t.sem("f_x1_loaded_sp_passed")
        x1_loaded, xb_ready = t.sem("f_x1_loaded"), t.sem("f_xb_ready")
        ring_done, ring_free = t.sem("ring_done"), t.sem("ring_free")
        s_used, h_used = t.sem("sT_used"), t.sem("hT_used")
        c_hi_ready, c_lo_ready, c_f_ready = t.sem("f_c_hi_ready"), t.sem("f_c_lo_ready"), t.sem("c_f_ready")
        logits_done, dist_ready, expd_ready = t.sem("logits_done"), t.sem("dist_ready"), t.sem("expd_ready")
        route = t.sem("route_step")
        gate_ready, gT_done, g_parts_ready = t.sem("gate_ready"), t.sem("gT_done"), t.sem("g_parts_ready")
        gated = t.sem("gated")
        gated_step, moe_ready = t.sem("gated_step"), t.sem("moe_ready")
        sp_hi_ready, sp_lo_ready, sp_used = t.sem("sp_hi_ready"), t.sem("sp_lo_ready"), t.sem("sp_used")
        y_ready = t.sem("y_ready")
        mv_ready, eps_ready, rstd_ready = t.sem("f_mv_ready"), t.sem("f_eps_ready"), t.sem("f_rstd_ready")
        stats_ready, scaled, passed_dve = t.sem("f_stats_ready"), t.sem("scaled"), t.sem("f_dve_passed")
        out_ready, out_stored = t.sem("out_ready"), t.sem("out_stored")

        def blocks(eng, body):
            body(0, 0, 0, False)
            body(1, 1, 0, False)
            with eng.Fori(1, QB // 2 - 1) as i:
                for u in range(2):
                    body(2 * i + u, u, i, False)
            body(QB - 2, 0, QB // 2 - 1, False)
            body(QB - 1, 1, QB // 2 - 1, True)

        SMALL_LOADS = 16
        ROUTE = 20

        with nc.Block() as block:
            @block.sync
            def _(sp):
                def load_x(b, u):
                    cols = bass.ds(b * BLK, BLK)
                    hold(sp, s_used, FC * (b - 1), passed)
                    sp.dma_start(as_f32(x_hi[:, u]), xT_hi[:, cols].rearrange("(c p) n -> p c n", p=P)).then_inc(x_loaded[u], 16)
                    sp.dma_start(as_f32(x_lo[:, u]), xT_lo[:, cols].rearrange("(c p) n -> p c n", p=P)).then_inc(x_loaded[u], 16)

                def load(b, u, before, last):
                    if not last:
                        load_x(b + 1, 1 - u)
                    hold(sp, out_ready, 4 * b, passed)
                    sp.dma_start(xb[:, :, :], x1_dram[bass.ds(b * BLK, BLK), :].rearrange("(t p) n -> p t n", p=P)
                                 ).then_inc(x1_loaded, 16)
                load_x(0, 0)
                loads = [(w2[:, :, :], w["W2"].rearrange("e (c p) m -> p (e c) m", p=P)),
                         (ws[:, :, 0, :], w["W_s2c"].rearrange("(c p) m -> p c m", p=P)),
                         (ws[:, :, 1, :], w["W_s2c"].rearrange("(c p) m -> p c m", p=P)),
                         (wc[0:M, :], w["W_c2s"]), (wc[M:P, :], w["W_c2s"]), (wr[:, :], w["Wr"]),
                         (bs_col[0:M, :], w["b_s2c"].rearrange("(p a) -> p a", a=1)),
                         (bs_col[M:P, :], w["b_s2c"].rearrange("(p a) -> p a", a=1))]
                for dst, src in loads:
                    sp.dma_start(dst, src).then_inc(small_loaded, 16)
                blocks(sp, load)

            @block.gpsimd
            def _(pool):
                pool.memset(sel_f[:, :, :, :], 0.0).then_inc(built, 1)
                for n, row in enumerate((0, HD)):
                    pool.wait_ge(built, n + 1)
                    pool.affine_select(out=sel_f[:, :, :, :], in_=sel_f[:, :, :, :], compare_op=ALU.not_equal, fill=1.0,
                                       base=-row, pattern=[[-2, PAIR], [-1, 2], [0, M]], channel_multiplier=1).then_inc(built, 1)
                for e in range(E):
                    pool.memset(rank[:, :, e:e + 1], float(E - e)).then_inc(built, 1)
                pool.wait_ge(small_loaded, 16 * SMALL_LOADS)
                pool.wait_ge(const_ready, 2)

                def body(b, u, before, last):
                    pool.wait_ge(x1_loaded, 16 * (b + 1))
                    for k in range(4):
                        pool.tensor_tensor(xb[:, k], xb[:, k], lnb_all[:, :], ALU.add).then_inc(xb_ready, 1)
                    pool.wait_ge(dist_ready, b + 1)
                    pool.tensor_tensor(expd[:, :, :], base_e[:, :, :], logits[:, :, :], ALU.pow).then_inc(expd_ready, 1)
                    pool.wait_ge(mv_ready, 4 * (b + 1))
                    pool.tensor_tensor(var_eps[:, :], mean_var[:, :, 1], eps[:, :], ALU.add).then_inc(eps_ready, 1)
                    pool.wait_ge(eps_ready, b + 1)
                    pool.tensor_tensor(rstd[:, :], var_eps[:, :], neg_half[:, 0:4], ALU.pow).then_inc(rstd_ready, 1)
                    pool.wait_ge(out_ready, 4 * (b + 1))
                    pool.dma_start(out[bass.ds(b * BLK, BLK), :].rearrange("(t p) n -> p t n", p=P), y[:, :, :]).then_inc(out_stored, 16)
                blocks(pool, body)
                pool.wait_ge(out_stored, 16 * QB)

            @block.scalar
            def _(act):
                loads = [(be_col[:, :], w["b_enc"]), (b1_col[:, :], w["b1"]), (b2_col[:, :], w["b2"]), (bc_col[:, :], w["b_c2s"]),
                         (br_all[:, :], w["br"].partition_broadcast(P)), (bd_all[:, :], w["b_dec"].partition_broadcast(P)),
                         (lng_all[:, :], w["ln_g"].partition_broadcast(P)), (lnb_all[:, :], w["ln_b"].partition_broadcast(P))]
                for dst, src in loads:
                    act.dma_start(dst, src).then_inc(small_loaded, 16)
                act.wait_ge(x_loaded[0], 32)
                for n, stage in enumerate((y, hT)):
                    for top in (0, M):
                        act.dma_start(stage[top:top + M, :, :], w["W1"][n * E // 2:(n + 1) * E // 2].rearrange("e m n -> m e n")
                                      ).then_inc(w1_loaded[n], 16)

                def body(b, u, before, last):
                    def spikes_in(block, m, src):
                        reach(act, s_used, FC * (block - 1) + m + 1)
                        act.activation(sT[:, m], src[:, :], ACT.Sigmoid, bias=be_col[:, m:m + 1]).then_inc(ring_free, 1)

                    for n, (kind, k) in enumerate(RING_JOBS[last]):
                        act.wait_ge(ring_done, JOBS * b + AHEAD + n + 1)
                        src = ring[(AHEAD + n) % RING]
                        if kind == "enc":
                            spikes_in(b, k, src)
                            if k == FC - 1:
                                act.wait_ge(s_used, FC * (b + 1))
                                act.activation(c_parts[:, 0], acc[0][:, :], ACT.Identity, bias=bs_col[:, 0:1]
                                               ).then_inc(c_hi_ready, 1)
                        elif kind == "next":
                            spikes_in(b + 1, k, src)
                        elif kind == "gate":
                            if k == 0:
                                reach(act, out_stored, 16 * b)
                            act.activation(g_sb[:, k], src[:, :], ACT.Copy).then_inc(ring_free, 1)
                        elif kind == "w1":
                            p, c, half = k // (2 * EC), k % (2 * EC) // 2, k % 2
                            act.wait_ge(h_used, E * EC // 2 * b + k // 2 + 1)
                            col = (2 * p + half) * EC + c
                            act.activation(hT[:, k % RING], src[:, :], ACT.Relu, bias=b1_col[:, col:col + 1]).then_inc(ring_free, 1)
                        else:
                            act.wait_ge(sp_lo_ready, FC * b + k + 1)
                            act.activation(sp_f[:, k % 2], src[:, :], ACT.Sigmoid, bias=bc_col[:, k:k + 1]).then_inc(ring_free, 1)

                act.wait_ge(small_loaded, 16 * SMALL_LOADS)
                for m in range(AHEAD):
                    act.wait_ge(ring_done, m + 1)
                    act.activation(sT[:, m], ring[m % RING][:, :], ACT.Sigmoid, bias=be_col[:, m:m + 1]).then_inc(ring_free, 1)
                for n, stage in enumerate((y, hT)):
                    act.wait_ge(w1_loaded[n], 32)
                    act.activation(w1_parts[:, n * E // 2:(n + 1) * E // 2, :], stage[:, :, :], ACT.Copy).then_inc(w1_hi_ready, 1)
                act.wait_ge(w1_lo_ready, 2)
                blocks(act, body)

            @block.vector
            def _(dve):
                dve.memset(as_f32(g_parts[:, :]), 0.0)
                dve.sem_inc(sp_lo_ready, 2)
                dve.memset(base_e[:, :, :], 2.718281828459045).then_inc(const_ready, 1)
                dve.wait_ge(built, 3 + E)
                dve.tensor_copy(select[:, :, :], sel_f[:, :, :, :].rearrange("p a b c -> p a (b c)")).then_inc(const_ready, 1)
                for n, stage in enumerate((y, hT)):
                    low = w1_parts[M:P, n * E // 2:(n + 1) * E // 2, :]
                    dve.wait_ge(w1_hi_ready, n + 1)
                    dve.tensor_tensor(low, stage[M:P, :, :], as_f32(low), ALU.subtract).then_inc(w1_lo_ready, 1)
                dve.wait_ge(small_loaded, 16 * SMALL_LOADS)

                def body(b, u, before, last):
                    dve.wait_ge(c_hi_ready, b + 1)
                    dve.scalar_tensor_tensor(c_parts[:, 1], acc[0][:, :], bs_col[:, 0:1], as_f32(c_parts[:, 0]),
                                             ALU.add, ALU.subtract).then_inc(c_lo_ready, 1)
                    dve.tensor_scalar(c_f[:, :], acc[0][0:M, :], bs_col[0:M, 0:1], None, ALU.add).then_inc(c_f_ready, 1)

                    steps = [0]

                    def step(ins):
                        steps[0] += 1
                        ins.then_inc(route, 1)
                        dve.wait_ge(route, ROUTE * b + steps[0])

                    def over(col):
                        return top[:, col].unsqueeze(2).to_broadcast([P, 4, E])

                    dve.wait_ge(logits_done, b + 1)
                    step(dve.tensor_tensor(logits[:, :, :], acc[1][:, 0:4 * E].rearrange("p (t e) -> p t e", e=E),
                                           br_all[:, :].unsqueeze(1).to_broadcast([P, 4, E]), ALU.add))
                    step(dve.tensor_reduce(top[:, 0], logits[:, :, :], AX_X, ALU.max))
                    dve.tensor_tensor(logits[:, :, :], logits[:, :, :], over(0), ALU.subtract).then_inc(dist_ready, 1)
                    dve.wait_ge(expd_ready, b + 1)
                    step(dve.tensor_reduce(top[:, 1], expd[:, :, :], AX_X, ALU.add))
                    step(dve.reciprocal(top[:, 2], top[:, 1]))
                    step(dve.tensor_tensor(prob[:, :, :], expd[:, :, :], over(2), ALU.mult))
                    step(dve.tensor_reduce(top[:, 3], prob[:, :, :], AX_X, ALU.max))
                    step(dve.tensor_tensor(same[:, :, :], prob[:, :, :], over(3), ALU.is_equal))
                    step(dve.tensor_tensor(same[:, :, :], same[:, :, :], rank[:, :, :], ALU.mult))
                    step(dve.tensor_reduce(top[:, 4], same[:, :, :], AX_X, ALU.max))
                    step(dve.tensor_tensor(first1[:, :, :], same[:, :, :], over(4), ALU.is_equal))
                    step(dve.scalar_tensor_tensor(prob[:, :, :], first1[:, :, :], -2.0, prob[:, :, :], ALU.mult, ALU.add))
                    step(dve.tensor_reduce(top[:, 5], prob[:, :, :], AX_X, ALU.max))
                    step(dve.tensor_tensor(same[:, :, :], prob[:, :, :], over(5), ALU.is_equal))
                    step(dve.tensor_tensor(same[:, :, :], same[:, :, :], rank[:, :, :], ALU.mult))
                    step(dve.tensor_reduce(top[:, 6], same[:, :, :], AX_X, ALU.max))
                    step(dve.tensor_tensor(top[:, 7], top[:, 3], top[:, 5], ALU.add))
                    step(dve.tensor_tensor(first2[:, :, :], same[:, :, :], over(6), ALU.is_equal))
                    step(dve.reciprocal(top[:, 7], top[:, 7]))
                    step(dve.tensor_tensor(first2[:, :, :], first2[:, :, :], over(5), ALU.mult))
                    step(dve.tensor_tensor(first1[:, :, :], first1[:, :, :], over(3), ALU.mult))
                    assert steps[0] == ROUTE
                    gather_gate(b)

                    dve.wait_ge(gT_done, b + 1)
                    dve.tensor_copy(g_parts[0:E, :], acc[1][0:E, :]).then_inc(g_parts_ready, 1)
                    dve.wait_ge(g_parts_ready, 2 * b + 1)
                    dve.tensor_tensor(g_parts[HD:HD + E, :], acc[1][0:E, :], as_f32(g_parts[0:E, :]), ALU.subtract
                                      ).then_inc(g_parts_ready, 1)

                    for p in range(PAIR):
                        dve.wait_ge(h_used, 2 + EC * (PAIR * b + p + 1))
                        dve.wait_ge(ring_free, RING + JOBS * b + PLACE[last]["gate", p] + 1)
                        reach(dve, moe_ready, (PAIR - 1) * b + max(0, p - 1))
                        dst = moe if p == 0 else y_gated
                        dve.scalar_tensor_tensor(dst[:, :], acc[2 + p % 2][:, :], b2_col[:, p:p + 1], g_sb[:, p],
                                                 ALU.add, ALU.mult).then_inc(gated, 1)
                        if p:
                            dve.wait_ge(gated, PAIR * b + p + 1)
                            dve.tensor_tensor(moe[:, :], moe[:, :], y_gated[:, :], ALU.add).then_inc(moe_ready, 1)
                    for m in range(FC):
                        dve.wait_ge(ring_free, RING + JOBS * b + PLACE[last]["c2s", m] + 1)
                        dve.wait_ge(sp_used, FC * b + m + 1)
                        dve.tensor_copy(sp_hi[:, m % 2], sp_f[:, m % 2]).then_inc(sp_hi_ready, 1)
                        dve.wait_ge(sp_hi_ready, FC * b + m + 1)
                        dve.tensor_tensor(sp_lo[:, m % 2], sp_f[:, m % 2], as_f32(sp_hi[:, m % 2]), ALU.subtract
                                          ).then_inc(sp_lo_ready, 1)
                    dve.wait_ge(sp_used, 2 + FC * (b + 1))
                    reach(dve, out_stored, 16 * b)
                    for k in range(4):
                        dve.tensor_tensor(y[:, k], acc[k][:, :], bd_all[:, :], ALU.add).then_inc(y_ready, 1)
                    for k in range(4):
                        dve.wait_ge(y_ready, 4 * b + k + 1)
                        dve.bn_stats(stats[:, k], y[:, k]).then_inc(stats_ready, 1)
                    hold(dve, stats_ready, 4 * (b + 1), passed_dve)
                    for k in range(4):
                        dve.bn_aggr(mean_var[:, k], stats[:, k]).then_inc(mv_ready, 1)
                    dve.wait_ge(mv_ready, 4 * (b + 1))
                    for k in range(4):
                        dve.scalar_tensor_tensor(y[:, k], y[:, k], mean_var[:, k, 0:1], lng_all[:, :], ALU.subtract, ALU.mult
                                                 ).then_inc(scaled, 1)
                    dve.wait_ge(rstd_ready, b + 1)
                    dve.wait_ge(xb_ready, 4 * (b + 1))
                    dve.wait_ge(scaled, 4 * (b + 1))
                    for k in range(4):
                        dve.scalar_tensor_tensor(y[:, k], y[:, k], rstd[:, k:k + 1], xb[:, k], ALU.mult, ALU.add
                                                 ).then_inc(out_ready, 1)

                def gather_gate(b):
                    dve.tensor_tensor(gate[:, :, :], first1[:, :, :], first2[:, :, :], ALU.add).then_inc(gated_step, 1)
                    dve.wait_ge(gated_step, b + 1)
                    dve.tensor_tensor(gate[:, :, :], gate[:, :, :], top[:, 7].unsqueeze(2).to_broadcast([P, 4, E]), ALU.mult
                                      ).then_inc(gate_ready, 1)
                blocks(dve, body)

            @block.tensor
            def _(pe):
                pe.sem_inc(h_used, 2)
                pe.sem_inc(sp_used, 2)
                pe.sem_inc(ring_free, RING)

                def encode(dst, m, u):
                    cols = slice(m * P, (m + 1) * P)
                    for c in range(DC):
                        for k, (ww, xx) in enumerate(((we_hi, x_hi), (we_hi, x_lo), (we_lo, x_hi))):
                            mm = pe.matmul(dst[:, :], ww[:, c, cols], xx[:, u, c], start=(c == 0 and k == 0),
                                           stop=(c == DC - 1 and k == 2))
                    mm.then_inc(ring_done, 1)

                def body(b, u, before, last):
                    def bank(job):
                        n = PLACE[last][job]
                        pe.wait_ge(ring_free, JOBS * b + n + 1)
                        return ring[n % RING]

                    def to_cont(m):
                        if m == 0:
                            reach(pe, y_ready, 4 * b)
                        if m < AHEAD:
                            place = PLACE[False]["next", m] - JOBS if not (isinstance(b, int) and b == 0) else m
                        else:
                            place = PLACE[last]["enc", m]
                        pe.wait_ge(ring_free, RING + JOBS * b + place + 1)
                        mm = pe.matmul(acc[0][:, :], ws[:, m].rearrange("p a b -> p (a b)"), sT[:, m], start=m == 0, stop=m == FC - 1)
                        mm.then_inc(s_used, 1)

                    def encode_next(m):
                        if not last:
                            if m == 0:
                                pe.wait_ge(x_loaded[1 - u], 32 * (before + u + 1))
                            encode(bank(("next", m)), m, 1 - u)

                    for m in range(AHEAD, FC):
                        encode(bank(("enc", m)), m, u)
                        if m == FC - 2:
                            for n in range(AHEAD):
                                to_cont(n)
                    for m in range(AHEAD, FC):
                        to_cont(m)
                    encode_next(0)

                    def hidden(k):
                        p, c, half = k // (2 * EC), k % (2 * EC) // 2, k % 2
                        dst = bank(("w1", k))
                        if k == 0:
                            pe.wait_ge(w1_lo_ready, 2)
                            pe.wait_ge(c_lo_ready, b + 1)
                        for part in range(2):
                            mm = pe.matmul(dst[:, :], w1_parts[:, 2 * p + half, c * P:(c + 1) * P], c_parts[:, part],
                                           start=part == 0, stop=part == 1)
                        mm.then_inc(ring_done, 1)

                    def expert_out(q):
                        p, c = q // EC, q % EC
                        pe.wait_ge(ring_free, RING + JOBS * b + PLACE[last]["w1", 2 * q + 1] + 1)
                        if c == 0:
                            reach(pe, gated, PAIR * b + max(0, p - 1))
                        for half in range(2):
                            mm = pe.matmul(acc[2 + p % 2][half * M:(half + 1) * M, :], w2[:, (2 * p + half) * EC + c, :],
                                           hT[:, (2 * q + half) % RING], start=c == 0, stop=c == EC - 1)
                        mm.then_inc(h_used, 1)

                    def router():
                        pe.wait_ge(c_f_ready, b + 1)
                        for k in range(4):
                            mm = pe.matmul(acc[1][:, k * E:(k + 1) * E], c_f[:, k * P:(k + 1) * P], wr[:, :], start=True, stop=True)
                        mm.then_inc(logits_done, 1)

                    def spread_gates():
                        encode_next(1)
                        pe.wait_ge(gate_ready, b + 1)
                        for k in range(4):
                            mm = pe.transpose(acc[1][0:E, k * P:(k + 1) * P], gate[:, k], ident[:, :])
                        mm.then_inc(gT_done, 1)
                        encode_next(2)
                        for p in range(PAIR):
                            dst = bank(("gate", p))
                            pe.wait_ge(g_parts_ready, 2 * (b + 1))
                            pe.matmul(dst[:, :], select[:, p], g_parts[:, :], start=True, stop=True).then_inc(ring_done, 1)

                    for q in range(E * EC // 2):
                        if 2 * q == GATE_AT:
                            spread_gates()
                        hidden(2 * q)
                        hidden(2 * q + 1)
                        if q == 0:
                            router()
                        if q:
                            expert_out(q - 1)
                    expert_out(E * EC // 2 - 1)

                    def spikes(m):
                        dst = bank(("c2s", m))
                        if m == 0:
                            pe.wait_ge(moe_ready, (PAIR - 1) * (b + 1))
                        pe.matmul(dst[:, :], wc[:, m * P:(m + 1) * P], moe[:, :], start=True, stop=True).then_inc(ring_done, 1)

                    def decode(m):
                        pe.wait_ge(sp_lo_ready, 2 + FC * b + m + 1)
                        for k in range(4):
                            rows = slice(k * P, (k + 1) * P)
                            for n, (a, ww) in enumerate(((sp_hi, wd_hi), (sp_hi, wd_lo), (sp_lo, wd_hi))):
                                mm = pe.matmul(acc[k][:, :], a[:, m % 2, rows], ww[:, m], start=(m == 0 and n == 0),
                                               stop=(m == FC - 1 and n == 2))
                        mm.then_inc(sp_used, 1)

                    encode_next(3)
                    spikes(0)
                    spikes(1)
                    encode_next(4)
                    for m in range(FC):
                        if m and m + 1 < FC:
                            spikes(m + 1)
                        decode(m)
                pe.wait_ge(x_loaded[0], 32)
                for m in range(AHEAD):
                    pe.wait_ge(ring_free, m + 1)
                    encode(ring[m % RING], m, 0)
                pe.wait_ge(small_loaded, 16 * SMALL_LOADS)
                pe.wait_ge(const_ready, 2)
                blocks(pe, body)


def decoder_layer(nc, a):
    ctx = ExitStack()
    with ctx:
        t = Tools(nc, ctx)

        def scratch(name, shape, dt):
            return nc.dram_tensor(name, shape, dt, kind="Internal").ap()

        kT_hi, kT_lo = scratch("kT_hi", (D, NK_PAD), F32), scratch("kT_lo", (D, NK_PAD), F32)
        v_dram = scratch("v_dram", (NK_PAD, D), F32)
        qT_hi, qT_lo = scratch("qT_hi", (D, NQ), F32), scratch("qT_lo", (D, NQ), F32)
        aT = scratch("aT", (D, NQ), F32)
        x1 = scratch("x1_dram", (NQ, D), F32)
        nT_hi, nT_lo = scratch("nT_hi", (D, NQ), F32), scratch("nT_lo", (D, NQ), F32)

        ident, ident_b = t.sb("ident", [P, P]), t.sb("ident_b", [P, P], BF16)
        mask, maskT = t.sb("mask", [P, P], BF16), t.sb("maskT", [P, P], BF16)
        head_rows = t.sb("head_rows", [P, HG])
        neg_half, eps = t.sb("neg_half", [P, 4]), t.sb("eps", [P, 4])
        built = t.sem("const_built")
        with nc.Block() as block:
            @block.gpsimd
            def _(pool):
                for m in (ident, ident_b, mask, maskT):
                    pool.memset(m[:, :], 0.0).then_inc(built, 1)
                pool.memset(head_rows[:, :], 1.0).then_inc(built, 1)
                pool.memset(neg_half[:, :], -0.5).then_inc(built, 1)
                pool.memset(eps[:, :], EPS).then_inc(built, 1)
                pool.wait_ge(built, 7)
                for m in (ident, ident_b):
                    pool.affine_select(out=m[:, :], in_=m[:, :], compare_op=ALU.not_equal, fill=1.0, base=0,
                                       pattern=[[-1, P]], channel_multiplier=1).then_inc(built, 1)
                pool.affine_select(out=mask[:, :], in_=mask[:, :], compare_op=ALU.is_ge, fill=MASKED, base=0,
                                   pattern=[[-1, P]], channel_multiplier=1).then_inc(built, 1)
                pool.affine_select(out=maskT[:, :], in_=maskT[:, :], compare_op=ALU.is_ge, fill=MASKED, base=0,
                                   pattern=[[1, P]], channel_multiplier=-1).then_inc(built, 1)
                pool.affine_select(out=head_rows[:, :], in_=head_rows[:, :], compare_op=ALU.is_ge, fill=0.0, base=-R_MAX,
                                   pattern=[[-2, HG]], channel_multiplier=1).then_inc(built, 1)
                pool.wait_ge(built, 12)
                pool.affine_select(out=head_rows[:, :], in_=head_rows[:, :], compare_op=ALU.is_ge, fill=0.0, base=R_MAX + 1,
                                   pattern=[[2, HG]], channel_multiplier=-1).then_inc(built, 1)

        project_keys_values(nc, a["ctxT"], a["wkT"], a["wvT"], a["bk"], a["bv"], kT_hi, kT_lo, v_dram)
        project_queries(nc, a["x"], a["wqT"], a["bq"], ident, neg_half, eps, qT_hi, qT_lo)
        raw = t.sb("raw", [P, DC, D])
        wo_loaded = t.sem("wo_loaded")

        def load_weights(sp):
            sp.dma_start(raw[:, :, :], a["woT"].rearrange("(c p) n -> p c n", p=P)).then_inc(wo_loaded, 16)

        attend(nc, qT_hi, qT_lo, kT_hi, kT_lo, v_dram, aT, ident_b, mask, maskT, head_rows, load_weights)

        we_hi, we_lo = t.sb("we_hi", [P, DC, FH], F32R), t.sb("we_lo", [P, DC, FH], F32R)
        wd_hi, wd_lo = t.sb("wd_hi", [P, FC, D], F32R), t.sb("wd_lo", [P, FC, D], F32R)
        wo_w1 = t.sb("wo_w1", [P, E, EH], F32R)
        assert E == 2 * DC and EH == D == BLK and RING == DC and FH == 2 * D
        pieces = []
        for i in range(2):
            half = slice(i * DC // 2, (i + 1) * DC // 2)
            pieces.append((raw[:, :, :].rearrange("p (c h) n -> p c (h n)", h=2),
                           a["W_enc"][i * D // 2:(i + 1) * D // 2, :].rearrange("(c p) n -> p c n", p=P),
                           we_hi[:, half, :], we_lo[:, half, :]))
        for i in range(2):
            half = slice(i * FC // 2, (i + 1) * FC // 2)
            pieces.append((raw[:, :, :], a["W_dec"][i * FH // 2:(i + 1) * FH // 2, :].rearrange("(c p) n -> p c n", p=P),
                           wd_hi[:, half, :], wd_lo[:, half, :]))
        project_output(nc, a["x"], aT, wo_w1, wo_loaded, a["bo"], ident, neg_half, eps, x1, nT_hi, nT_lo, raw, pieces)
        feed_forward(nc, nT_hi, nT_lo, x1, a, we_hi, we_lo, wd_hi, wd_lo, wo_w1, raw, ident, neg_half, eps, a["out"])


def kernel(**inputs):
    import numpy as np
    import concourse.bacc as bacc
    from concourse.bass_utils import run_bass_kernel_spmd

    i = {name: np.asarray(value) for name, value in inputs.items()}
    ctxT = np.zeros((D, NK_PAD), i["ctx_1024"].dtype)
    ctxT[:, :NK] = i["ctx_1024"][0].T
    arrays = {"x": i["x"][0], "ctxT": ctxT}
    for n in "qkvo":
        arrays[f"w{n}T"] = i[f"L0_xattn_W{n}"].T
        arrays[f"b{n}"] = i[f"L0_xattn_b{n}"]
    for n in ("W_enc", "b_enc", "W_s2c", "b_s2c", "Wr", "br", "W1", "b1", "W2", "b2", "W_c2s", "b_c2s", "W_dec", "b_dec",
              "ln_g", "ln_b"):
        arrays[n] = i[f"L0_ffn_{n}"]
    for n in ("bq", "bk", "b_enc", "b1", "b2", "b_c2s"):
        arrays[n] = arrays[n].reshape(-1, P).T
    arrays = {n: np.ascontiguousarray(v) for n, v in arrays.items()}

    nc = bacc.Bacc("TRN2", target_bir_lowering=False, num_devices=1)
    dram = {n: nc.dram_tensor(f"in_{n}", v.shape, mybir.dt.from_np(v.dtype), kind="ExternalInput").ap() for n, v in arrays.items()}
    dram["out"] = nc.dram_tensor("out_rows", (NQ, D), F32, kind="ExternalOutput").ap()
    decoder_layer(nc, dram)
    r = run_bass_kernel_spmd(nc, [{f"in_{n}": v for n, v in arrays.items()}], core_ids=[0])
    return r.results[0]["out_rows"].reshape(1, NQ, D)
```
